# Optimizing a Trainium2 kernel written in Bass

```python
import numpy as np
import jax
import jax.numpy as jnp

def _softmax(x, axis=-1):
    return jax.nn.softmax(x, axis=axis)

def _gelu(x):
    return jax.nn.gelu(x, approximate=True)

def _silu(x):
    return jax.nn.silu(x)

def _sigmoid(x):
    return jax.nn.sigmoid(x)

def _layernorm(x, axis=-1, eps=1e-05):
    m = jnp.mean(x, axis=axis, keepdims=True)
    v = jnp.var(x, axis=axis, keepdims=True)
    return (x - m) / jnp.sqrt(v + eps)

def _scatter_add(tgt, idx, src, axis=0):
    return tgt.at[idx].add(src)

def _segment_sum(src, seg, n):
    return jax.ops.segment_sum(src, seg, n)
kernel_name = 'mk_pixart_resid_d1_seqx_r8_d622d4'

def setup_inputs(seed: int=0):
    np.random.seed(seed)
    _w = jnp.asarray

    def _rec_inputs():
        import jax
        import jax.numpy as jnp
        _rk = jax.random.key(seed)
        x = -0.003379 + 0.9984 * jax.random.normal(jax.random.fold_in(_rk, 1), (16, 256, 128), jnp.float32)
        _lenS = 256 - jax.random.randint(jax.random.fold_in(_rk, 7), (16,), 0, max(1, 256 // 4) + 1, jnp.int32)
        _lenS2 = 1601 - jax.random.randint(jax.random.fold_in(_rk, 8), (16,), 0, max(1, 1601 // 4) + 1, jnp.int32)
        cond_1024 = -0.0142567 + 1.00875 * jax.random.normal(jax.random.fold_in(_rk, 11), (16, 128), jnp.float32)
        _ctx_1024P = jax.random.normal(jax.random.fold_in(_rk, 12), (16, 16, 128), jnp.float32)
        _ctx_1024c = jax.random.dirichlet(jax.random.fold_in(_rk, 512), 0.3 * jnp.ones((16,), jnp.float32), (16, 1601))
        _ctx_1024t = jnp.einsum('bsk,bkd->bsd', _ctx_1024c, _ctx_1024P)
        _ctx_1024t = _ctx_1024t * jax.lax.rsqrt(jnp.mean(jnp.square(_ctx_1024t)) + 1e-12) * 0.953939
        ctx_1024 = -5.72187e-05 + 0.999849 * (_ctx_1024t + 0.3 * jax.random.normal(jax.random.fold_in(_rk, 612), (16, 1601, 128), jnp.float32))
        return (x, cond_1024, ctx_1024)
    x, cond_1024, ctx_1024 = _rec_inputs()

    def _L0_xcond_setup():
        import jax, jax.numpy as jnp
        import numpy as np
        B, N, K, D, T = (16, 512, 16, 128, 3)
        EPS_ATTN = 1e-08
        LN_EPS = 1e-05

        def _ln(x, g, b):
            mu = jnp.mean(x, axis=-1, keepdims=True)
            var = jnp.mean(jnp.square(x - mu), axis=-1, keepdims=True)
            return (x - mu) * jax.lax.rsqrt(var + LN_EPS) * g + b
        key = jax.random.key(seed)
        ks = jax.random.split(key, 16)
        w = lambda k, i, o: jax.random.normal(k, (i, o), jnp.float32) * 0.02
        inp = {'x_cls': jax.random.normal(ks[0], (B, D), jnp.float32), 'x': jax.random.normal(ks[1], (B, N, D), jnp.float32), 'noise': jax.random.normal(ks[2], (B, K, D), jnp.float32), 'q_mu': jax.random.normal(ks[3], (1, 1, D), jnp.float32), 'q_logsig': jax.random.normal(ks[4], (1, 1, D), jnp.float32) * 0.02, 'lnkv_g': jnp.ones((D,), jnp.float32), 'lnkv_b': jnp.zeros((D,), jnp.float32), 'lnq_g': jnp.ones((D,), jnp.float32), 'lnq_b': jnp.zeros((D,), jnp.float32), 'lnm_g': jnp.ones((D,), jnp.float32), 'lnm_b': jnp.zeros((D,), jnp.float32), 'lnp_g': jnp.ones((D,), jnp.float32), 'lnp_b': jnp.zeros((D,), jnp.float32), 'wk': w(ks[5], D, D), 'bk': jnp.zeros((D,), jnp.float32), 'wv': w(ks[6], D, D), 'bv': jnp.zeros((D,), jnp.float32), 'wq': w(ks[7], D, D), 'bq': jnp.zeros((D,), jnp.float32), 'wu': w(ks[8], D, D), 'bu': jnp.zeros((D,), jnp.float32), 'w1': w(ks[9], D, D), 'b1': jnp.zeros((D,), jnp.float32), 'w2': w(ks[10], D, D), 'b2': jnp.zeros((D,), jnp.float32)}
        return inp
    _L0_xcond_all = _L0_xcond_setup()
    _L0_xcond_in = {k: v for k, v in _L0_xcond_all.items() if k in ('q_mu', 'q_logsig', 'lnkv_g', 'lnkv_b', 'lnq_g', 'lnq_b', 'lnm_g', 'lnm_b', 'lnp_g', 'lnp_b', 'wk', 'bk', 'wv', 'bv', 'wq', 'bq', 'wu', 'bu', 'w1', 'b1', 'w2', 'b2')}
    del _L0_xcond_all

    def _L0_ffn_setup():
        import jax, jax.numpy as jnp
        import numpy as np
        D_MODEL = 128
        D_HIDDEN = 512
        NUM_EXPERTS = 8
        B, T = (2, 256)
        key = jax.random.key(seed)
        ks = jax.random.split(key, 8)
        s = 0.02
        x = jax.random.normal(ks[0], (B, T, D_MODEL), dtype=jnp.float32)
        Wg = jax.random.normal(ks[1], (D_MODEL, NUM_EXPERTS), dtype=jnp.float32) * s
        bg = jnp.zeros((NUM_EXPERTS,), dtype=jnp.float32)
        W1 = jax.random.normal(ks[2], (NUM_EXPERTS, D_MODEL, D_HIDDEN), dtype=jnp.float32) * s
        b1 = jnp.zeros((NUM_EXPERTS, D_HIDDEN), dtype=jnp.float32)
        W2 = jax.random.normal(ks[3], (NUM_EXPERTS, D_HIDDEN, D_MODEL), dtype=jnp.float32) * s
        b2 = jnp.zeros((NUM_EXPERTS, D_MODEL), dtype=jnp.float32)
        return {'x': x, 'Wg': Wg, 'bg': bg, 'W1': W1, 'b1': b1, 'W2': W2, 'b2': b2}
    _L0_ffn_all = _L0_ffn_setup()
    _L0_ffn_in = {k: v for k, v in _L0_ffn_all.items() if k in ('Wg', 'bg', 'W1', 'b1', 'W2', 'b2')}
    del _L0_ffn_all
    return {'x': x, 'cond_1024': cond_1024, 'ctx_1024': ctx_1024, 'L0_xcond_q_mu': _L0_xcond_in['q_mu'], 'L0_xcond_q_logsig': _L0_xcond_in['q_logsig'], 'L0_xcond_lnkv_g': _L0_xcond_in['lnkv_g'], 'L0_xcond_lnkv_b': _L0_xcond_in['lnkv_b'], 'L0_xcond_lnq_g': _L0_xcond_in['lnq_g'], 'L0_xcond_lnq_b': _L0_xcond_in['lnq_b'], 'L0_xcond_lnm_g': _L0_xcond_in['lnm_g'], 'L0_xcond_lnm_b': _L0_xcond_in['lnm_b'], 'L0_xcond_lnp_g': _L0_xcond_in['lnp_g'], 'L0_xcond_lnp_b': _L0_xcond_in['lnp_b'], 'L0_xcond_wk': _L0_xcond_in['wk'], 'L0_xcond_bk': _L0_xcond_in['bk'], 'L0_xcond_wv': _L0_xcond_in['wv'], 'L0_xcond_bv': _L0_xcond_in['bv'], 'L0_xcond_wq': _L0_xcond_in['wq'], 'L0_xcond_bq': _L0_xcond_in['bq'], 'L0_xcond_wu': _L0_xcond_in['wu'], 'L0_xcond_bu': _L0_xcond_in['bu'], 'L0_xcond_w1': _L0_xcond_in['w1'], 'L0_xcond_b1': _L0_xcond_in['b1'], 'L0_xcond_w2': _L0_xcond_in['w2'], 'L0_xcond_b2': _L0_xcond_in['b2'], 'L0_ffn_Wg': _L0_ffn_in['Wg'], 'L0_ffn_bg': _L0_ffn_in['bg'], 'L0_ffn_W1': _L0_ffn_in['W1'], 'L0_ffn_b1': _L0_ffn_in['b1'], 'L0_ffn_W2': _L0_ffn_in['W2'], 'L0_ffn_b2': _L0_ffn_in['b2']}

def reference(x, cond_1024, ctx_1024, L0_xcond_q_mu, L0_xcond_q_logsig, L0_xcond_lnkv_g, L0_xcond_lnkv_b, L0_xcond_lnq_g, L0_xcond_lnq_b, L0_xcond_lnm_g, L0_xcond_lnm_b, L0_xcond_lnp_g, L0_xcond_lnp_b, L0_xcond_wk, L0_xcond_bk, L0_xcond_wv, L0_xcond_bv, L0_xcond_wq, L0_xcond_bq, L0_xcond_wu, L0_xcond_bu, L0_xcond_w1, L0_xcond_b1, L0_xcond_w2, L0_xcond_b2, L0_ffn_Wg, L0_ffn_bg, L0_ffn_W1, L0_ffn_b1, L0_ffn_W2, L0_ffn_b2):
    import jax
    import jax.numpy as jnp

    def _L0_xcond_ref(x_cls, x, noise, q_mu, q_logsig, lnkv_g, lnkv_b, lnq_g, lnq_b, lnm_g, lnm_b, lnp_g, lnp_b, wk, bk, wv, bv, wq, bq, wu, bu, w1, b1, w2, b2):
        import jax, jax.numpy as jnp
        import numpy as np
        B, N, K, D, T = (16, 512, 16, 128, 3)
        EPS_ATTN = 1e-08
        LN_EPS = 1e-05

        def _ln(x, g, b):
            mu = jnp.mean(x, axis=-1, keepdims=True)
            var = jnp.mean(jnp.square(x - mu), axis=-1, keepdims=True)
            return (x - mu) * jax.lax.rsqrt(var + LN_EPS) * g + b
        scale = D ** (-0.5)
        x_in = _ln(x, lnkv_g, lnkv_b)
        k = x_in @ wk + bk
        v = x_in @ wv + bv
        slots = q_mu + jnp.exp(q_logsig) * noise
        for _ in range(T):
            prev = slots
            q = _ln(slots, lnq_g, lnq_b) @ wq + bq
            logits = jnp.einsum('bnd,bkd->bnk', k, q) / scale
            attn = jax.nn.softmax(logits, axis=-1) + EPS_ATTN
            attn = attn / jnp.sum(attn, axis=1, keepdims=True)
            upd = jnp.einsum('bnk,bnd->bkd', attn, v)
            slots = upd @ wu + bu + prev
            h = _ln(slots, lnm_g, lnm_b) @ w1 + b1
            slots = jax.nn.gelu(h, approximate=False) @ w2 + b2 + slots
            slots = _ln(slots + x_cls[:, None, :], lnp_g, lnp_b)
        return slots

    def _L0_ffn_ref(x, Wg, bg, W1, b1, W2, b2):
        import jax, jax.numpy as jnp
        import numpy as np
        D_MODEL = 128
        D_HIDDEN = 512
        NUM_EXPERTS = 8
        B, T = (2, 256)
        gate_logits = jnp.einsum('btd,de->bte', x, Wg) + bg
        gate_scores = jax.nn.softmax(gate_logits, axis=-1)
        top1_idx = jnp.argmax(gate_scores, axis=-1)
        top1_mask = jax.nn.one_hot(top1_idx, NUM_EXPERTS, dtype=x.dtype)
        top1_weight = jnp.sum(gate_scores * top1_mask, axis=-1, keepdims=True)
        h = jax.nn.silu(jnp.einsum('btd,edh->bteh', x, W1) + b1)
        o = jnp.einsum('bteh,ehd->bted', h, W2) + b2
        y = jnp.sum(o * top1_mask[..., None], axis=2) * top1_weight
        return y
    x = x + _L0_xcond_ref(cond_1024, ctx_1024, _layernorm(x, axis=-1), L0_xcond_q_mu, L0_xcond_q_logsig, L0_xcond_lnkv_g, L0_xcond_lnkv_b, L0_xcond_lnq_g, L0_xcond_lnq_b, L0_xcond_lnm_g, L0_xcond_lnm_b, L0_xcond_lnp_g, L0_xcond_lnp_b, L0_xcond_wk, L0_xcond_bk, L0_xcond_wv, L0_xcond_bv, L0_xcond_wq, L0_xcond_bq, L0_xcond_wu, L0_xcond_bu, L0_xcond_w1, L0_xcond_b1, L0_xcond_w2, L0_xcond_b2)
    x = x + _L0_ffn_ref(_layernorm(x, axis=-1), L0_ffn_Wg, L0_ffn_bg, L0_ffn_W1, L0_ffn_b1, L0_ffn_W2, L0_ffn_b2)
    return x

_drawn_inputs = setup_inputs


def setup_inputs(seed=0):
    import zlib

    import numpy as np

    out = dict(_drawn_inputs(seed))
    spreads = {'L0_xcond_lnkv_g': (1.0, 0.6),
     'L0_xcond_lnkv_b': (0.0, 0.8),
     'L0_xcond_lnq_g': (1.0, 0.6),
     'L0_xcond_lnq_b': (0.0, 0.8),
     'L0_xcond_lnm_g': (1.0, 0.6),
     'L0_xcond_lnm_b': (0.0, 0.8),
     'L0_xcond_lnp_g': (1.0, 0.2),
     'L0_xcond_lnp_b': (0.0, 0.1),
     'L0_xcond_bk': (0.0, 0.8),
     'L0_xcond_bv': (0.0, 0.622),
     'L0_xcond_bq': (0.0, 0.8),
     'L0_xcond_bu': (0.0, 0.1),
     'L0_xcond_b1': (0.0, 0.8),
     'L0_xcond_b2': (0.0, 0.1),
     'L0_ffn_bg': (0.0, 0.8),
     'L0_ffn_b1': (0.0, 0.8),
     'L0_ffn_b2': (0.0, 0.714)}
    factors = {'ctx_1024': 2.857,
     'L0_xcond_q_logsig': 8.0,
     'L0_xcond_wk': 3.854,
     'L0_xcond_wq': 3.921,
     'L0_xcond_w1': 3.221,
     'L0_xcond_w2': 3.044,
     'L0_ffn_Wg': 4.883,
     'L0_ffn_W1': 8.0,
     'L0_ffn_W2': 8.0}
    for name, (base, spread) in spreads.items():
        noise = np.random.default_rng([zlib.crc32(name.encode()), seed]).standard_normal(out[name].shape)
        drawn = base * np.exp(spread * noise) if base else spread * noise
        out[name] = jnp.asarray(drawn.astype(out[name].dtype))
    for name, factor in factors.items():
        out[name] = (out[name] * factor).astype(out[name].dtype)
    return out
```

```python
import concourse.bass as bass
from concourse import mybir
from contextlib import ExitStack

F32 = mybir.dt.float32
F32R = mybir.dt.float32r
U32 = mybir.dt.uint32
I32 = mybir.dt.int32
ALU = mybir.AluOpType
ACT = mybir.ActivationFunctionType
AX = mybir.AxisListType

B, K, D, S = 16, 256, 128, 1601
P = 128
LN_EPS, ATTN_EPS = 1e-5, 1e-8
GROUPS = B // 4
FULL = S // P
TAIL = S - FULL * P
TILES = FULL + 1
CH = 7
SLOTS = 2 * CH
ROUNDS = 6
TRIP = ROUNDS * SLOTS
NL = 3
NE = 4
CREDIT = 4
AHEAD = 2
PAD = 2
PRE = 7
PRE_SLOT = [0, 2, 4, 6, 8, 9, 10]
E, H = 8, 512
HT = H // P
BLK = 256
NBLK = B * K // BLK + E
NT = B * K // P
REC = 2 * D + 4


def tiles_of(c):
    b, k = c // CH, c % CH
    return (b, 2 * k, 2, P) if k < CH - 1 else (b, 2 * k, 1, TAIL)


def pre_tiles(r):
    if r < PRE - 1:
        return [(r // 3, 4 * (r % 3), 4, P)]
    return [(0, FULL, 1, TAIL), (1, FULL, 1, TAIL)]


def last_dim(ap, n):
    return ap.rearrange("p (a b) -> p a b", b=1).to_broadcast([ap.shape[0], ap.shape[1], n])


def mid_dim(ap, n):
    return ap.rearrange("p (b a) -> p b a", b=1).to_broadcast([ap.shape[0], n, ap.shape[1]])


def build(nc, a, out):
    ctx = ExitStack()
    with ctx:
        def sb(name, shape, dt=F32):
            return ctx.enter_context(nc.sbuf_tensor(name, shape, dt))

        def pb(name, shape, dt=F32):
            return ctx.enter_context(nc.psum_tensor(name, shape, dt))

        def sem(name):
            return ctx.enter_context(nc.semaphore(name))

        W = {n: sb("w_" + n, [P, D]) for n in ("wk", "wv", "wq", "wu", "w1", "w2")}
        COLS = ("lnkv_g", "lnkv_b", "lnq_g", "lnq_b", "lnm_g", "lnm_b", "bk", "bv", "bq", "b1")
        cols = sb("cols", [P, len(COLS)])
        col = {n: cols[:, i:i + 1] for i, n in enumerate(COLS)}
        ROWS = ("lnp_g", "lnp_b", "b2", "bu", "q_mu", "q_logsig")
        rowt = sb("rowt", [P, len(ROWS), D])
        row = {n: rowt[:, i, :] for i, n in enumerate(ROWS)}
        ident = sb("ident", [P, P])
        ones = sb("ones", [P, P])
        negones = sb("negones", [P, P])
        meanw = sb("meanw", [P, 1])
        epst = sb("epst", [P, 32])
        neghalf = sb("neghalf", [P, 32])
        half = sb("half", [P, 32])
        wtmp = sb("wtmp", [P, 6, D])
        ctmp = sb("ctmp", [P, 8])
        wqk = sb("wqk", [P, D])
        wvu = sb("wvu", [P, D])
        w1g = sb("w1g", [P, D])
        bvu = sb("bvu", [P, D])
        v1b = sb("v1b", [P, P])
        esig = sb("esig", [P, D])
        bqk, b1m = ctmp[:, 0:1], ctmp[:, 1:2]
        wg = sb("wg", [P, E])
        bgr = sb("bgr", [P, E])
        b1r = sb("b1r", [E * HT, P])
        b1c = sb("b1c", [P, E * HT])

        big = sb("big", [P, 4 * 2 * TILES * D])
        half_big = 2 * 2 * TILES * D
        stage = big[:, 0:half_big].rearrange("p (x b t d) -> p x b t d", x=2, b=2, t=TILES)
        nat = big[:, half_big:2 * half_big].rearrange("p (x b t d) -> p x b t d", x=2, b=2, t=TILES)
        th = sb("th", [P, 2, 2, S], F32R)
        tl = sb("tl", [P, 2, 2, S], F32R)
        x1 = sb("x1", [P, PAD + B, 2 * D])
        xb = sb("xb", [P, PAD + B, D])

        ex = sb("ex", [P, NE, 2, K])
        xs = sb("xs", [P, NE, 2, D])
        nmin = sb("nmin", [P, NE, 2])
        rsum = sb("rsum", [P, NE, 2])
        rinv = sb("rinv", [P, NE, 2])

        slots = sb("slots", [P, 2, 4, D])
        prevb = sb("prevb", [P, 2, 4, D])
        qhi = sb("qhi", [P, 2, 4 * P], F32R)
        qlo = sb("qlo", [P, 2, 4 * P], F32R)
        epsc = sb("epsc", [P, 2, 2])
        cpart = sb("cpart", [P, 2, 2, 4])
        ut = sb("ut", [P, 4 * P])
        s1 = sb("s1", [P, 4, D])
        s1b = sb("s1b", [P, 4, D])
        sn = sb("sn", [P, 4, D])
        snt = sb("snt", [P, 4 * P])
        gt = sb("gt", [P, 4 * P])
        zt = sb("zt", [P, 4, D])
        rsig = sb("rsig", [P, 4])
        bst = sb("bst", [P, 4, 6])
        mv = sb("mv", [P, 4, 2])
        ve = sb("ve", [P, 4])
        rstd = sb("rstd", [P, 4])
        NS = 2 * TILES + 4
        xbst = sb("xbst", [P, NS, 6])
        xmv = sb("xmv", [P, 2, NS, 2])
        xve = sb("xve", [P, 32])
        xrs = sb("xrs", [P, 2, NS])
        xsd = sb("xsd", [P, 32])

        w1e = sb("w1e", [P, 2, H])
        w2e = sb("w2e", [P, 2, HT, D])
        MS = 32
        rec = big[:, 0:NT * REC].rearrange("p (t r) -> p t r", r=REC)
        at_ = [NT * REC]

        def cut(n):
            at_[0] += n
            return big[:, at_[0] - n:at_[0]]

        xnt = cut(2 * 512).rearrange("p (b n) -> p b n", b=2)
        brow = cut(2 * 2 * REC).rearrange("p (b j r) -> p b j r", b=2, j=2)
        xte = cut(2 * BLK).rearrange("p (b n) -> p b n", b=2)
        ht = ex[:, :, :, :].rearrange("p a b k -> p (a b k)").rearrange("p (b j n) -> p b j n", b=2, j=HT)
        b2e = cut(2 * D).rearrange("p (b n) -> p b n", b=2)
        yo = cut(2 * 2 * D).rearrange("p (b j n) -> p b j n", b=2, j=2)
        ys = cut(2 * 2 * D).rearrange("p (b j n) -> p b j n", b=2, j=2)
        b1e = cut(2 * HT).rearrange("p (b n) -> p b n", b=2)
        fbst = sb("fbst", [P, NT, 6])
        fmv = sb("fmv", [P, NT, 2])
        fve = sb("fve", [P, NT])
        frs = sb("frs", [P, NT])
        ga = [sb(f"ga{i}", [P, E, NT]) for i in range(4)]
        gr = sb("gr", [P, 3, NT])
        ltri = sb("ltri", [P, P])
        iota8 = sb("iota8", [P, E])
        iotaj = sb("iotaj", [P, NBLK])
        scanm = sb("scanm", [P, E * NT])
        cnt = sb("cnt", [P, 6, E])
        cmpb = sb("cmpb", [P, NBLK, E])
        bexp = sb("bexp", [P, NBLK])
        bexpi = sb("bexpi", [P, NBLK], I32)
        posi = sb("posi", [P, NT], U32)
        fill = sb("fill", [P, REC])

        lg = [pb(f"lg{i}", [P, 2, K]) for i in range(NL)]
        pv = [pb(f"pv{i}", [P, 2 * K]) for i in range(2)]
        px = pb("px", [P, 4 * P])
        py = pb("py", [P, 4 * P])
        pz = pb("pz", [P, 4 * P])
        hbank = [lg[0][:, 0, :], lg[1][:, 0, :], lg[2][:, 0, :], pv[0][:, 0:BLK]]

        scratch = nc.dram_tensor("routed", (NBLK * BLK, REC), F32, kind="Internal").ap()

        weights_in = sem("weights_in")
        x_in = sem("x_in")
        rows_in = sem("rows_in")
        stage_in = [sem("stage_p_in"), sem("stage_q_in")]
        consts = sem("consts")
        prep = sem("prep")
        fill_in = sem("fill_in")
        wstep = sem("wstep")
        lg_ready = sem("lg_ready")
        min_ready = sem("min_ready")
        exp_done = sem("exp_done")
        inv_ready = sem("inv_ready")
        xs_ready = sem("xs_ready")
        pv_done = sem("pv_done")
        ut_ready = sem("ut_ready")
        upd_ready = sem("upd_ready")
        stat_ready = sem("stat_ready")
        rstd_ready = sem("rstd_ready")
        sn_ready = sem("sn_ready")
        tr_ready = sem("tr_ready")
        tc_ready = sem("tc_ready")
        h_ready = sem("h_ready")
        g_ready = sem("g_ready")
        s1b_ready = sem("s1b_ready")
        o_ready = sem("o_ready")
        slots_ready = sem("slots_ready")
        qk_ready = sem("qk_ready")
        qhi_ready = sem("qhi_ready")
        qlo_ready = sem("qlo_ready")
        xstat_ready = sem("xstat_ready")
        xrs_ready = sem("xrs_ready")
        ap_ready = sem("ap_ready")
        z_ready = sem("z_ready")
        hi_ready = sem("hi_ready")
        lo_ready = sem("lo_ready")
        fstat = sem("fstat")
        frs_ready = sem("frs_ready")
        xn_ready = sem("xn_ready")
        xt_ready = sem("xt_ready")
        xtc_ready = sem("xtc_ready")
        gate_ready = sem("gate_ready")
        gmax_ready = sem("gmax_ready")
        gexp_ready = sem("gexp_ready")
        hot_ready = sem("hot_ready")
        rank_ready = sem("rank_ready")
        pos_ready = sem("pos_ready")
        recx_ready = sem("recx_ready")
        recid_ready = sem("recid_ready")
        scattered = sem("scattered")
        we_in = [sem(f"we_in{i}") for i in range(2)]
        row_in = [sem(f"row_in{i}") for i in range(2)]
        b1e_ready = sem("b1e_ready")
        bt_ready = sem("bt_ready")
        btc_ready = sem("btc_ready")
        bh_ready = sem("bh_ready")
        bg_ready = sem("bg_ready")
        by_ready = sem("by_ready")
        yo_ready = sem("yo_ready")
        ys_ready = sem("ys_ready")
        out_done = [sem(f"out_done{i}") for i in range(2)]

        WEIGHTS_IN = 16 * (len(W) + 2)
        ROWS_IN = 16 * (len(COLS) + len(ROWS) + 2)

        def ctx_dram(b):
            rows = a["ctx_1024"][b]
            return rows[0:FULL * P, :].rearrange("(p t) d -> p t d", t=FULL), rows[FULL * P:S, :]

        def cols_of(t0, n, rows):
            return slice(t0 * P, t0 * P + (n - 1) * P + rows)

        block = ctx.enter_context(nc.Block())

        @block.sync
        def _(sp):
            def load_stage(x, group):
                for b in range(2):
                    full, tail = ctx_dram(group * 4 + 2 * x + b)
                    sp.dma_start(stage[:, x, b, 0:FULL, :], full).then_inc(stage_in[x], 16)
                    sp.dma_start(stage[0:TAIL, x, b, FULL, :], tail).then_inc(stage_in[x], 16)

            load_stage(0, 0)
            sp.dma_start(x1[:, PAD:PAD + B, :], a["x"].rearrange("b (p j) d -> p b (j d)", j=2)).then_inc(x_in, 16)
            for n in W:
                sp.dma_start(W[n][:, :], a["L0_xcond_" + n]).then_inc(weights_in, 16)
            load_stage(1, 0)
            sp.dma_start(wg[:, :], a["L0_ffn_Wg"]).then_inc(weights_in, 16)
            sp.dma_start(b1r[:, :], a["L0_ffn_b1"].rearrange("e (j p) -> (e j) p", p=P)).then_inc(weights_in, 16)
            sp.wait_ge(fill_in, 1)
            n = NBLK * BLK // P
            for i in range(n):
                sp.dma_start(scratch[i * P:(i + 1) * P, :], fill[:, :]).then_inc(fill_in, 16)

            with sp.Fori(0, GROUPS) as i:
                nxt = (i * 4 + 4) % B
                for x in range(2):
                    sp.wait_ge(ap_ready, i * (2 * PRE) + PRE * (x + 1))
                    for b in range(2):
                        full, tail = ctx_dram(nxt + (2 * x + b))
                        sp.dma_start(stage[:, x, b, 0:FULL, :], full).then_inc(stage_in[x], 16)
                        sp.dma_start(stage[0:TAIL, x, b, FULL, :], tail).then_inc(stage_in[x], 16)

            w1d = a["L0_ffn_W1"]
            w2d = a["L0_ffn_W2"].rearrange("e (j p) d -> e p j d", p=P)
            b2d = a["L0_ffn_b2"]
            rows = scratch.rearrange("(k p j) r -> k p j r", p=P, j=2)
            sp.wait_ge(pos_ready, 1)
            def feed(i, first):
                for k in range(2):
                    e = sp.value_load(bexpi[0:1, bass.ds(i * 2 + k, 1)], min_val=0, max_val=E - 1)
                    if not first:
                        sp.wait_ge(yo_ready, i * 2 + (k - 1))
                    sp.dma_start(w1e[:, k, :], w1d[e]).then_inc(we_in[k], 16)
                    sp.dma_start(w2e[:, k, :, :], w2d[e]).then_inc(we_in[k], 16)
                    sp.dma_start(b2e[:, k, :], b2d[e].partition_broadcast(P)).then_inc(we_in[k], 16)
                    if first:
                        sp.wait_ge(scattered, 16 * NT)
                    else:
                        sp.wait_ge(out_done[k], i * 32)
                    sp.dma_start(brow[:, k, :, :], rows[i * 2 + k]).then_inc(row_in[k], 16)

            feed(0, True)
            with sp.Fori(1, NBLK // 2) as i:
                feed(i, False)

        @block.gpsimd
        def _(pool):
            g = nc.gpsimd
            g.memset(ident[:, :], 0.0)
            g.memset(ltri[:, :], 0.0)
            pool.drain()
            g.affine_select(out=ident[:, :], in_=ident[:, :], compare_op=ALU.not_equal, fill=1.0, base=0,
                            pattern=[[-1, P]], channel_multiplier=1)
            g.affine_select(out=ltri[:, :], in_=ltri[:, :], compare_op=ALU.is_ge, fill=1.0, base=0,
                            pattern=[[-1, P]], channel_multiplier=1)
            g.memset(ones[:, :], 1.0)
            g.memset(negones[:, :], -1.0)
            g.memset(meanw[:, :], 1.0 / D)
            g.memset(epst[:, :], LN_EPS)
            g.memset(neghalf[:, :], -0.5)
            g.memset(half[:, :], 0.5).then_inc(consts, 1)
            g.memset(fill[:, :], 0.0)
            pool.drain()
            g.iota(fill[:, REC - 3:REC - 2].bitcast(U32), [[0, 1]], base=2 * B * K,
                   channel_multiplier=0).then_inc(fill_in, 1)
            g.iota(iota8[:, :], [[1, E]], base=0, channel_multiplier=0, allow_small_or_imprecise_dtypes=True)
            g.iota(iotaj[:, :], [[1, NBLK]], base=0, channel_multiplier=0, allow_small_or_imprecise_dtypes=True)
            g.memset(scanm[:, :], 1.0)
            pool.drain()
            g.memset(scanm[:, :].rearrange("p (e t) -> p e t", t=NT)[:, :, 0:1], 0.0).then_inc(consts, 1)
            with nc.allow_non_contiguous_dma(reason="bias columns: 128 elements each"):
                for n in COLS:
                    pool.dma_start(col[n], a["L0_xcond_" + n].rearrange("(p o) -> p o", o=1)).then_inc(rows_in, 16)
            for n in ROWS:
                src = a["L0_xcond_" + n]
                src = src[0, 0] if len(src.shape) == 3 else src
                pool.dma_start(row[n], src.partition_broadcast(P)).then_inc(rows_in, 16)
            pool.dma_start(bgr[:, :], a["L0_ffn_bg"].partition_broadcast(P)).then_inc(rows_in, 16)
            pool.dma_start(xb[:, PAD:PAD + B, :].rearrange("p b d -> p (b d)"),
                           a["cond_1024"].rearrange("b d -> (b d)").partition_broadcast(P)).then_inc(rows_in, 16)
            g.memset(xb[:, 0:PAD, :], 0.0)
            g.memset(prevb[:, 1, :, :], 0.0)
            pool.wait_ge(rows_in, ROWS_IN)
            g.tensor_tensor(xb[:, PAD:PAD + B, :], xb[:, PAD:PAD + B, :], mid_dim(row["b2"], B), ALU.add)

            def context_rstd(x, count):
                pool.wait_ge(xstat_ready, count)
                g.tensor_tensor(xve[:, 0:NS], xmv[:, x, :, 1], epst[:, 0:NS], ALU.add)
                pool.drain()
                g.tensor_tensor(xrs[:, x, :], xve[:, 0:NS], neghalf[:, 0:NS], ALU.pow)
                g.tensor_tensor(xsd[:, 0:NS], xve[:, 0:NS], half[:, 0:NS], ALU.pow)
                pool.drain()
                m = xmv[:, x, 0:2 * TILES, 0]
                g.tensor_tensor(m, m, xsd[:, 0:2 * TILES], ALU.subtract).then_inc(xrs_ready, 1)

            def layer_rstd(count):
                pool.wait_ge(stat_ready, count)
                g.tensor_tensor(ve[:, :], mv[:, :, 1], epst[:, 0:4], ALU.add)
                pool.drain()
                g.tensor_tensor(rstd[:, :], ve[:, :], neghalf[:, 0:4], ALU.pow).then_inc(rstd_ready, 1)

            def scale_rows(i, n):
                m = n % TRIP
                b, t0, nt, rows = tiles_of(m % SLOTS)
                x = (m // SLOTS) % 2
                k = n % NE
                pool.wait_ge(pv_done, i * TRIP + (n + 1 - NE + CREDIT))
                pool.wait_ge(inv_ready, i * TRIP + (n + 1))
                g.tensor_tensor(xs[0:rows, k, 0:nt, :], nat[0:rows, x, b, t0:t0 + nt, :],
                                last_dim(rinv[0:rows, k, 0:nt], D), ALU.mult).then_inc(xs_ready, 1)

            def new_prevb(x, count):
                pool.wait_ge(slots_ready, count)
                g.tensor_tensor(prevb[:, x, :, :], slots[:, x, :, :], mid_dim(bvu[:, :], 4), ALU.add)

            def add_cond(i, s):
                at = i * 4 + (0 if s == 0 else 4 if s % 2 == 0 else 2)
                for b in range(2):
                    src = xb[:, bass.ds(at + b, 1), :].to_broadcast([P, 2, D])
                    last = g.tensor_tensor(s1b[:, 2 * b:2 * b + 2, :], s1[:, 2 * b:2 * b + 2, :], src, ALU.add)
                last.then_inc(s1b_ready, 1)

            def update_a(i, s, slot):
                u = i * 6 + s
                if slot == 2:
                    layer_rstd(u * 3 + 2)
                    add_cond(i, s)
                if slot == 6:
                    layer_rstd(u * 3 + 3)

            def update_b(i, s, slot):
                u = i * 6 + s
                if slot == 7:
                    layer_rstd(u * 3 + 4)
                    new_prevb(1 - s % 2, u + 2)

            context_rstd(0, 1)
            pool.wait_ge(prep, 3)
            layer_rstd(1)
            new_prevb(0, 1)
            context_rstd(1, 2)
            scale_rows(0, 0)
            with pool.Fori(0, GROUPS) as i:
                for s in range(ROUNDS):
                    for c in range(SLOTS):
                        scale_rows(i, s * SLOTS + c + 1)
                        update_a(i, s, c)
                        update_b(i, s, c)
                        if c == SLOTS - 1 and s in (2, 4):
                            context_rstd(s // 2 - 1, i * 2 + (3 if s == 2 else 4))
            for c in range(SLOTS):
                update_a(GROUPS, 0, c)

            pool.wait_ge(fstat, 1)
            g.tensor_tensor(fve[:, :], fmv[:, :, 1], epst[:, :], ALU.add)
            pool.drain()
            g.tensor_tensor(frs[:, :], fve[:, :], neghalf[:, :], ALU.pow).then_inc(frs_ready, 1)
            g.iota(rec[:, :, 2 * D + 1].bitcast(U32).rearrange("p (b j) -> p b j", j=2), [[K, B], [1, 2]], base=0,
                   channel_multiplier=2).then_inc(recid_ready, 1)
            g.memset(rec[:, :, 2 * D + 2:REC], 0.0).then_inc(recid_ready, 1)
            pool.wait_ge(fill_in, 1 + 16 * (NBLK * BLK // P))
            pool.wait_ge(pos_ready, 1)
            pool.wait_ge(recx_ready, 1)
            pool.wait_ge(recid_ready, 2)
            for t in range(NT):
                g.indirect_dma_start(scratch, bass.IndirectOffsetOnAxis(posi[:, t:t + 1], 0), rec[:, t, :],
                                     None).then_inc(scattered, 16)
            last_row = pool.to_reg(B * K - 1)

            def store(i, first):
                for k in range(2):
                    if not first:
                        pool.wait_ge(out_done[k], i * 32)
                    pool.wait_ge(yo_ready, i * 2 + (k + 1))
                    g.tensor_tensor(ys[:, k, :, :], yo[:, k, :, :], brow[:, k, :, D:2 * D], ALU.add).then_inc(ys_ready, 1)
                    pool.drain()
                    for j in range(2):
                        idx = brow[:, k, j, 2 * D + 1:2 * D + 2].bitcast(U32)
                        g.indirect_dma_start(out.rearrange("b k d -> (b k) d"), bass.IndirectOffsetOnAxis(idx, 0),
                                             ys[:, k, j, :], None, bounds_check=last_row,
                                             oob_is_err=False).then_inc(out_done[k], 16)

            store(0, True)
            with pool.Fori(1, NBLK // 2) as i:
                store(i, False)
            for k in range(2):
                pool.wait_ge(out_done[k], 32 * (NBLK // 2))

        @block.scalar
        def _(act):
            A = nc.scalar.activation

            def exp(i, n):
                _, _, nt, rows = tiles_of(n % SLOTS)
                k = n % NE
                act.wait_ge(pv_done, i * TRIP + (n + 1 - NE + CREDIT))
                act.wait_ge(min_ready, i * TRIP + (n + 1))
                for j in range(nt):
                    last = A(ex[0:rows, k, j, :], lg[n % NL][0:rows, j, :], ACT.Exp, bias=nmin[0:rows, k, j:j + 1],
                             scale=-1.0, accum_out=rsum[0:rows, k, j:j + 1])
                last.then_inc(exp_done, 1)

            def update_a(i, s, slot):
                u = i * 6 + s
                x = 1 - s % 2
                if slot == 0:
                    act.wait_ge(pv_done, i * TRIP + (s * SLOTS + CREDIT))
                    for b in range(2):
                        last = A(ut[:, b * K:(b + 1) * K], pv[x][:, b * K:(b + 1) * K], ACT.Identity,
                                 bias=epsc[:, x, b:b + 1])
                    last.then_inc(ut_ready, 1)
                if slot == 3:
                    act.wait_ge(tr_ready, u * 2 + 2)
                    A(snt[:, :], py[:, :], ACT.Copy).then_inc(tc_ready, 1)
                if slot == 4:
                    act.wait_ge(h_ready, u + 1)
                    A(gt[:, :], px[:, :], ACT.Gelu, bias=b1m).then_inc(g_ready, 1)

            def q_copy(count):
                act.wait_ge(tr_ready, count)
                A(snt[:, :], px[:, :], ACT.Copy).then_inc(tc_ready, 1)

            def q_hi(x, count):
                act.wait_ge(qk_ready, count)
                A(qhi[:, x, :], py[:, :], ACT.Identity, bias=bqk).then_inc(qhi_ready, 1)

            def pre_hi(i, x, r, base):
                act.wait_ge(z_ready, base + r + 1)
                at = 0
                for b, t0, nt, rows in pre_tiles(r):
                    n = (nt - 1) * P + rows
                    q = r % 3 if r < PRE - 1 else 3
                    last = A(th[:, x, b, cols_of(t0, nt, rows)], pz[:, at:at + n], ACT.Copy,
                             accum_out=cpart[:, x, b, q:q + 1])
                    at += P
                last.then_inc(hi_ready, 1)

            act.sem_inc(exp_done, CREDIT)
            act.wait_ge(rows_in, ROWS_IN)
            A(esig[:, :], row["q_logsig"], ACT.Exp).then_inc(prep, 1)
            for r in range(PRE):
                pre_hi(0, 0, r, 0)
            q_copy(1)
            q_hi(0, 1)
            exp(0, 0)
            exp(0, 1)
            with act.Fori(0, GROUPS) as i:
                for s in range(ROUNDS):
                    for c in range(SLOTS):
                        exp(i, s * SLOTS + c + AHEAD)
                        update_a(i, s, c)
                        if c == 9:
                            q_copy(i * 12 + (2 * s + 3))
                        if c == 10:
                            q_hi(1 - s % 2, i * 6 + (s + 2))
                        if s in (0, 5):
                            for r in range(PRE):
                                if PRE_SLOT[r] + 1 == c:
                                    pre_hi(i, 1 if s == 0 else 0, r, i * (2 * PRE) + (PRE if s == 0 else 2 * PRE))
            for c in range(SLOTS):
                update_a(GROUPS, 0, c)

            act.wait_ge(frs_ready, 1)
            for t in range(0, NT, 8):
                last = A(rec[:, t:t + 8, D:2 * D],
                         x1[:, PAD + t // 2:PAD + t // 2 + 4, :].rearrange("p b (j d) -> p (b j) d", d=D), ACT.Copy)
            last.then_inc(recx_ready, 1)
            for r in range(NT // 4):
                act.wait_ge(xt_ready, r + 1)
                if r >= 2:
                    act.wait_ge(gate_ready, r - 1)
                A(xnt[:, r % 2, :], lg[r % 2][:, :, :].rearrange("p a b -> p (a b)"), ACT.Copy).then_inc(xtc_ready, 1)
            act.wait_ge(gmax_ready, 1)
            A(ga[1][:, :, :], ga[1][:, :, :], ACT.Exp).then_inc(gexp_ready, 1)
            with act.Fori(0, NBLK // 2) as i:
                for k in range(2):
                    act.wait_ge(bt_ready, i * 2 + (k + 1))
                    A(xte[:, k, :], px[:, 0:BLK], ACT.Copy).then_inc(btc_ready, 1)
                    act.wait_ge(b1e_ready, i * 2 + (k + 1))
                    for j in range(HT):
                        act.wait_ge(bh_ready, i * (2 * HT) + (k * HT + j + 1))
                        A(ht[:, k, j, :], hbank[j], ACT.Silu,
                          bias=b1e[:, k, j:j + 1]).then_inc(bg_ready, 1)

        @block.vector
        def _(dve):
            v = nc.vector

            def layer_stats(tiles):
                for j in range(4):
                    v.bn_stats(bst[:, j, :], tiles(j))
                dve.drain()
                for j in range(4):
                    last = v.bn_aggr(mv[:, j, :], bst[:, j, :])
                last.then_inc(stat_ready, 1)

            def layer_apply(tiles, count):
                dve.wait_ge(rstd_ready, count)
                for j in range(4):
                    last = v.tensor_scalar(sn[:, j, :], tiles(j), mv[:, j, 0:1], rstd[:, j:j + 1],
                                           ALU.subtract, ALU.mult)
                last.then_inc(sn_ready, 1)

            def row_min(i, n):
                _, _, nt, rows = tiles_of(n % SLOTS)
                dve.wait_ge(lg_ready, i * TRIP + (n + 1))
                v.tensor_reduce(nmin[0:rows, n % NE, 0:nt], lg[n % NL][0:rows, 0:nt, :], AX.X,
                                ALU.min).then_inc(min_ready, 1)

            def row_inv(i, n):
                _, _, nt, rows = tiles_of(n % SLOTS)
                dve.wait_ge(exp_done, i * TRIP + (n + 1 + CREDIT))
                v.reciprocal(rinv[0:rows, n % NE, 0:nt], rsum[0:rows, n % NE, 0:nt]).then_inc(inv_ready, 1)

            def slots_from_x(i, x, at):
                xt = [x1[:, bass.ds(at + j // 2, 1), (j % 2) * D:(j % 2 + 1) * D].rearrange("p a d -> p (a d)")
                      for j in range(4)]
                for j in range(4):
                    n = 2 * TILES + j
                    v.scalar_tensor_tensor(zt[:, j, :], xt[j], xmv[:, x, n, 0:1], esig[:, :], ALU.subtract, ALU.mult)
                dve.drain()
                for j in range(4):
                    n = 2 * TILES + j
                    last = v.scalar_tensor_tensor(slots[:, x, j, :], zt[:, j, :], xrs[:, x, n:n + 1], row["q_mu"],
                                                  ALU.mult, ALU.add)
                last.then_inc(slots_ready, 1)
                dve.drain()

            def context_stats(i, x, n0, n1):
                for n in range(n0, n1):
                    b, t = n // TILES, n % TILES
                    rows = P if t < FULL else TAIL
                    v.bn_stats(xbst[0:rows, n, :], stage[0:rows, x, b, t, :])

            def context_aggr(i, x, at):
                for j in range(4):
                    v.bn_stats(xbst[:, 2 * TILES + j, :],
                               x1[:, bass.ds(at + j // 2, 1), (j % 2) * D:(j % 2 + 1) * D].rearrange("p a d -> p (a d)"))
                dve.drain()
                for n in range(NS):
                    rows = TAIL if n < 2 * TILES and n % TILES == FULL else P
                    last = v.bn_aggr(xmv[0:rows, x, n, :], xbst[0:rows, n, :])
                last.then_inc(xstat_ready, 1)

            def pre_apply(x, r):
                for b, t0, nt, rows in pre_tiles(r):
                    for t in range(t0, t0 + nt):
                        n = b * TILES + t
                        last = v.tensor_scalar(nat[0:rows, x, b, t, :], stage[0:rows, x, b, t, :],
                                               xmv[0:rows, x, n, 0:1], xrs[0:rows, x, n:n + 1],
                                               ALU.subtract, ALU.mult)
                last.then_inc(ap_ready, 1)

            def pre_lo(x, r, base):
                dve.wait_ge(hi_ready, base + r + 1)
                at = 0
                for b, t0, nt, rows in pre_tiles(r):
                    n = (nt - 1) * P + rows
                    cs = cols_of(t0, nt, rows)
                    last = v.tensor_tensor(tl[:, x, b, cs], pz[:, at:at + n], th[:, x, b, cs].bitcast(F32),
                                           ALU.subtract)
                    at += P
                last.then_inc(lo_ready, 1)
                if r == PRE - 1:
                    v.tensor_reduce(epsc[:, x, :], cpart[:, x, :, :], AX.X, ALU.add)
                    dve.drain()
                    v.tensor_scalar(epsc[:, x, :], epsc[:, x, :], ATTN_EPS, None, ALU.mult)

            def q_lo(x, count):
                dve.wait_ge(qhi_ready, count)
                v.scalar_tensor_tensor(qlo[:, x, :], py[:, :], bqk, qhi[:, x, :].bitcast(F32), ALU.add,
                                       ALU.subtract).then_inc(qlo_ready, 1)

            def update_a(i, s, slot):
                u = i * 6 + s
                x = 1 - s % 2
                if slot == 1:
                    dve.wait_ge(upd_ready, u + 1)
                    v.reciprocal(rsig[:, :], py[:, 0:4])
                    dve.drain()
                    for j in range(4):
                        v.scalar_tensor_tensor(s1[:, j, :], px[:, j * D:(j + 1) * D], rsig[:, j:j + 1],
                                               prevb[:, x, j, :], ALU.mult, ALU.add)
                    dve.drain()
                    layer_stats(lambda j: s1[:, j, :])
                if slot == 2:
                    layer_apply(lambda j: s1[:, j, :], u * 3 + 2)
                if slot == 5:
                    dve.wait_ge(s1b_ready, u + 1)
                    dve.wait_ge(o_ready, u + 1)
                    v.tensor_tensor(zt[:, :, :], py[:, :].rearrange("p (j d) -> p j d", j=4), s1b[:, :, :], ALU.add)
                    dve.drain()
                    layer_stats(lambda j: zt[:, j, :])
                if slot == 6:
                    dve.wait_ge(rstd_ready, u * 3 + 3)
                    for j in range(4):
                        v.scalar_tensor_tensor(sn[:, j, :], zt[:, j, :], mv[:, j, 0:1], row["lnp_g"],
                                               ALU.subtract, ALU.mult)
                    dve.drain()
                    for j in range(4):
                        last = v.scalar_tensor_tensor(slots[:, x, j, :], sn[:, j, :], rstd[:, j:j + 1], row["lnp_b"],
                                                      ALU.mult, ALU.add)
                    if s not in (0, 5):
                        last.then_inc(slots_ready, 1)
                    dve.drain()
                    if s in (0, 5):
                        at = i * 4 + (0 if s == 0 else 2)
                        dst = x1[:, bass.ds(at, 2), :] if not isinstance(at, int) else x1[:, at:at + 2, :]
                        v.tensor_tensor(dst, dst, slots[:, x, :, :].rearrange("p (b j) d -> p b (j d)", j=2),
                                        ALU.add)
                        dve.drain()

            def update_b(i, s, slot):
                u = i * 6 + s
                x = 1 - s % 2
                if slot == 6:
                    if s == 0:
                        slots_from_x(i, 1, i * 4 + (PAD + 2))
                    if s == 5:
                        slots_from_x(i, 0, (i * 4 + 4) % B + PAD)
                    layer_stats(lambda j: slots[:, x, j, :])
                if slot == 8:
                    layer_apply(lambda j: slots[:, x, j, :], u * 3 + 4)
                if slot == 11:
                    q_lo(x, u + 2)

            v.memset(x1[:, 0:PAD, :], 0.0)
            v.memset(slots[:, 1, :, :], 0.0)
            v.memset(epsc[:, :, :], 0.0)
            v.memset(xmv[:, :, :, :], 0.0)
            v.memset(xbst[:, :, :], 0.0)
            v.memset(pv[1][:, :], 1.0).then_inc(prep, 1)
            dve.drain()
            dve.wait_ge(stage_in[0], 64)
            context_stats(0, 0, 0, 2 * TILES)
            dve.wait_ge(x_in, 16)
            context_aggr(0, 0, PAD)
            dve.wait_ge(weights_in, WEIGHTS_IN)
            dve.wait_ge(rows_in, ROWS_IN)
            v.tensor_scalar(wtmp[:, 0, :], W["wk"][:, :], col["lnkv_g"], None, ALU.mult)
            v.tensor_scalar(wtmp[:, 1, :], W["wq"][:, :], col["lnq_g"], None, ALU.mult)
            v.tensor_scalar(wtmp[:, 2, :], W["wv"][:, :], col["lnkv_g"], None, ALU.mult)
            v.tensor_scalar(w1g[:, :], W["w1"][:, :], col["lnm_g"], None, ALU.mult).then_inc(consts, 1)
            dve.wait_ge(wstep, 1)
            pc = px[:, 0:8]
            v.tensor_tensor(ctmp[:, 2:3], pc[:, 0:1], col["bk"], ALU.add)
            v.tensor_tensor(ctmp[:, 3:4], pc[:, 1:2], col["bq"], ALU.add)
            v.tensor_tensor(ctmp[:, 4:5], pc[:, 2:3], col["bv"], ALU.add)
            v.tensor_tensor(b1m, pc[:, 3:4], col["b1"], ALU.add)
            dve.drain()
            v.tensor_tensor(ctmp[:, 5:6], ctmp[:, 2:3], pc[:, 4:5], ALU.subtract)
            dve.drain()
            v.tensor_scalar(ctmp[:, 6:7], ctmp[:, 5:6], 1.0 / D, None, ALU.mult)
            dve.drain()
            v.tensor_scalar(wtmp[:, 3, :], py[:, 0:D], ctmp[:, 6:7], None, ALU.add)
            v.tensor_copy(wtmp[:, 4, :], py[:, D:2 * D])
            v.tensor_copy(wtmp[:, 5, :], py[:, 2 * D:3 * D])
            v.tensor_scalar(v1b[:, :], ones[:, :], ctmp[:, 4:5], None, ALU.mult).then_inc(consts, 1)
            dve.wait_ge(wstep, 2)
            v.tensor_scalar(wqk[:, :], pz[:, 0:D], -float(D) ** 0.5, None, ALU.mult)
            v.tensor_scalar(bqk, pz[:, 2 * D:2 * D + 1], -float(D) ** 0.5, None, ALU.mult)
            v.tensor_copy(wvu[:, :], pz[:, D:2 * D]).then_inc(consts, 1)
            dve.wait_ge(wstep, 3)
            v.tensor_tensor(bvu[:, :], px[:, 0:D], row["bu"], ALU.add)
            v.tensor_copy(b1c[:, :], py[:, 0:E * HT]).then_inc(prep, 1)
            dve.wait_ge(prep, 3)
            dve.wait_ge(xrs_ready, 1)
            for r in range(PRE):
                pre_apply(0, r)
                if r:
                    pre_lo(0, r - 1, 0)
                if r == 1:
                    slots_from_x(0, 0, PAD)
                    layer_stats(lambda j: slots[:, 0, j, :])
                if r == 3:
                    layer_apply(lambda j: slots[:, 0, j, :], 1)
            pre_lo(0, PRE - 1, 0)
            q_lo(0, 1)
            row_min(0, 0)
            dve.wait_ge(stage_in[1], 64)
            row_min(0, 1)
            row_inv(0, 0)
            context_stats(0, 1, 0, 2 * TILES)
            context_aggr(0, 1, PAD + 2)

            with dve.Fori(0, GROUPS) as i:
                for s in range(ROUNDS):
                    px_ = 1 if s == 0 else 0
                    for c in range(SLOTS):
                        n = s * SLOTS + c
                        if s in (0, 5):
                            for r in range(PRE):
                                if PRE_SLOT[r] + 2 == c:
                                    pre_lo(px_, r, i * (2 * PRE) + (PRE if s == 0 else 2 * PRE))
                        row_min(i, n + AHEAD)
                        row_inv(i, n + 1)
                        update_a(i, s, c)
                        update_b(i, s, c)
                        if s in (0, 5):
                            for r in range(PRE):
                                if PRE_SLOT[r] == c:
                                    if r == 0:
                                        dve.wait_ge(xrs_ready, i * 2 + (2 if s == 0 else 3))
                                        dve.wait_ge(pv_done, i * TRIP + (s * SLOTS + CREDIT))
                                    pre_apply(px_, r)
                        if s in (2, 4):
                            x = s // 2 - 1
                            if c == 0:
                                dve.wait_ge(stage_in[x], i * 64 + 128)
                            if c < TILES:
                                context_stats(i, x, 2 * c, 2 * c + 2)
                            else:
                                context_aggr(i, x, (i * 4 + 4) % B + (PAD + 2 * x))
            for c in range(7):
                update_a(GROUPS, 0, c)

            def x1t(t):
                return x1[:, PAD + t // 2, (t % 2) * D:(t % 2 + 1) * D]

            for t in range(NT):
                v.bn_stats(fbst[:, t, :], x1t(t))
            dve.drain()
            for t in range(NT):
                last = v.bn_aggr(fmv[:, t, :], fbst[:, t, :])
            last.then_inc(fstat, 1)
            dve.wait_ge(frs_ready, 1)
            for t in range(NT):
                last = v.tensor_scalar(rec[:, t, 0:D], x1t(t), fmv[:, t, 0:1], frs[:, t:t + 1],
                                       ALU.subtract, ALU.mult)
                if t % 4 == 3:
                    last.then_inc(xn_ready, 1)
            dve.wait_ge(gate_ready, NT // 4)
            v.tensor_tensor(ga[0][:, :, :], pv[0][:, 0:NT * E].rearrange("p (t e) -> p e t", e=E),
                            last_dim(bgr[:, :], NT), ALU.add)
            dve.drain()
            v.tensor_reduce(gr[:, 0, :], ga[0][:, :, :].rearrange("p e t -> p t e"), AX.X, ALU.max)
            dve.drain()
            v.tensor_tensor(ga[1][:, :, :], ga[0][:, :, :], mid_dim(gr[:, 0, :], E), ALU.subtract).then_inc(gmax_ready, 1)
            v.tensor_tensor(ga[2][:, :, :], ga[0][:, :, :], mid_dim(gr[:, 0, :], E), ALU.is_equal)
            dve.drain()
            v.scalar_tensor_tensor(ga[3][:, :, :], ga[2][:, :, :], -64.0, last_dim(iota8[:, :], NT), ALU.mult, ALU.add)
            dve.drain()
            v.tensor_reduce(gr[:, 1, :], ga[3][:, :, :].rearrange("p e t -> p t e"), AX.X, ALU.min)
            dve.drain()
            v.tensor_tensor(ga[2][:, :, :], ga[3][:, :, :], mid_dim(gr[:, 1, :], E), ALU.is_equal).then_inc(hot_ready, 1)
            dve.wait_ge(gexp_ready, 1)
            v.tensor_reduce(gr[:, 2, :], ga[1][:, :, :].rearrange("p e t -> p t e"), AX.X, ALU.add)
            dve.drain()
            v.reciprocal(rec[:, :, 2 * D], gr[:, 2, :])
            dve.wait_ge(rank_ready, 1)
            prefix = pv[1][:, 0:E * NT].rearrange("p (e t) -> p e t", e=E)
            totals = pv[1][:, E * NT:2 * E * NT].rearrange("p (e t) -> p e t", e=E)
            v.tensor_tensor_scan(ga[3][:, :, :].rearrange("p e t -> p (e t)"), scanm[:, :],
                                 pv[1][:, E * NT:2 * E * NT], 0.0, ALU.mult, ALU.add)
            dve.drain()
            v.tensor_tensor(ga[0][:, :, :], ga[3][:, :, :], totals, ALU.subtract)
            v.tensor_scalar(cnt[:, 0, :], ga[3][:, :, NT - 1], 1.0 / BLK, None, ALU.mult)
            dve.drain()
            v.tensor_tensor(cmpb[:, :, :], mid_dim(cnt[:, 0, :], NBLK), last_dim(iotaj[:, :], E), ALU.is_gt)
            v.tensor_tensor(ga[0][:, :, :], ga[0][:, :, :], prefix, ALU.add)
            dve.drain()
            v.tensor_reduce(cnt[:, 1, :], cmpb[:, :, :].rearrange("p j e -> p e j"), AX.X, ALU.add)
            dve.drain()
            src = 1
            for step, dst in ((1, 2), (2, 3), (4, 4)):
                v.tensor_copy(cnt[:, dst, 0:step], cnt[:, src, 0:step])
                v.tensor_tensor(cnt[:, dst, step:E], cnt[:, src, step:E], cnt[:, src, 0:E - step], ALU.add)
                dve.drain()
                src = dst
            v.tensor_tensor(cnt[:, 5, :], cnt[:, 4, :], cnt[:, 1, :], ALU.subtract)
            v.tensor_tensor(cmpb[:, :, :], last_dim(iotaj[:, :], E), mid_dim(cnt[:, 4, :], NBLK), ALU.is_ge)
            dve.drain()
            v.scalar_tensor_tensor(ga[1][:, :, :], last_dim(cnt[:, 5, :], NT), float(BLK), ga[0][:, :, :],
                                   ALU.mult, ALU.add)
            v.tensor_reduce(bexp[:, :], cmpb[:, :, :], AX.X, ALU.add)
            dve.drain()
            v.tensor_tensor(ga[3][:, :, :], ga[1][:, :, :], ga[2][:, :, :], ALU.mult)
            v.tensor_scalar(bexpi[:, :], bexp[:, :], float(E - 1), None, ALU.min)
            dve.drain()
            v.tensor_reduce(gr[:, 0, :], ga[3][:, :, :].rearrange("p e t -> p t e"), AX.X, ALU.add)
            dve.drain()
            v.tensor_copy(posi[:, :], gr[:, 0, :]).then_inc(pos_ready, 1)
            dve.drain()

            def finish(i, first):
                for k in range(2):
                    e = dve.value_load(bexpi[0:1, bass.ds(i * 2 + k, 1)], min_val=0, max_val=E - 1)
                    v.tensor_copy(b1e[:, k, :], b1c[:, bass.ds(e * HT, HT)]).then_inc(b1e_ready, 1)
                    dve.wait_ge(we_in[k], i * 48 + 48)
                    dve.wait_ge(row_in[k], i * 16 + 16)
                    if not first:
                        dve.wait_ge(ys_ready, i * 2 + (k - 1))
                    dve.wait_ge(by_ready, i * 2 + (k + 1))
                    v.tensor_tensor(yo[:, k, :, :], pz[:, 0:2 * D].rearrange("p (j d) -> p j d", j=2),
                                    mid_dim(b2e[:, k, :], 2), ALU.add)
                    dve.drain()
                    for j in range(2):
                        last = v.tensor_scalar(yo[:, k, j, :], yo[:, k, j, :], brow[:, k, j, 2 * D:2 * D + 1], None,
                                               ALU.mult)
                    last.then_inc(yo_ready, 1)

            finish(0, True)
            with dve.Fori(1, NBLK // 2) as i:
                finish(i, False)

        @block.tensor
        def _(pe):
            mm = nc.tensor.matmul

            def logits(i, n):
                m = n % TRIP
                x, c = (m // SLOTS) % 2, m % SLOTS
                b, t0, nt, rows = tiles_of(c)
                pe.wait_ge(exp_done, i * TRIP + (n + 1 - NL + CREDIT))
                for j in range(nt):
                    cs = slice((t0 + j) * P, (t0 + j) * P + rows)
                    qs = slice(b * K, (b + 1) * K)
                    o = lg[n % NL][0:rows, j, :]
                    mm(o, th[:, x, b, cs], qhi[:, x, qs], start=True, stop=False)
                    mm(o, tl[:, x, b, cs], qhi[:, x, qs], start=False, stop=False)
                    last = mm(o, th[:, x, b, cs], qlo[:, x, qs], start=False, stop=True)
                last.then_inc(lg_ready, 1)

            def product(i, n):
                x, c = (n // SLOTS) % 2, n % SLOTS
                b, t0, nt, rows = tiles_of(c)
                k = n % NE
                pe.wait_ge(xs_ready, i * TRIP + (n + 1))
                for j in range(nt):
                    last = mm(pv[x][:, b * K:(b + 1) * K], xs[0:rows, k, j, :], ex[0:rows, k, j, :],
                              start=(t0 + j == 0), stop=(t0 + j == FULL))
                last.then_inc(pv_done, 1)

            def update_a(i, s, slot):
                u = i * 6 + s
                if slot == 1:
                    pe.wait_ge(ut_ready, u + 1)
                    for j in range(4):
                        mm(py[:, j:j + 1], ut[:, j * P:(j + 1) * P], meanw[:, :], start=True, stop=True)
                    for j in range(4):
                        last = mm(px[:, j * D:(j + 1) * D], ut[:, j * P:(j + 1) * P], wvu[:, :], start=True, stop=True)
                    last.then_inc(upd_ready, 1)
                if slot == 3:
                    pe.wait_ge(sn_ready, u * 2 + 2)
                    for j in range(4):
                        last = nc.tensor.transpose(py[:, j * P:(j + 1) * P], sn[:, j, :], ident[:, :])
                    last.then_inc(tr_ready, 1)
                if slot == 4:
                    pe.wait_ge(tc_ready, u * 2 + 2)
                    mm(px[:, :], w1g[:, :], snt[:, :], start=True, stop=True).then_inc(h_ready, 1)
                if slot == 5:
                    pe.wait_ge(g_ready, u + 1)
                    for j in range(4):
                        last = mm(py[:, j * D:(j + 1) * D], gt[:, j * P:(j + 1) * P], W["w2"][:, :],
                                  start=True, stop=True)
                    last.then_inc(o_ready, 1)

            def q_transpose(count):
                pe.wait_ge(sn_ready, count)
                for j in range(4):
                    last = nc.tensor.transpose(px[:, j * P:(j + 1) * P], sn[:, j, :], ident[:, :])
                last.then_inc(tr_ready, 1)

            def q_product(count):
                pe.wait_ge(tc_ready, count)
                mm(py[:, :], wqk[:, :], snt[:, :], start=True, stop=True).then_inc(qk_ready, 1)

            def pre_transpose(x, r, base, first=False):
                if not first:
                    pe.wait_ge(lo_ready, base + r)
                pe.wait_ge(ap_ready, base + r + 1)
                at = 0
                for b, t0, nt, rows in pre_tiles(r):
                    for t in range(t0, t0 + nt):
                        last = nc.tensor.transpose(pz[:, at:at + rows], nat[0:rows, x, b, t, :], ident[0:rows, 0:rows])
                        at += P
                last.then_inc(z_ready, 1)

            pe.sem_inc(pv_done, CREDIT)
            pe.wait_ge(consts, 3)
            pe.wait_ge(weights_in, WEIGHTS_IN)
            pe.wait_ge(rows_in, ROWS_IN)
            mm(px[:, 0:1], W["wk"][:, :], col["lnkv_b"], start=True, stop=True)
            mm(px[:, 1:2], W["wq"][:, :], col["lnq_b"], start=True, stop=True)
            mm(px[:, 2:3], W["wv"][:, :], col["lnkv_b"], start=True, stop=True)
            mm(px[:, 3:4], W["w1"][:, :], col["lnm_b"], start=True, stop=True)
            mm(px[:, 4:5], wtmp[:, 0, :], ones[:, 0:1], start=True, stop=True)
            for j in range(3):
                last = nc.tensor.transpose(py[:, j * D:(j + 1) * D], wtmp[:, j, :], ident[:, :])
            last.then_inc(wstep, 1)
            pe.wait_ge(consts, 4)
            mm(pz[:, 0:D], wtmp[:, 4, :], wtmp[:, 3, :], start=True, stop=True)
            mm(pz[:, D:2 * D], wtmp[:, 5, :], W["wu"][:, :], start=True, stop=True)
            mm(pz[:, 2 * D:2 * D + 1], wtmp[:, 3, :], ctmp[:, 3:4], start=True, stop=True).then_inc(wstep, 1)
            pe.wait_ge(consts, 5)
            mm(px[:, 0:D], v1b[:, :], W["wu"][:, :], start=True, stop=False)
            mm(px[:, 0:D], negones[:, :], wvu[:, :], start=False, stop=True)
            nc.tensor.transpose(py[:, 0:E * HT], b1r[:, :], ident[0:E * HT, 0:E * HT]).then_inc(wstep, 1)
            for r in range(PRE):
                pre_transpose(0, r, 0, first=(r == 0))
            q_transpose(1)
            q_product(1)
            pe.wait_ge(lo_ready, PRE)
            pe.wait_ge(qlo_ready, 1)
            logits(0, 0)
            logits(0, 1)

            with pe.Fori(0, GROUPS) as i:
                for s in range(ROUNDS):
                    for c in range(SLOTS):
                        n = s * SLOTS + c
                        if (n + AHEAD) % SLOTS == 0:
                            if s == 0:
                                pe.wait_ge(lo_ready, i * (2 * PRE) + 2 * PRE)
                            if s == 5:
                                pe.wait_ge(lo_ready, i * (2 * PRE) + 3 * PRE)
                            pe.wait_ge(qlo_ready, i * 6 + (s + 2))
                        logits(i, n + AHEAD)
                        product(i, n)
                        update_a(i, s, c)
                        if c == 9:
                            q_transpose(i * 12 + (2 * s + 3))
                        if c == 10:
                            q_product(i * 12 + (2 * s + 3))
                        if s in (0, 5):
                            for r in range(PRE):
                                if PRE_SLOT[r] + 1 == c:
                                    pre_transpose(1 if s == 0 else 0, r, i * (2 * PRE) + (PRE if s == 0 else 2 * PRE))
            for c in range(SLOTS):
                update_a(GROUPS, 0, c)

            pe.wait_ge(exp_done, GROUPS * TRIP + AHEAD + CREDIT)
            for r in range(NT // 4):
                pe.wait_ge(xn_ready, r + 1)
                if r >= 2:
                    pe.wait_ge(xtc_ready, r - 1)
                for j in range(4):
                    last = nc.tensor.transpose(lg[r % 2][:, j // 2, (j % 2) * P:(j % 2 + 1) * P],
                                               rec[:, 4 * r + j, 0:D], ident[:, :])
                last.then_inc(xt_ready, 1)
                pe.wait_ge(xtc_ready, r + 1)
                for j in range(4):
                    t = 4 * r + j
                    last = mm(pv[0][:, t * E:(t + 1) * E], xnt[:, r % 2, j * P:(j + 1) * P], wg[:, :],
                              start=True, stop=True)
                last.then_inc(gate_ready, 1)
            pe.wait_ge(hot_ready, 1)
            hot = ga[2][:, :, :].rearrange("p e t -> p (e t)")
            mm(pv[1][:, 0:E * NT], ltri[:, :], hot, start=True, stop=True)
            mm(pv[1][:, E * NT:2 * E * NT], ones[:, :], hot, start=True, stop=True).then_inc(rank_ready, 1)

            def expert(i, first):
                for k in range(2):
                    pe.wait_ge(row_in[k], i * 16 + 16)
                    for j in range(2):
                        last = nc.tensor.transpose(px[:, j * P:(j + 1) * P], brow[:, k, j, 0:D], ident[:, :])
                    last.then_inc(bt_ready, 1)
                    pe.wait_ge(we_in[k], i * 48 + 48)
                    pe.wait_ge(btc_ready, i * 2 + (k + 1))
                    for j in range(HT):
                        mm(hbank[j], w1e[:, k, j * P:(j + 1) * P], xte[:, k, :],
                           start=True, stop=True).then_inc(bh_ready, 1)
                    if k or not first:
                        pe.wait_ge(yo_ready, i * 2 + k)
                    for r in range(2):
                        for j in range(HT):
                            if r == 0:
                                pe.wait_ge(bg_ready, i * (2 * HT) + (k * HT + j + 1))
                            last = mm(pz[:, r * D:(r + 1) * D], ht[:, k, j, r * P:(r + 1) * P], w2e[:, k, j, :],
                                      start=(j == 0), stop=(j == HT - 1))
                    last.then_inc(by_ready, 1)

            expert(0, True)
            with pe.Fori(1, NBLK // 2) as i:
                expert(i, False)


_INS = ['x', 'cond_1024', 'ctx_1024'] + ['L0_xcond_' + n for n in (
    'q_mu', 'q_logsig', 'lnkv_g', 'lnkv_b', 'lnq_g', 'lnq_b', 'lnm_g', 'lnm_b', 'lnp_g', 'lnp_b', 'wk', 'bk',
    'wv', 'bv', 'wq', 'bq', 'wu', 'bu', 'w1', 'b1', 'w2', 'b2')] + ['L0_ffn_' + n for n in (
        'Wg', 'bg', 'W1', 'b1', 'W2', 'b2')]


def kernel(**inputs):
    import numpy as _np
    import concourse.bacc as _bacc
    from concourse import mybir as _mybir
    from concourse.bass_utils import run_bass_kernel_spmd as _run

    nc = _bacc.Bacc("TRN2", target_bir_lowering=False, num_devices=1)
    arrays, aps = {}, {}
    for name in _INS:
        arr = _np.ascontiguousarray(inputs[name])
        arrays[f"in_{name}"] = arr
        aps[name] = nc.dram_tensor(f"in_{name}", arr.shape, _mybir.dt.from_np(arr.dtype), kind="ExternalInput").ap()
    out = nc.dram_tensor("out", (B, K, D), F32, kind="ExternalOutput").ap()
    build(nc, aps, out)
    r = _run(nc, [arrays], core_ids=[0])
    return r.results[0]["out"]
```

```python
import concourse.bass as bass
from concourse import mybir
from contextlib import ExitStack

F32 = mybir.dt.float32
F32R = mybir.dt.float32r
U32 = mybir.dt.uint32
I32 = mybir.dt.int32
ALU = mybir.AluOpType
ACT = mybir.ActivationFunctionType
AX = mybir.AxisListType

B, K, D, S = 16, 256, 128, 1601
P = 128
LN_EPS, ATTN_EPS = 1e-5, 1e-8
GROUPS = B // 4
FULL = S // P
TAIL = S - FULL * P
TILES = FULL + 1
CH = 7
SLOTS = 2 * CH
ROUNDS = 6
TRIP = ROUNDS * SLOTS
NL = 3
NE = 4
CR = 2
CREDIT = 4
AHEAD = 3
SCALE = 2
PAD = 2
PRE = 8
PRE_SLOT = [0, 1, 2, 4, 6, 7, 9, 10]
POOLQ = 0
ORDER = 1
TRANSPOSE = 2
LOWER = 3
PPRE = 6
E, H = 8, 512
HT = H // P
BLK = 256
NBLK = B * K // BLK + E
NT = B * K // P
REC = 2 * D + 4


STEPS = dict(
    ut=0, upd=0, s1=1, ap1=2, tr1=2, tc1=2, cond=3, hid=3, gelu=3,
    mm2=6, z=7, rsp=7, nrm=9, stq=10, prev=11,
    apq=11, trq=13, tcq=13, qk=15, qhi=15, qlo=17)
Q_STEPS = ("stq", "apq", "trq", "tcq", "qk", "qhi", "qlo")


def when(step, h):
    at = CH * (h + 1) + STEPS[step]
    return at % SLOTS, at // SLOTS


def tiles_of(c):
    b, k = c // CH, c % CH
    return (b, 2 * k, 2, P) if k < CH - 1 else (b, 2 * k, 1, TAIL)


def pre_tiles(r):
    return (r // 4, 4 * (r % 4), 4, P) if r % 4 < 3 else (r // 4, FULL, 1, TAIL)


def last_dim(ap, n):
    return ap.rearrange("p (a b) -> p a b", b=1).to_broadcast([ap.shape[0], ap.shape[1], n])


def mid_dim(ap, n):
    return ap.rearrange("p (b a) -> p b a", b=1).to_broadcast([ap.shape[0], n, ap.shape[1]])


def build(nc, a, out):
    ctx = ExitStack()
    with ctx:
        def sb(name, shape, dt=F32):
            return ctx.enter_context(nc.sbuf_tensor(name, shape, dt))

        def pb(name, shape, dt=F32):
            return ctx.enter_context(nc.psum_tensor(name, shape, dt))

        def sem(name):
            return ctx.enter_context(nc.semaphore(name))

        W = {n: sb("w_" + n, [P, D]) for n in ("wk", "wv", "wq", "wu", "w1", "w2")}
        COLS = ("lnkv_g", "lnkv_b", "lnq_g", "lnq_b", "lnm_g", "lnm_b", "bk", "bv", "bq", "b1")
        cols = sb("cols", [P, len(COLS)])
        col = {n: cols[:, i:i + 1] for i, n in enumerate(COLS)}
        ROWS = ("lnp_g", "lnp_b", "b2", "bu", "q_mu", "q_logsig")
        rowt = sb("rowt", [P, len(ROWS), D])
        row = {n: rowt[:, i, :] for i, n in enumerate(ROWS)}
        ident = sb("ident", [P, P])
        ones = sb("ones", [P, P])
        negones = sb("negones", [P, P])
        meanw = sb("meanw", [P, 1])
        epst = sb("epst", [P, 32])
        neghalf = sb("neghalf", [P, 32])
        half = sb("half", [P, 32])
        wtmp = sb("wtmp", [P, 6, D])
        ctmp = sb("ctmp", [P, 8])
        wqk = sb("wqk", [P, D])
        wvu = sb("wvu", [P, D])
        w1g = sb("w1g", [P, D])
        bvu = sb("bvu", [P, D])
        v1b = sb("v1b", [P, P])
        esig = sb("esig", [P, D])
        bqk, b1m = ctmp[:, 0:1], ctmp[:, 1:2]
        wg = sb("wg", [P, E])
        bgr = sb("bgr", [P, E])
        b1r = sb("b1r", [E * HT, P])
        b1c = sb("b1c", [P, E * HT])

        big = sb("big", [P, 4 * 2 * TILES * D])
        half_big = 2 * 2 * TILES * D
        stage = big[:, 0:half_big].rearrange("p (x b t d) -> p x b t d", x=2, b=2, t=TILES)
        nat = big[:, half_big:2 * half_big].rearrange("p (x b t d) -> p x b t d", x=2, b=2, t=TILES)
        th = sb("th", [P, 2, 2, S], F32R)
        tl = sb("tl", [P, 2, 2, S], F32R)
        x1 = sb("x1", [P, PAD + B, 2 * D])
        xb = sb("xb", [P, PAD + B, D])

        ex = sb("ex", [P, NE, 2, K])
        xs = sb("xs", [P, NE, 2, D])
        nmin = sb("nmin", [P, NE, 2])
        rsum = sb("rsum", [P, NE, 2])
        rinv = sb("rinv", [P, NE, 2])

        slots = sb("slots", [P, 4, D])
        slots0 = sb("slots0", [P, 2, 4, D])
        prevb = sb("prevb", [P, 2, 4, D])
        qhi = sb("qhi", [P, 2, 4 * P], F32R)
        qlo = sb("qlo", [P, 2, 4 * P], F32R)
        epsc = sb("epsc", [P, 2, 2])
        cpart = sb("cpart", [P, 2, 2, 4])
        ut = sb("ut", [P, 2, K])
        upd = sb("upd", [P, 8 * 4 * D])
        s1, s1b, sn1, zt, zg, snq = [upd[:, k * 4 * D:(k + 1) * 4 * D].rearrange("p (j d) -> p j d", j=4)
                                     for k in (0, 1, 2, 3, 4, 5)]
        snt, gt = [upd[:, k * 4 * D:(k + 1) * 4 * D] for k in (6, 7)]
        snqt = sb("snqt", [P, 2, K])
        rsig = sb("rsig", [P, 4])
        bst = sb("bst", [P, 3, 4, 6])
        mv = sb("mv", [P, 3, 4, 2])
        ve = sb("ve", [P, 3, 4])
        mneg = sb("mneg", [P, 3, 4])
        rstd = sb("rstd", [P, 3, 4])
        NS = 2 * TILES + 4
        xbst = sb("xbst", [P, NS, 6])
        xmv = sb("xmv", [P, 2, NS, 2])
        xve = sb("xve", [P, 32])
        xrs = sb("xrs", [P, 2, NS])
        xsd = sb("xsd", [P, 32])

        w1e = upd[:, 0:2 * H].rearrange("p (b n) -> p b n", b=2)
        w2e = upd[:, 2 * H:2 * H + 2 * HT * D].rearrange("p (b j d) -> p b j d", b=2, j=HT)
        MS = 32
        rec = big[:, 0:NT * REC].rearrange("p (t r) -> p t r", r=REC)
        at_ = [NT * REC]

        def cut(n):
            at_[0] += n
            return big[:, at_[0] - n:at_[0]]

        xnt = cut(2 * 512).rearrange("p (b n) -> p b n", b=2)
        brow = cut(2 * 2 * REC).rearrange("p (b j r) -> p b j r", b=2, j=2)
        xte = cut(2 * BLK).rearrange("p (b n) -> p b n", b=2)
        ht = ex[:, :, :, :].rearrange("p a b k -> p (a b k)")[:, 0:2 * HT * BLK].rearrange("p (b j n) -> p b j n", b=2, j=HT)
        b2e = cut(2 * D).rearrange("p (b n) -> p b n", b=2)
        yo = cut(2 * 2 * D).rearrange("p (b j n) -> p b j n", b=2, j=2)
        ys = cut(2 * 2 * D).rearrange("p (b j n) -> p b j n", b=2, j=2)
        b1e = cut(2 * HT).rearrange("p (b n) -> p b n", b=2)
        fbst = sb("fbst", [P, NT, 6])
        fmv = sb("fmv", [P, NT, 2])
        fve = sb("fve", [P, NT])
        frs = sb("frs", [P, NT])
        ga = [cut(E * NT).rearrange("p (e t) -> p e t", e=E) for i in range(4)]
        gr = sb("gr", [P, 3, NT])
        ltri = sb("ltri", [P, P])
        iota8 = sb("iota8", [P, E])
        iotaj = sb("iotaj", [P, NBLK])
        scanm = sb("scanm", [P, E * NT])
        cnt = sb("cnt", [P, 6, E])
        cmpb = sb("cmpb", [P, NBLK, E])
        bexp = sb("bexp", [P, NBLK])
        bexpi = sb("bexpi", [P, NBLK], I32)
        posi = sb("posi", [P, NT], U32)
        fill = sb("fill", [P, REC])

        lg = [pb(f"lg{i}", [P, 2, K]) for i in range(NL)]
        pv = [pb(f"pv{i}", [P, 2 * K]) for i in range(2)]
        px = pb("px", [P, 4 * P])
        py = pb("py", [P, 4 * P])
        pz = pb("pz", [P, 4 * P])
        hbank = [lg[0][:, 0, :], lg[1][:, 0, :], lg[2][:, 0, :], pv[0][:, 0:BLK]]

        scratch = nc.dram_tensor("routed", (NBLK * BLK, REC), F32, kind="Internal").ap()

        weights_in = sem("weights_in")
        x_in = sem("x_in")
        rows_in = sem("rows_in")
        stage_in = [sem("stage_p_in"), sem("stage_q_in")]
        consts = sem("consts")
        prep = sem("prep")
        fill_in = sem("fill_in")
        wstep = sem("wstep")
        lg_ready = sem("lg_ready")
        min_ready = sem("min_ready")
        exp_done = sem("exp_done")
        inv_ready = sem("inv_ready")
        xs_ready = sem("xs_ready")
        pv_done = sem("pv_done")
        def halves(name):
            return [sem(name + "_a"), sem(name + "_b")]

        ut_ready = halves("ut_ready")
        upd_ready = halves("upd_ready")
        st1_ready = halves("st1_ready")
        sn1_ready = halves("sn1_ready")
        tr1_ready = halves("tr1_ready")
        tc1_ready = halves("tc1_ready")
        s1b_ready = halves("s1b_ready")
        h_ready = halves("h_ready")
        g_ready = halves("g_ready")
        o_ready = halves("o_ready")
        stp_ready = halves("stp_ready")
        rsp_ready = halves("rsp_ready")
        slots_ready = halves("slots_ready")
        stq_ready = halves("stq_ready")
        snq_ready = halves("snq_ready")
        trq_ready = halves("trq_ready")
        tcq_ready = halves("tcq_ready")
        qk_ready = halves("qk_ready")
        qhi_ready = halves("qhi_ready")
        qlo_ready = halves("qlo_ready")
        slots0_ready = sem("slots0_ready")
        x1_done = sem("x1_done")
        xstat_ready = sem("xstat_ready")
        xrs_ready = sem("xrs_ready")
        ap_ready = sem("ap_ready")
        app_ready = sem("app_ready")
        z_ready = sem("z_ready")
        hi_ready = sem("hi_ready")
        epsc_ready = sem("epsc_ready")
        lo_ready = sem("lo_ready")
        fstat = sem("fstat")
        frs_ready = sem("frs_ready")
        xn_ready = sem("xn_ready")
        xt_ready = sem("xt_ready")
        xtc_ready = sem("xtc_ready")
        gate_ready = sem("gate_ready")
        gmax_ready = sem("gmax_ready")
        gexp_ready = sem("gexp_ready")
        hot_ready = sem("hot_ready")
        rank_ready = sem("rank_ready")
        pos_ready = sem("pos_ready")
        recx_ready = sem("recx_ready")
        recid_ready = sem("recid_ready")
        scattered = sem("scattered")
        we_in = [sem(f"we_in{i}") for i in range(2)]
        row_in = [sem(f"row_in{i}") for i in range(2)]
        b1e_ready = sem("b1e_ready")
        bt_ready = sem("bt_ready")
        btc_ready = sem("btc_ready")
        bh_ready = sem("bh_ready")
        bg_ready = sem("bg_ready")
        by_ready = sem("by_ready")
        yo_ready = sem("yo_ready")
        ys_ready = sem("ys_ready")
        out_done = [sem(f"out_done{i}") for i in range(2)]

        WEIGHTS_IN = 16 * (len(W) + 2)
        ROWS_IN = 16 * (len(COLS) + len(ROWS) + 2)

        def ctx_dram(b):
            rows = a["ctx_1024"][b]
            return rows[0:FULL * P, :].rearrange("(p t) d -> p t d", t=FULL), rows[FULL * P:S, :]

        def pre_pair(s):
            return 1 if s == 0 else 0

        def pre_base(i, s, per_pair):
            return i * (2 * per_pair) + (per_pair if s == 0 else 2 * per_pair)

        def pool_step(r):
            return r - r // 4

        def in_prologue(step, h):
            return when(step, h)[1] == 1 and step in Q_STEPS

        def credit(eng, sems, step):
            for h in range(2):
                eng.sem_inc(sems[h], CR - 1 if in_prologue(step, h) else CR)

        def made(i, s, source, step, h):
            return i * ROUNDS + (s + 1 + CR - (when(step, h)[1] - when(source, h)[1]))

        def latest(i, s, c, source, h):
            return i * ROUNDS + (s + CR + (1 if when(source, h)[0] < c else 0))

        def pair_of(s, step, h):
            return (s - when(step, h)[1]) % 2

        def finished(s, step, h):
            return (s - when(step, h)[1]) % ROUNDS >= ROUNDS - 2

        def now(c, step, h, final):
            if final and (when(step, h)[1] != 1 or step in Q_STEPS):
                return False
            return when(step, h)[0] == c

        def final_at(i, s):
            return i * 4 + (0 if s == 0 else 2)

        def cols_of(t0, n, rows):
            return slice(t0 * P, t0 * P + (n - 1) * P + rows)

        block = ctx.enter_context(nc.Block())

        @block.sync
        def _(sp):
            def load_stage(x, group):
                for b in range(2):
                    full, tail = ctx_dram(group * 4 + 2 * x + b)
                    sp.dma_start(stage[:, x, b, 0:FULL, :], full).then_inc(stage_in[x], 16)
                    sp.dma_start(stage[0:TAIL, x, b, FULL, :], tail).then_inc(stage_in[x], 16)

            load_stage(0, 0)
            sp.dma_start(x1[:, PAD:PAD + B, :], a["x"].rearrange("b (p j) d -> p b (j d)", j=2)).then_inc(x_in, 16)
            for n in W:
                sp.dma_start(W[n][:, :], a["L0_xcond_" + n]).then_inc(weights_in, 16)
            load_stage(1, 0)
            sp.dma_start(wg[:, :], a["L0_ffn_Wg"]).then_inc(weights_in, 16)
            sp.dma_start(b1r[:, :], a["L0_ffn_b1"].rearrange("e (j p) -> (e j) p", p=P)).then_inc(weights_in, 16)
            sp.wait_ge(fill_in, 1)
            n = NBLK * BLK // P
            for i in range(n):
                sp.dma_start(scratch[i * P:(i + 1) * P, :], fill[:, :]).then_inc(fill_in, 16)

            with sp.Fori(0, GROUPS) as i:
                nxt = (i * 4 + 4) % B
                for x in range(2):
                    sp.wait_ge(z_ready, i * (2 * PRE) + PRE * (x + 1))
                    for b in range(2):
                        full, tail = ctx_dram(nxt + (2 * x + b))
                        sp.dma_start(stage[:, x, b, 0:FULL, :], full).then_inc(stage_in[x], 16)
                        sp.dma_start(stage[0:TAIL, x, b, FULL, :], tail).then_inc(stage_in[x], 16)

            w1d = a["L0_ffn_W1"]
            w2d = a["L0_ffn_W2"].rearrange("e (j p) d -> e p j d", p=P)
            b2d = a["L0_ffn_b2"]
            rows = scratch.rearrange("(k p j) r -> k p j r", p=P, j=2)
            sp.wait_ge(pos_ready, 1)
            def feed(i, first):
                for k in range(2):
                    e = sp.value_load(bexpi[0:1, bass.ds(i * 2 + k, 1)], min_val=0, max_val=E - 1)
                    if not first:
                        sp.wait_ge(yo_ready, i * 2 + (k - 1))
                    sp.dma_start(w1e[:, k, :], w1d[e]).then_inc(we_in[k], 16)
                    sp.dma_start(w2e[:, k, :, :], w2d[e]).then_inc(we_in[k], 16)
                    sp.dma_start(b2e[:, k, :], b2d[e].partition_broadcast(P)).then_inc(we_in[k], 16)
                    if first:
                        sp.wait_ge(scattered, 16 * NT)
                    else:
                        sp.wait_ge(out_done[k], i * 32)
                    sp.dma_start(brow[:, k, :, :], rows[i * 2 + k]).then_inc(row_in[k], 16)

            feed(0, True)
            with sp.Fori(1, NBLK // 2) as i:
                feed(i, False)

        @block.gpsimd
        def _(pool):
            g = nc.gpsimd
            g.memset(ident[:, :], 0.0)
            g.memset(ltri[:, :], 0.0)
            pool.drain()
            g.affine_select(out=ident[:, :], in_=ident[:, :], compare_op=ALU.not_equal, fill=1.0, base=0,
                            pattern=[[-1, P]], channel_multiplier=1)
            g.affine_select(out=ltri[:, :], in_=ltri[:, :], compare_op=ALU.is_ge, fill=1.0, base=0,
                            pattern=[[-1, P]], channel_multiplier=1)
            g.memset(ones[:, :], 1.0)
            g.memset(negones[:, :], -1.0)
            g.memset(meanw[:, :], 1.0 / D)
            g.memset(epst[:, :], LN_EPS)
            g.memset(neghalf[:, :], -0.5)
            g.memset(half[:, :], 0.5).then_inc(consts, 1)
            g.memset(fill[:, :], 0.0)
            pool.drain()
            g.iota(fill[:, REC - 3:REC - 2].bitcast(U32), [[0, 1]], base=2 * B * K,
                   channel_multiplier=0).then_inc(fill_in, 1)
            g.iota(iota8[:, :], [[1, E]], base=0, channel_multiplier=0, allow_small_or_imprecise_dtypes=True)
            g.iota(iotaj[:, :], [[1, NBLK]], base=0, channel_multiplier=0, allow_small_or_imprecise_dtypes=True)
            g.memset(scanm[:, :], 1.0)
            pool.drain()
            g.memset(scanm[:, :].rearrange("p (e t) -> p e t", t=NT)[:, :, 0:1], 0.0).then_inc(consts, 1)
            with nc.allow_non_contiguous_dma(reason="bias columns: 128 elements each"):
                for n in COLS:
                    pool.dma_start(col[n], a["L0_xcond_" + n].rearrange("(p o) -> p o", o=1)).then_inc(rows_in, 16)
            for n in ROWS:
                src = a["L0_xcond_" + n]
                src = src[0, 0] if len(src.shape) == 3 else src
                pool.dma_start(row[n], src.partition_broadcast(P)).then_inc(rows_in, 16)
            pool.dma_start(bgr[:, :], a["L0_ffn_bg"].partition_broadcast(P)).then_inc(rows_in, 16)
            pool.dma_start(xb[:, PAD:PAD + B, :].rearrange("p b d -> p (b d)"),
                           a["cond_1024"].rearrange("b d -> (b d)").partition_broadcast(P)).then_inc(rows_in, 16)
            g.memset(xb[:, 0:PAD, :], 0.0)
            g.memset(prevb[:, 1, :, :], 0.0)
            pool.wait_ge(rows_in, ROWS_IN)
            g.tensor_tensor(xb[:, PAD:PAD + B, :], xb[:, PAD:PAD + B, :], mid_dim(row["b2"], B), ALU.add)

            def context_rstd(x, n0, n1, count):
                ns = slice(n0, n1)
                pool.wait_ge(xstat_ready, count)
                g.tensor_tensor(xve[:, ns], xmv[:, x, ns, 1], epst[:, ns], ALU.add)
                pool.drain()
                g.tensor_tensor(xrs[:, x, ns], xve[:, ns], neghalf[:, ns], ALU.pow)
                pool.drain()
                g.tensor_tensor(xsd[:, ns], xve[:, ns], xrs[:, x, ns], ALU.mult)
                pool.drain()
                m = xmv[:, x, n0:min(n1, 2 * TILES), 0]
                last = g.tensor_tensor(m, xsd[:, n0:min(n1, 2 * TILES)], m, ALU.subtract)
                if n1 == NS:
                    last.then_inc(xrs_ready, 1)
                pool.drain()

            def layer_rstd(k, h, sem_in, count, sem_out=None):
                t0, t1 = 2 * h, 2 * h + 2
                pool.wait_ge(sem_in, count)
                g.tensor_tensor(ve[:, k, t0:t1], mv[:, k, t0:t1, 1], epst[:, t0:t1], ALU.add)
                if sem_out is None:
                    g.tensor_tensor(mneg[:, k, t0:t1], mv[:, k, t0:t1, 0], negones[:, t0:t1], ALU.mult)
                pool.drain()
                last = g.tensor_tensor(rstd[:, k, t0:t1], ve[:, k, t0:t1], neghalf[:, t0:t1], ALU.pow)
                if sem_out is not None:
                    last.then_inc(sem_out, 1)

            def layer_norm(k, h, src, dst, sem_in, count, sem_out):
                layer_rstd(k, h, sem_in, count)
                pool.drain()
                for t in range(2 * h, 2 * h + 2):
                    last = g.tensor_scalar(dst[:, t, :], src[:, t, :], mneg[:, k, t:t + 1], rstd[:, k, t:t + 1],
                                           ALU.add, ALU.mult)
                last.then_inc(sem_out, 1)

            def scale_rows(i, n, behind=None):
                m = n % TRIP
                b, t0, nt, rows = tiles_of(m % SLOTS)
                x = (m // SLOTS) % 2
                k = n % NE
                pool.wait_ge(pv_done, i * TRIP + (n + 1 - NE + CREDIT if behind is None else behind))
                pool.wait_ge(inv_ready, i * TRIP + (n + 1))
                g.tensor_tensor(xs[0:rows, k, 0:nt, :], nat[0:rows, x, b, t0:t0 + nt, :],
                                last_dim(rinv[0:rows, k, 0:nt], D), ALU.mult).then_inc(xs_ready, 1)

            def pre_apply(x, r):
                b, t0, nt, rows = pre_tiles(r)
                for t in range(t0, t0 + 2):
                    n = b * TILES + t
                    last = g.tensor_scalar(nat[:, x, b, t, :], stage[:, x, b, t, :], xmv[:, x, n, 0:1],
                                           xrs[:, x, n:n + 1], ALU.add, ALU.mult)
                last.then_inc(app_ready, 1)

            def add_cond(i, s, h):
                at = i * 4 + (PAD + 2 * pair_of(s, "cond", h) - (4 if s < when("cond", h)[1] else 0))
                src = xb[:, bass.ds(at + h, 1), :].to_broadcast([P, 2, D])
                g.tensor_tensor(s1b[:, 2 * h:2 * h + 2, :], s1[:, 2 * h:2 * h + 2, :], src,
                                ALU.add).then_inc(s1b_ready[h], 1)

            def new_prev(i, s, h, final):
                x, last_round = pair_of(s, "prev", h), finished(s, "prev", h)
                src = slots0[:, x, :, :] if last_round else slots
                pool.wait_ge(slots_ready[h], made(i, s, "nrm", "prev", h))
                if not final:
                    g.tensor_tensor(prevb[:, x, 2 * h:2 * h + 2, :], src[:, 2 * h:2 * h + 2, :], mid_dim(bvu[:, :], 2),
                                    ALU.add)
                if last_round:
                    at = final_at(i, s)
                    dst = x1[:, bass.ds(at + h, 1), :]
                    g.tensor_tensor(dst, dst, slots[:, 2 * h:2 * h + 2, :].rearrange("p (o j) d -> p o (j d)", o=1),
                                    ALU.add).then_inc(x1_done, 1)

            def update_first(i, s, c, final=False):
                for h in (1, 0):
                    if now(c, "ap1", h, final):
                        layer_norm(0, h, s1, sn1, st1_ready[h], made(i, s, "s1", "ap1", h), sn1_ready[h])
                    if POOLQ and now(c, "apq", h, final):
                        norm_q(i, s, h)

            def norm_q(i, s, h):
                layer_norm(2, h, slots0[:, pair_of(s, "apq", h), :, :] if finished(s, "apq", h) else slots,
                           snq, stq_ready[h], made(i, s, "stq", "apq", h), snq_ready[h])

            def update(i, s, c, final=False):
                for h in (1, 0):
                    if now(c, "cond", h, final):
                        add_cond(i, s, h)
                    if now(c, "rsp", h, final):
                        layer_rstd(1, h, stp_ready[h], made(i, s, "z", "rsp", h), rsp_ready[h])
                    if not POOLQ and now(c, "apq", h, final):
                        norm_q(i, s, h)
                    if now(c, "prev", h, final):
                        new_prev(i, s, h, final)

            for sems, step in ((sn1_ready, "ap1"), (s1b_ready, "cond"), (rsp_ready, "rsp"), (snq_ready, "apq")):
                credit(pool, sems, step)
            context_rstd(0, 0, NS, 1)
            for r in range(PRE):
                if r % 4 < 3:
                    pre_apply(0, r)
            pool.wait_ge(prep, 3)
            for h in range(2):
                layer_norm(2, h, slots0[:, 0, :, :], snq, stq_ready[h], CR, snq_ready[h])
            pool.wait_ge(slots0_ready, 1)
            g.tensor_tensor(prevb[:, 0, :, :], slots0[:, 0, :, :], mid_dim(bvu[:, :], 4), ALU.add)
            for n in range(SCALE - 1):
                scale_rows(0, n)
            context_rstd(1, 0, NS, 2)
            scale_rows(0, SCALE - 1)
            with pool.Fori(0, GROUPS) as i:
                for s in range(ROUNDS):
                    for c in range(SLOTS):
                        n = s * SLOTS + c
                        pre = s in (0, 5)
                        update_first(i, s, c)
                        steps = [r for r in range(PRE) if pre and PRE_SLOT[r] == c and r % 4 < 3]
                        for r in steps:
                            if r:
                                pre_apply(pre_pair(s), r)
                        scale_rows(i, n + SCALE, n + CREDIT if pre and c == 0 else None)
                        if 0 in steps:
                            pre_apply(pre_pair(s), 0)
                        update(i, s, c)
                        if s in (2, 4) and 4 <= c < 10:
                            context_rstd(s // 2 - 1, 5 * (c - 4), 5 * (c - 4) + 5, i * 2 + (3 if s == 2 else 4))
            for c in range(SLOTS):
                update_first(GROUPS, 0, c, final=True)
                update(GROUPS, 0, c, final=True)

            pool.wait_ge(fstat, 1)
            g.tensor_tensor(fve[:, :], fmv[:, :, 1], epst[:, :], ALU.add)
            pool.drain()
            g.tensor_tensor(frs[:, :], fve[:, :], neghalf[:, :], ALU.pow).then_inc(frs_ready, 1)
            g.iota(rec[:, :, 2 * D + 1].bitcast(U32).rearrange("p (b j) -> p b j", j=2), [[K, B], [1, 2]], base=0,
                   channel_multiplier=2).then_inc(recid_ready, 1)
            g.memset(rec[:, :, 2 * D + 2:REC], 0.0).then_inc(recid_ready, 1)
            pool.wait_ge(fill_in, 1 + 16 * (NBLK * BLK // P))
            pool.wait_ge(pos_ready, 1)
            pool.wait_ge(recx_ready, 1)
            pool.wait_ge(recid_ready, 2)
            for t in range(NT):
                g.indirect_dma_start(scratch, bass.IndirectOffsetOnAxis(posi[:, t:t + 1], 0), rec[:, t, :],
                                     None).then_inc(scattered, 16)
            last_row = pool.to_reg(B * K - 1)

            def store(i, first):
                for k in range(2):
                    if not first:
                        pool.wait_ge(out_done[k], i * 32)
                    pool.wait_ge(yo_ready, i * 2 + (k + 1))
                    g.tensor_tensor(ys[:, k, :, :], yo[:, k, :, :], brow[:, k, :, D:2 * D], ALU.add).then_inc(ys_ready, 1)
                    pool.drain()
                    for j in range(2):
                        idx = brow[:, k, j, 2 * D + 1:2 * D + 2].bitcast(U32)
                        g.indirect_dma_start(out.rearrange("b k d -> (b k) d"), bass.IndirectOffsetOnAxis(idx, 0),
                                             ys[:, k, j, :], None, bounds_check=last_row,
                                             oob_is_err=False).then_inc(out_done[k], 16)

            store(0, True)
            with pool.Fori(1, NBLK // 2) as i:
                store(i, False)
            for k in range(2):
                pool.wait_ge(out_done[k], 32 * (NBLK // 2))

        @block.scalar
        def _(act):
            A = nc.scalar.activation

            def exp(i, n):
                _, _, nt, rows = tiles_of(n % SLOTS)
                k = n % NE
                act.wait_ge(pv_done, i * TRIP + (n + 1 - NE + CREDIT))
                act.wait_ge(min_ready, i * TRIP + (n + 1))
                for j in range(nt):
                    last = A(ex[0:rows, k, j, :], lg[n % NL][0:rows, j, :], ACT.Exp, bias=nmin[0:rows, k, j:j + 1],
                             scale=-1.0, accum_out=rsum[0:rows, k, j:j + 1])
                last.then_inc(exp_done, 1)

            def copy_u(h, x, products, i):
                act.wait_ge(pv_done, i * TRIP + (products + CREDIT))
                A(ut[:, h, :], pv[h][:, 0:K], ACT.Identity, bias=epsc[:, x, h:h + 1]).then_inc(ut_ready[h], 1)

            def copy_1(h, count):
                act.wait_ge(tr1_ready[h], count)
                A(snt[:, h * K:(h + 1) * K], px[:, K:2 * K], ACT.Copy).then_inc(tc1_ready[h], 1)

            def gelu(h, count):
                act.wait_ge(h_ready[h], count)
                A(gt[:, h * K:(h + 1) * K], px[:, 0:K], ACT.Gelu, bias=b1m).then_inc(g_ready[h], 1)

            def q_copy(h, count):
                act.wait_ge(trq_ready[h], count)
                A(snqt[:, h, :], px[:, K:2 * K], ACT.Copy).then_inc(tcq_ready[h], 1)

            def q_hi(h, x, count):
                act.wait_ge(qk_ready[h], count)
                A(qhi[:, x, h * K:(h + 1) * K], pv[h][:, K:2 * K], ACT.Identity, bias=bqk).then_inc(qhi_ready[h], 1)

            def update_first(i, s, c, final=False):
                for h in (1, 0):
                    if now(c, "ut", h, final):
                        copy_u(h, pair_of(s, "ut", h), (s + 1 - when("ut", h)[1]) * SLOTS - (0 if h else CH), i)

            def update(i, s, c, final=False):
                for h in (1, 0):
                    if now(c, "tc1", h, final):
                        copy_1(h, made(i, s, "tr1", "tc1", h))
                    if now(c, "gelu", h, final):
                        gelu(h, made(i, s, "hid", "gelu", h))
                    if now(c, "tcq", h, final):
                        q_copy(h, made(i, s, "trq", "tcq", h))
                    if now(c, "qhi", h, final):
                        q_hi(h, pair_of(s, "qhi", h), made(i, s, "qk", "qhi", h))

            def pre_hi(i, x, r, base):
                act.wait_ge(z_ready, base + r + 1)
                b, t0, nt, rows = pre_tiles(r)
                n = (nt - 1) * P + rows
                A(th[:, x, b, cols_of(t0, nt, rows)], pz[:, 0:n], ACT.Copy,
                  accum_out=cpart[:, x, b, r % 4:r % 4 + 1]).then_inc(hi_ready, 1)

            act.sem_inc(exp_done, CREDIT)
            for sems, step in ((ut_ready, "ut"), (tc1_ready, "tc1"), (g_ready, "gelu"),
                               (tcq_ready, "tcq"), (qhi_ready, "qhi")):
                credit(act, sems, step)
            act.wait_ge(rows_in, ROWS_IN)
            A(esig[:, :], row["q_logsig"], ACT.Exp).then_inc(prep, 1)
            for r in range(PRE):
                pre_hi(0, 0, r, 0)
            for h in range(2):
                if in_prologue("tcq", h):
                    q_copy(h, CR)
                if in_prologue("qhi", h):
                    q_hi(h, 0, CR)
            for n in range(AHEAD):
                exp(0, n)
            with act.Fori(0, GROUPS) as i:
                for s in range(ROUNDS):
                    for c in range(SLOTS):
                        update_first(i, s, c)
                        exp(i, s * SLOTS + c + AHEAD)
                        if s in (0, 5):
                            for r in range(PRE):
                                if PRE_SLOT[r] + TRANSPOSE == c:
                                    pre_hi(i, pre_pair(s), r, pre_base(i, s, PRE))
                        update(i, s, c)
            for c in range(SLOTS):
                update_first(GROUPS, 0, c, final=True)
                update(GROUPS, 0, c, final=True)

            act.wait_ge(frs_ready, 1)
            for t in range(0, NT, 8):
                last = A(rec[:, t:t + 8, D:2 * D],
                         x1[:, PAD + t // 2:PAD + t // 2 + 4, :].rearrange("p b (j d) -> p (b j) d", d=D), ACT.Copy)
            last.then_inc(recx_ready, 1)
            for r in range(NT // 4):
                act.wait_ge(xt_ready, r + 1)
                if r >= 2:
                    act.wait_ge(gate_ready, r - 1)
                A(xnt[:, r % 2, :], lg[r % 2][:, :, :].rearrange("p a b -> p (a b)"), ACT.Copy).then_inc(xtc_ready, 1)
            act.wait_ge(gmax_ready, 1)
            A(ga[1][:, :, :], ga[1][:, :, :], ACT.Exp).then_inc(gexp_ready, 1)
            with act.Fori(0, NBLK // 2) as i:
                for k in range(2):
                    act.wait_ge(bt_ready, i * 2 + (k + 1))
                    A(xte[:, k, :], px[:, 0:BLK], ACT.Copy).then_inc(btc_ready, 1)
                    act.wait_ge(b1e_ready, i * 2 + (k + 1))
                    for j in range(HT):
                        act.wait_ge(bh_ready, i * (2 * HT) + (k * HT + j + 1))
                        A(ht[:, k, j, :], hbank[j], ACT.Silu,
                          bias=b1e[:, k, j:j + 1]).then_inc(bg_ready, 1)

        @block.vector
        def _(dve):
            v = nc.vector

            def layer_stats(k, t0, t1, tiles, sem_out):
                for j in range(t0, t1):
                    v.bn_stats(bst[:, k, j, :], tiles[:, j, :])
                dve.drain()
                for j in range(t0, t1):
                    last = v.bn_aggr(mv[:, k, j, :], bst[:, k, j, :])
                last.then_inc(sem_out, 1)

            def row_min(i, n):
                _, _, nt, rows = tiles_of(n % SLOTS)
                dve.wait_ge(lg_ready, i * TRIP + (n + 1))
                v.tensor_reduce(nmin[0:rows, n % NE, 0:nt], lg[n % NL][0:rows, 0:nt, :], AX.X,
                                ALU.min).then_inc(min_ready, 1)

            def row_inv(i, n):
                _, _, nt, rows = tiles_of(n % SLOTS)
                dve.wait_ge(exp_done, i * TRIP + (n + 1 + CREDIT))
                v.reciprocal(rinv[0:rows, n % NE, 0:nt], rsum[0:rows, n % NE, 0:nt]).then_inc(inv_ready, 1)

            def slots_from_x(i, x, at, h):
                for j in range(2):
                    t = 2 * h + j
                    xt = x1[:, bass.ds(at + h, 1), j * D:(j + 1) * D].rearrange("p a d -> p (a d)")
                    n = 2 * TILES + t
                    v.scalar_tensor_tensor(zg[:, t, :], xt, xmv[:, x, n, 0:1], esig[:, :], ALU.subtract, ALU.mult)
                dve.drain()
                for t in range(2 * h, 2 * h + 2):
                    n = 2 * TILES + t
                    last = v.scalar_tensor_tensor(slots0[:, x, t, :], zg[:, t, :], xrs[:, x, n:n + 1], row["q_mu"],
                                                  ALU.mult, ALU.add)
                return last

            def context_stats(i, x, n0, n1):
                for n in range(n0, n1):
                    b, t = n // TILES, n % TILES
                    rows = P if t < FULL else TAIL
                    v.bn_stats(xbst[0:rows, n, :], stage[0:rows, x, b, t, :])

            def x_stats(i, at):
                for j in range(4):
                    v.bn_stats(xbst[:, 2 * TILES + j, :],
                               x1[:, bass.ds(at + j // 2, 1), (j % 2) * D:(j % 2 + 1) * D].rearrange("p a d -> p (a d)"))

            def context_aggr(x, n0, n1):
                for n in range(n0, n1):
                    rows = TAIL if n < 2 * TILES and n % TILES == FULL else P
                    last = v.bn_aggr(xmv[0:rows, x, n, :], xbst[0:rows, n, :])
                return last

            def pre_apply(x, r, first=False):
                b, t0, nt, rows = pre_tiles(r)
                for t in range(t0 + (2 if nt == 4 else 0), t0 + nt):
                    n = b * TILES + t
                    last = v.tensor_scalar(nat[0:rows, x, b, t, :], stage[0:rows, x, b, t, :],
                                           xmv[0:rows, x, n, 0:1], xrs[0:rows, x, n:n + 1],
                                           ALU.add, ALU.mult)
                last.then_inc(ap_ready, 1)

            def pre_lo(x, r, base):
                dve.wait_ge(hi_ready, base + r + 1)
                b, t0, nt, rows = pre_tiles(r)
                n = (nt - 1) * P + rows
                cs = cols_of(t0, nt, rows)
                v.tensor_tensor(tl[:, x, b, cs], pz[:, 0:n], th[:, x, b, cs].bitcast(F32),
                                ALU.subtract).then_inc(lo_ready, 1)
                if r % 4 == 3:
                    v.tensor_reduce(epsc[:, x, b:b + 1], cpart[:, x, b, :], AX.X, ALU.add)
                    dve.drain()
                    v.tensor_scalar(epsc[:, x, b:b + 1], epsc[:, x, b:b + 1], ATTN_EPS, None,
                                    ALU.mult).then_inc(epsc_ready, 1)

            def q_lo(h, x, count):
                dve.wait_ge(qhi_ready[h], count)
                v.scalar_tensor_tensor(qlo[:, x, h * K:(h + 1) * K], pv[h][:, K:2 * K], bqk,
                                       qhi[:, x, h * K:(h + 1) * K].bitcast(F32), ALU.add,
                                       ALU.subtract).then_inc(qlo_ready[h], 1)

            def slots_1(h, x, count):
                dve.wait_ge(upd_ready[h], count)
                v.reciprocal(rsig[:, 2 * h:2 * h + 2], px[:, K:K + 2])
                dve.drain()
                for j in range(2):
                    t = 2 * h + j
                    v.scalar_tensor_tensor(s1[:, t, :], px[:, j * D:(j + 1) * D], rsig[:, t:t + 1],
                                           prevb[:, x, t, :], ALU.mult, ALU.add)
                dve.drain()
                layer_stats(0, 2 * h, 2 * h + 2, s1, st1_ready[h])

            def slots_2(i, s, h):
                dve.wait_ge(s1b_ready[h], made(i, s, "cond", "z", h))
                dve.wait_ge(o_ready[h], made(i, s, "mm2", "z", h))
                v.tensor_tensor(zt[:, 2 * h:2 * h + 2, :], py[:, 0:K].rearrange("p (j d) -> p j d", j=2),
                                s1b[:, 2 * h:2 * h + 2, :], ALU.add)
                dve.drain()
                layer_stats(1, 2 * h, 2 * h + 2, zt, stp_ready[h])

            def new_slots(h, count):
                dve.wait_ge(rsp_ready[h], count)
                for t in range(2 * h, 2 * h + 2):
                    v.scalar_tensor_tensor(zg[:, t, :], zt[:, t, :], mv[:, 1, t, 0:1], row["lnp_g"],
                                           ALU.subtract, ALU.mult)
                dve.drain()
                for t in range(2 * h, 2 * h + 2):
                    last = v.scalar_tensor_tensor(slots[:, t, :], zg[:, t, :], rstd[:, 1, t:t + 1],
                                                  row["lnp_b"], ALU.mult, ALU.add)
                last.then_inc(slots_ready[h], 1)
                dve.drain()

            def update_first(i, s, c):
                for h in (1, 0):
                    if now(c, "qlo", h, False):
                        q_lo(h, pair_of(s, "qlo", h), made(i, s, "qhi", "qlo", h))

            def update(i, s, c, final=False):
                for h in (1, 0):
                    if now(c, "s1", h, final):
                        slots_1(h, pair_of(s, "s1", h), made(i, s, "upd", "s1", h))
                    if now(c, "z", h, final):
                        slots_2(i, s, h)
                    if now(c, "nrm", h, final):
                        new_slots(h, made(i, s, "rsp", "nrm", h))
                    if now(c, "stq", h, final):
                        layer_stats(2, 2 * h, 2 * h + 2,
                                    slots0[:, pair_of(s, "stq", h), :, :] if finished(s, "stq", h) else slots,
                                    stq_ready[h])

            for sems, step in ((st1_ready, "s1"), (stp_ready, "z"), (slots_ready, "nrm"),
                               (stq_ready, "stq"), (qlo_ready, "qlo")):
                credit(dve, sems, step)
            v.memset(x1[:, 0:PAD, :], 0.0)
            v.memset(upd[:, :], 0.0)
            v.memset(epsc[:, :, :], 0.0)
            v.memset(xmv[:, :, :, :], 0.0)
            v.memset(xbst[:, :, :], 0.0)
            v.memset(pv[1][:, :], 1.0).then_inc(prep, 1)
            dve.drain()
            dve.wait_ge(stage_in[0], 64)
            context_stats(0, 0, 0, 2 * TILES)
            dve.wait_ge(x_in, 16)
            x_stats(0, PAD)
            dve.drain()
            context_aggr(0, 0, NS).then_inc(xstat_ready, 1)
            dve.wait_ge(weights_in, WEIGHTS_IN)
            dve.wait_ge(rows_in, ROWS_IN)
            v.tensor_scalar(wtmp[:, 0, :], W["wk"][:, :], col["lnkv_g"], None, ALU.mult)
            v.tensor_scalar(wtmp[:, 1, :], W["wq"][:, :], col["lnq_g"], None, ALU.mult)
            v.tensor_scalar(wtmp[:, 2, :], W["wv"][:, :], col["lnkv_g"], None, ALU.mult)
            v.tensor_scalar(w1g[:, :], W["w1"][:, :], col["lnm_g"], None, ALU.mult).then_inc(consts, 1)
            dve.wait_ge(wstep, 1)
            pc = px[:, 0:8]
            v.tensor_tensor(ctmp[:, 2:3], pc[:, 0:1], col["bk"], ALU.add)
            v.tensor_tensor(ctmp[:, 3:4], pc[:, 1:2], col["bq"], ALU.add)
            v.tensor_tensor(ctmp[:, 4:5], pc[:, 2:3], col["bv"], ALU.add)
            v.tensor_tensor(b1m, pc[:, 3:4], col["b1"], ALU.add)
            dve.drain()
            v.tensor_tensor(ctmp[:, 5:6], ctmp[:, 2:3], pc[:, 4:5], ALU.subtract)
            dve.drain()
            v.tensor_scalar(ctmp[:, 6:7], ctmp[:, 5:6], 1.0 / D, None, ALU.mult)
            dve.drain()
            v.tensor_scalar(wtmp[:, 3, :], py[:, 0:D], ctmp[:, 6:7], None, ALU.add)
            v.tensor_copy(wtmp[:, 4, :], py[:, D:2 * D])
            v.tensor_copy(wtmp[:, 5, :], py[:, 2 * D:3 * D])
            v.tensor_scalar(v1b[:, :], ones[:, :], ctmp[:, 4:5], None, ALU.mult).then_inc(consts, 1)
            dve.wait_ge(wstep, 2)
            v.tensor_scalar(wqk[:, :], pz[:, 0:D], -float(D) ** 0.5, None, ALU.mult)
            v.tensor_scalar(bqk, pz[:, 2 * D:2 * D + 1], -float(D) ** 0.5, None, ALU.mult)
            v.tensor_copy(wvu[:, :], pz[:, D:2 * D]).then_inc(consts, 1)
            dve.wait_ge(wstep, 3)
            v.tensor_tensor(bvu[:, :], px[:, 0:D], row["bu"], ALU.add)
            v.tensor_copy(b1c[:, :], py[:, 0:E * HT]).then_inc(prep, 1)
            dve.wait_ge(prep, 3)
            dve.wait_ge(xrs_ready, 1)
            for r in range(PRE):
                pre_apply(0, r)
                if r:
                    pre_lo(0, r - 1, 0)
                if r == 1:
                    for h in range(2):
                        last = slots_from_x(0, 0, PAD, h)
                    last.then_inc(slots0_ready, 1)
                    dve.drain()
                    for h in range(2):
                        layer_stats(2, 2 * h, 2 * h + 2, slots0[:, 0, :, :], stq_ready[h])
            pre_lo(0, PRE - 1, 0)
            for h in range(2):
                if in_prologue("qlo", h):
                    q_lo(h, 0, CR)
            for n in range(AHEAD):
                row_min(0, n)
            for n in range(SCALE - 1):
                row_inv(0, n)
            dve.wait_ge(stage_in[1], 64)
            context_stats(0, 1, 0, 2 * TILES)
            x_stats(0, PAD + 2)
            dve.drain()
            context_aggr(1, 0, NS).then_inc(xstat_ready, 1)
            row_inv(0, SCALE - 1)
            dve.wait_ge(xrs_ready, 2)
            for h in range(2):
                slots_from_x(0, 1, PAD + 2, h)
            dve.drain()

            with dve.Fori(0, GROUPS) as i:
                for s in range(ROUNDS):
                    for c in range(SLOTS):
                        n = s * SLOTS + c
                        update_first(i, s, c)
                        row_min(i, n + AHEAD)
                        row_inv(i, n + SCALE)
                        if s in (0, 5):
                            for r in range(PRE):
                                if PRE_SLOT[r] + LOWER == c:
                                    pre_lo(pre_pair(s), r, pre_base(i, s, PRE))
                        update(i, s, c)
                        if s in (0, 5):
                            for r in range(PRE):
                                if PRE_SLOT[r] == c:
                                    if r == 0:
                                        dve.wait_ge(xrs_ready, i * 2 + (2 if s == 0 else 3))
                                        dve.wait_ge(pv_done, i * TRIP + (s * SLOTS + CREDIT))
                                    pre_apply(pre_pair(s), r)
                        if s in (1, 3):
                            x = s // 2
                            if c == 0:
                                dve.wait_ge(stage_in[x], i * 64 + 128)
                            if c < TILES:
                                context_stats(i, x, 2 * c, 2 * c + 2)
                            else:
                                x_stats(i, (i * 4 + 4) % B + (PAD + 2 * x))
                                dve.drain()
                        if s in (2, 4):
                            x = s // 2 - 1
                            if c < 4:
                                last = context_aggr(x, 8 * c, min(8 * c + 8, NS))
                                if c == 3:
                                    last.then_inc(xstat_ready, 1)
                            for h in range(2):
                                if c == 11 + h:
                                    if h == 0:
                                        dve.wait_ge(xrs_ready, i * 2 + (3 if s == 2 else 4))
                                    slots_from_x(i, x, (i * 4 + 4) % B + (PAD + 2 * x), h)
                                    if h == 1:
                                        dve.drain()
            for c in range(SLOTS):
                update(GROUPS, 0, c, final=True)
            dve.wait_ge(x1_done, 4 * GROUPS + 2)

            def x1t(t):
                return x1[:, PAD + t // 2, (t % 2) * D:(t % 2 + 1) * D]

            for t in range(NT):
                v.bn_stats(fbst[:, t, :], x1t(t))
            dve.drain()
            for t in range(NT):
                last = v.bn_aggr(fmv[:, t, :], fbst[:, t, :])
            last.then_inc(fstat, 1)
            dve.wait_ge(frs_ready, 1)
            for t in range(NT):
                last = v.tensor_scalar(rec[:, t, 0:D], x1t(t), fmv[:, t, 0:1], frs[:, t:t + 1],
                                       ALU.subtract, ALU.mult)
                if t % 4 == 3:
                    last.then_inc(xn_ready, 1)
            dve.wait_ge(gate_ready, NT // 4)
            v.tensor_tensor(ga[0][:, :, :], pv[0][:, 0:NT * E].rearrange("p (t e) -> p e t", e=E),
                            last_dim(bgr[:, :], NT), ALU.add)
            dve.drain()
            v.tensor_reduce(gr[:, 0, :], ga[0][:, :, :].rearrange("p e t -> p t e"), AX.X, ALU.max)
            dve.drain()
            v.tensor_tensor(ga[1][:, :, :], ga[0][:, :, :], mid_dim(gr[:, 0, :], E), ALU.subtract).then_inc(gmax_ready, 1)
            v.tensor_tensor(ga[2][:, :, :], ga[0][:, :, :], mid_dim(gr[:, 0, :], E), ALU.is_equal)
            dve.drain()
            v.scalar_tensor_tensor(ga[3][:, :, :], ga[2][:, :, :], -64.0, last_dim(iota8[:, :], NT), ALU.mult, ALU.add)
            dve.drain()
            v.tensor_reduce(gr[:, 1, :], ga[3][:, :, :].rearrange("p e t -> p t e"), AX.X, ALU.min)
            dve.drain()
            v.tensor_tensor(ga[2][:, :, :], ga[3][:, :, :], mid_dim(gr[:, 1, :], E), ALU.is_equal).then_inc(hot_ready, 1)
            dve.wait_ge(gexp_ready, 1)
            v.tensor_reduce(gr[:, 2, :], ga[1][:, :, :].rearrange("p e t -> p t e"), AX.X, ALU.add)
            dve.drain()
            v.reciprocal(rec[:, :, 2 * D], gr[:, 2, :])
            dve.wait_ge(rank_ready, 1)
            prefix = pv[1][:, 0:E * NT].rearrange("p (e t) -> p e t", e=E)
            totals = pv[1][:, E * NT:2 * E * NT].rearrange("p (e t) -> p e t", e=E)
            v.tensor_tensor_scan(ga[3][:, :, :].rearrange("p e t -> p (e t)"), scanm[:, :],
                                 pv[1][:, E * NT:2 * E * NT], 0.0, ALU.mult, ALU.add)
            dve.drain()
            v.tensor_tensor(ga[0][:, :, :], ga[3][:, :, :], totals, ALU.subtract)
            v.tensor_scalar(cnt[:, 0, :], ga[3][:, :, NT - 1], 1.0 / BLK, None, ALU.mult)
            dve.drain()
            v.tensor_tensor(cmpb[:, :, :], mid_dim(cnt[:, 0, :], NBLK), last_dim(iotaj[:, :], E), ALU.is_gt)
            v.tensor_tensor(ga[0][:, :, :], ga[0][:, :, :], prefix, ALU.add)
            dve.drain()
            v.tensor_reduce(cnt[:, 1, :], cmpb[:, :, :].rearrange("p j e -> p e j"), AX.X, ALU.add)
            dve.drain()
            src = 1
            for step, dst in ((1, 2), (2, 3), (4, 4)):
                v.tensor_copy(cnt[:, dst, 0:step], cnt[:, src, 0:step])
                v.tensor_tensor(cnt[:, dst, step:E], cnt[:, src, step:E], cnt[:, src, 0:E - step], ALU.add)
                dve.drain()
                src = dst
            v.tensor_tensor(cnt[:, 5, :], cnt[:, 4, :], cnt[:, 1, :], ALU.subtract)
            v.tensor_tensor(cmpb[:, :, :], last_dim(iotaj[:, :], E), mid_dim(cnt[:, 4, :], NBLK), ALU.is_ge)
            dve.drain()
            v.scalar_tensor_tensor(ga[1][:, :, :], last_dim(cnt[:, 5, :], NT), float(BLK), ga[0][:, :, :],
                                   ALU.mult, ALU.add)
            v.tensor_reduce(bexp[:, :], cmpb[:, :, :], AX.X, ALU.add)
            dve.drain()
            v.tensor_tensor(ga[3][:, :, :], ga[1][:, :, :], ga[2][:, :, :], ALU.mult)
            v.tensor_scalar(bexpi[:, :], bexp[:, :], float(E - 1), None, ALU.min)
            dve.drain()
            v.tensor_reduce(gr[:, 0, :], ga[3][:, :, :].rearrange("p e t -> p t e"), AX.X, ALU.add)
            dve.drain()
            v.tensor_copy(posi[:, :], gr[:, 0, :]).then_inc(pos_ready, 1)
            dve.drain()

            def finish(i, first):
                for k in range(2):
                    e = dve.value_load(bexpi[0:1, bass.ds(i * 2 + k, 1)], min_val=0, max_val=E - 1)
                    v.tensor_copy(b1e[:, k, :], b1c[:, bass.ds(e * HT, HT)]).then_inc(b1e_ready, 1)
                    dve.wait_ge(we_in[k], i * 48 + 48)
                    dve.wait_ge(row_in[k], i * 16 + 16)
                    if not first:
                        dve.wait_ge(ys_ready, i * 2 + (k - 1))
                    dve.wait_ge(by_ready, i * 2 + (k + 1))
                    v.tensor_tensor(yo[:, k, :, :], pz[:, 0:2 * D].rearrange("p (j d) -> p j d", j=2),
                                    mid_dim(b2e[:, k, :], 2), ALU.add)
                    dve.drain()
                    for j in range(2):
                        last = v.tensor_scalar(yo[:, k, j, :], yo[:, k, j, :], brow[:, k, j, 2 * D:2 * D + 1], None,
                                               ALU.mult)
                    last.then_inc(yo_ready, 1)

            finish(0, True)
            with dve.Fori(1, NBLK // 2) as i:
                finish(i, False)

        @block.tensor
        def _(pe):
            mm = nc.tensor.matmul

            def logits(i, n):
                m = n % TRIP
                x, c = (m // SLOTS) % 2, m % SLOTS
                b, t0, nt, rows = tiles_of(c)
                pe.wait_ge(exp_done, i * TRIP + (n + 1 - NL + CREDIT))
                for j in range(nt):
                    cs = slice((t0 + j) * P, (t0 + j) * P + rows)
                    qs = slice(b * K, (b + 1) * K)
                    o = lg[n % NL][0:rows, j, :]
                    mm(o, th[:, x, b, cs], qhi[:, x, qs], start=True, stop=False)
                    mm(o, tl[:, x, b, cs], qhi[:, x, qs], start=False, stop=False)
                    last = mm(o, th[:, x, b, cs], qlo[:, x, qs], start=False, stop=True)
                last.then_inc(lg_ready, 1)

            def product(i, n):
                b, t0, nt, rows = tiles_of(n % SLOTS)
                k = n % NE
                if t0 == 0:
                    pe.wait_ge(ut_ready[b], latest(i, n // SLOTS, n % SLOTS, "ut", b))
                    pe.wait_ge(qlo_ready[b], latest(i, n // SLOTS, n % SLOTS, "qlo", b))
                pe.wait_ge(xs_ready, i * TRIP + (n + 1))
                for j in range(nt):
                    last = mm(pv[b][:, 0:K], xs[0:rows, k, j, :], ex[0:rows, k, j, :],
                              start=(t0 + j == 0), stop=(t0 + j == FULL))
                last.then_inc(pv_done, 1)

            def project_u(h, count):
                pe.wait_ge(ut_ready[h], count)
                for j in range(2):
                    mm(px[:, K + j:K + j + 1], ut[:, h, j * P:(j + 1) * P], meanw[:, :], start=True, stop=True)
                for j in range(2):
                    last = mm(px[:, j * D:(j + 1) * D], ut[:, h, j * P:(j + 1) * P], wvu[:, :], start=True, stop=True)
                last.then_inc(upd_ready[h], 1)

            def transpose_1(h, count):
                pe.wait_ge(sn1_ready[h], count)
                for j in range(2):
                    last = nc.tensor.transpose(px[:, K + j * P:K + (j + 1) * P], sn1[:, 2 * h + j, :], ident[:, :])
                last.then_inc(tr1_ready[h], 1)

            def q_transpose(h, count):
                pe.wait_ge(snq_ready[h], count)
                for j in range(2):
                    last = nc.tensor.transpose(px[:, K + j * P:K + (j + 1) * P], snq[:, 2 * h + j, :], ident[:, :])
                last.then_inc(trq_ready[h], 1)

            def q_product(h, count):
                pe.wait_ge(tcq_ready[h], count)
                mm(pv[h][:, K:2 * K], wqk[:, :], snqt[:, h, :], start=True, stop=True).then_inc(qk_ready[h], 1)

            def update(i, s, c, final=False):
                for h in (1, 0):
                    if now(c, "upd", h, final):
                        pe.wait_ge(g_ready[1 - h], latest(i, s, c, "gelu", 1 - h))
                        pe.wait_ge(tcq_ready[h], latest(i, s, c, "tcq", h))
                        project_u(h, made(i, s, "ut", "upd", h))
                    if now(c, "tr1", h, final):
                        transpose_1(h, made(i, s, "ap1", "tr1", h))
                    if now(c, "hid", h, final):
                        pe.wait_ge(tc1_ready[h], made(i, s, "tc1", "hid", h))
                        mm(px[:, 0:K], w1g[:, :], snt[:, h * K:(h + 1) * K], start=True,
                           stop=True).then_inc(h_ready[h], 1)
                    if now(c, "mm2", h, final):
                        pe.wait_ge(g_ready[h], made(i, s, "gelu", "mm2", h))
                        for j in range(2):
                            t = 2 * h + j
                            last = mm(py[:, j * D:(j + 1) * D], gt[:, t * P:(t + 1) * P], W["w2"][:, :],
                                      start=True, stop=True)
                        last.then_inc(o_ready[h], 1)
                    if now(c, "trq", h, final):
                        pe.wait_ge(g_ready[1 - h], latest(i, s, c, "gelu", 1 - h))
                        q_transpose(h, made(i, s, "apq", "trq", h))
                    if now(c, "qk", h, final):
                        pe.wait_ge(ut_ready[h], latest(i, s, c, "ut", h))
                        q_product(h, made(i, s, "tcq", "qk", h))

            for sems, step in ((upd_ready, "upd"), (tr1_ready, "tr1"), (h_ready, "hid"), (o_ready, "mm2"),
                               (trq_ready, "trq"), (qk_ready, "qk")):
                credit(pe, sems, step)

            def pre_transpose(x, r, base, pbase):
                if r or not isinstance(base, int):
                    pe.wait_ge(lo_ready, base + r)
                pe.wait_ge(ap_ready, base + r + 1)
                b, t0, nt, rows = pre_tiles(r)
                if nt == 4:
                    pe.wait_ge(app_ready, pbase + (pool_step(r) + 1))
                for t in range(t0, t0 + nt):
                    at = (t - t0) * P
                    last = nc.tensor.transpose(pz[:, at:at + rows], nat[0:rows, x, b, t, :], ident[0:rows, 0:rows])
                last.then_inc(z_ready, 1)

            pe.sem_inc(pv_done, CREDIT)
            pe.wait_ge(consts, 3)
            pe.wait_ge(weights_in, WEIGHTS_IN)
            pe.wait_ge(rows_in, ROWS_IN)
            mm(px[:, 0:1], W["wk"][:, :], col["lnkv_b"], start=True, stop=True)
            mm(px[:, 1:2], W["wq"][:, :], col["lnq_b"], start=True, stop=True)
            mm(px[:, 2:3], W["wv"][:, :], col["lnkv_b"], start=True, stop=True)
            mm(px[:, 3:4], W["w1"][:, :], col["lnm_b"], start=True, stop=True)
            mm(px[:, 4:5], wtmp[:, 0, :], ones[:, 0:1], start=True, stop=True)
            for j in range(3):
                last = nc.tensor.transpose(py[:, j * D:(j + 1) * D], wtmp[:, j, :], ident[:, :])
            last.then_inc(wstep, 1)
            pe.wait_ge(consts, 4)
            mm(pz[:, 0:D], wtmp[:, 4, :], wtmp[:, 3, :], start=True, stop=True)
            mm(pz[:, D:2 * D], wtmp[:, 5, :], W["wu"][:, :], start=True, stop=True)
            mm(pz[:, 2 * D:2 * D + 1], wtmp[:, 3, :], ctmp[:, 3:4], start=True, stop=True).then_inc(wstep, 1)
            pe.wait_ge(consts, 5)
            mm(px[:, 0:D], v1b[:, :], W["wu"][:, :], start=True, stop=False)
            mm(px[:, 0:D], negones[:, :], wvu[:, :], start=False, stop=True)
            nc.tensor.transpose(py[:, 0:E * HT], b1r[:, :], ident[0:E * HT, 0:E * HT]).then_inc(wstep, 1)
            for r in range(PRE):
                pre_transpose(0, r, 0, 0)
            for h in range(2):
                if in_prologue("trq", h):
                    if h:
                        pe.wait_ge(tcq_ready[0], CR)
                    q_transpose(h, CR)
                if in_prologue("qk", h):
                    q_product(h, CR)
            pe.wait_ge(lo_ready, PRE)
            pe.wait_ge(qlo_ready[0], CR)
            for n in range(AHEAD):
                logits(0, n)

            with pe.Fori(0, GROUPS) as i:
                for s in range(ROUNDS):
                    for c in range(SLOTS):
                        n = s * SLOTS + c
                        ahead = (c + AHEAD) % SLOTS
                        if ORDER == 0:
                            product(i, n)
                        if ahead == 0:
                            if s in (0, 5):
                                pe.wait_ge(lo_ready, pre_base(i, s, PRE) + PRE // 2)
                            pe.wait_ge(qlo_ready[0], latest(i, s, SLOTS, "qlo", 0))
                        if ahead == CH:
                            if s == 0:
                                pe.wait_ge(lo_ready, i * (2 * PRE) + PRE)
                            if s == 1:
                                pe.wait_ge(lo_ready, i * (2 * PRE) + 2 * PRE)
                            pe.wait_ge(qlo_ready[1], latest(i, s, SLOTS, "qlo", 1))
                        logits(i, n + AHEAD)
                        if ORDER == 2:
                            update(i, s, c)
                        if ORDER:
                            product(i, n)
                        if s in (0, 5):
                            for r in range(PRE):
                                if PRE_SLOT[r] + TRANSPOSE == c:
                                    pre_transpose(pre_pair(s), r, pre_base(i, s, PRE), pre_base(i, s, PPRE))
                        if ORDER < 2:
                            update(i, s, c)
            for c in range(SLOTS):
                update(GROUPS, 0, c, final=True)

            pe.wait_ge(exp_done, GROUPS * TRIP + AHEAD + CREDIT)
            for r in range(NT // 4):
                pe.wait_ge(xn_ready, r + 1)
                if r >= 2:
                    pe.wait_ge(xtc_ready, r - 1)
                for j in range(4):
                    last = nc.tensor.transpose(lg[r % 2][:, j // 2, (j % 2) * P:(j % 2 + 1) * P],
                                               rec[:, 4 * r + j, 0:D], ident[:, :])
                last.then_inc(xt_ready, 1)
                pe.wait_ge(xtc_ready, r + 1)
                for j in range(4):
                    t = 4 * r + j
                    last = mm(pv[0][:, t * E:(t + 1) * E], xnt[:, r % 2, j * P:(j + 1) * P], wg[:, :],
                              start=True, stop=True)
                last.then_inc(gate_ready, 1)
            pe.wait_ge(hot_ready, 1)
            hot = ga[2][:, :, :].rearrange("p e t -> p (e t)")
            mm(pv[1][:, 0:E * NT], ltri[:, :], hot, start=True, stop=True)
            mm(pv[1][:, E * NT:2 * E * NT], ones[:, :], hot, start=True, stop=True).then_inc(rank_ready, 1)

            def expert(i, first):
                for k in range(2):
                    pe.wait_ge(row_in[k], i * 16 + 16)
                    for j in range(2):
                        last = nc.tensor.transpose(px[:, j * P:(j + 1) * P], brow[:, k, j, 0:D], ident[:, :])
                    last.then_inc(bt_ready, 1)
                    pe.wait_ge(we_in[k], i * 48 + 48)
                    pe.wait_ge(btc_ready, i * 2 + (k + 1))
                    for j in range(HT):
                        mm(hbank[j], w1e[:, k, j * P:(j + 1) * P], xte[:, k, :],
                           start=True, stop=True).then_inc(bh_ready, 1)
                    if k or not first:
                        pe.wait_ge(yo_ready, i * 2 + k)
                    for r in range(2):
                        for j in range(HT):
                            if r == 0:
                                pe.wait_ge(bg_ready, i * (2 * HT) + (k * HT + j + 1))
                            last = mm(pz[:, r * D:(r + 1) * D], ht[:, k, j, r * P:(r + 1) * P], w2e[:, k, j, :],
                                      start=(j == 0), stop=(j == HT - 1))
                    last.then_inc(by_ready, 1)

            expert(0, True)
            with pe.Fori(1, NBLK // 2) as i:
                expert(i, False)


_INS = ['x', 'cond_1024', 'ctx_1024'] + ['L0_xcond_' + n for n in (
    'q_mu', 'q_logsig', 'lnkv_g', 'lnkv_b', 'lnq_g', 'lnq_b', 'lnm_g', 'lnm_b', 'lnp_g', 'lnp_b', 'wk', 'bk',
    'wv', 'bv', 'wq', 'bq', 'wu', 'bu', 'w1', 'b1', 'w2', 'b2')] + ['L0_ffn_' + n for n in (
        'Wg', 'bg', 'W1', 'b1', 'W2', 'b2')]


def kernel(**inputs):
    import numpy as _np
    import concourse.bacc as _bacc
    from concourse import mybir as _mybir
    from concourse.bass_utils import run_bass_kernel_spmd as _run

    nc = _bacc.Bacc("TRN2", target_bir_lowering=False, num_devices=1)
    arrays, aps = {}, {}
    for name in _INS:
        arr = _np.ascontiguousarray(inputs[name])
        arrays[f"in_{name}"] = arr
        aps[name] = nc.dram_tensor(f"in_{name}", arr.shape, _mybir.dt.from_np(arr.dtype), kind="ExternalInput").ap()
    out = nc.dram_tensor("out", (B, K, D), F32, kind="ExternalOutput").ap()
    build(nc, aps, out)
    r = _run(nc, [arrays], core_ids=[0])
    return r.results[0]["out"]
```

```python
import concourse.bass as bass
from concourse import mybir
from contextlib import ExitStack

F32 = mybir.dt.float32
F32R = mybir.dt.float32r
U32 = mybir.dt.uint32
I32 = mybir.dt.int32
ALU = mybir.AluOpType
ACT = mybir.ActivationFunctionType
AX = mybir.AxisListType

B, K, D, S = 16, 256, 128, 1601
P = 128
LN_EPS, ATTN_EPS = 1e-5, 1e-8
GROUPS = B // 4
FULL = S // P
TAIL = S - FULL * P
TILES = FULL + 1
CH = 7
SLOTS = 2 * CH
ROUNDS = 6
TRIP = ROUNDS * SLOTS
NL = 3
NE = 4
CR = 2
CREDIT = 4
AHEAD = 3
SCALE = 2
PAD = 2
PRE = 8
PRE_SLOT = [0, 1, 2, 4, 6, 8, 9, 10]
TRANSPOSE = 2
LOWER = 3
PIECES = 10
PPRE = 6
E, H = 8, 512
HT = H // P
BLK = 256
NBLK = B * K // BLK + E
RB = 4
NT = B * K // P
FIRST = 8
EARLY = NT - 4
REC = 2 * D + 4


STEPS = dict(
    ut=0, upd=0, s1=1, ap1=2, tr1=2, tc1=2, cond=2, hid=3, gelu=3,
    mm2=6, z=7, rsp=7, nrm=9, stq=10, prev=11,
    apq=10, trq=13, tcq=13, qk=15, qhi=15, qlo=16)
Q_STEPS = ("stq", "apq", "trq", "tcq", "qk", "qhi", "qlo")


def when(step, h):
    at = CH * (h + 1) + STEPS[step]
    return at % SLOTS, at // SLOTS


def tiles_of(c):
    b, k = c // CH, c % CH
    return (b, 2 * k, 2, P) if k < CH - 1 else (b, 2 * k, 1, TAIL)


def pre_tiles(r):
    return (r // 4, 4 * (r % 4), 4, P) if r % 4 < 3 else (r // 4, FULL, 1, TAIL)


def last_dim(ap, n):
    return ap.rearrange("p (a b) -> p a b", b=1).to_broadcast([ap.shape[0], ap.shape[1], n])


def mid_dim(ap, n):
    return ap.rearrange("p (b a) -> p b a", b=1).to_broadcast([ap.shape[0], n, ap.shape[1]])


def build(nc, a, out):
    ctx = ExitStack()
    with ctx:
        def sb(name, shape, dt=F32):
            return ctx.enter_context(nc.sbuf_tensor(name, shape, dt))

        def pb(name, shape, dt=F32):
            return ctx.enter_context(nc.psum_tensor(name, shape, dt))

        def sem(name):
            return ctx.enter_context(nc.semaphore(name))

        W = {n: sb("w_" + n, [P, D]) for n in ("wk", "wv", "wq", "wu", "w1", "w2")}
        COLS = ("lnkv_g", "lnkv_b", "lnq_g", "lnq_b", "lnm_g", "lnm_b", "bk", "bv", "bq", "b1")
        cols = sb("cols", [P, len(COLS)])
        col = {n: cols[:, i:i + 1] for i, n in enumerate(COLS)}
        ROWS = ("lnp_g", "lnp_b", "b2", "bu", "q_mu", "q_logsig")
        rowt = sb("rowt", [P, len(ROWS), D])
        row = {n: rowt[:, i, :] for i, n in enumerate(ROWS)}
        ident = sb("ident", [P, P])
        ones = sb("ones", [P, P])
        negones = sb("negones", [P, P])
        meanw = sb("meanw", [P, 1])
        epst = sb("epst", [P, 32])
        neghalf = sb("neghalf", [P, 32])
        wtmp = sb("wtmp", [P, 6, D])
        ctmp = sb("ctmp", [P, 8])
        wqk = sb("wqk", [P, D])
        wvu = sb("wvu", [P, D])
        w1g = sb("w1g", [P, D])
        bvu = sb("bvu", [P, D])
        v1b = sb("v1b", [P, P])
        esig = sb("esig", [P, D])
        bqk, b1m = ctmp[:, 0:1], ctmp[:, 1:2]
        wg = sb("wg", [P, E])
        bgr = sb("bgr", [P, E])
        b1r = sb("b1r", [E * HT, P])
        b1c = sb("b1c", [P, E * HT])

        big = sb("big", [P, 4 * 2 * TILES * D])
        half_big = 2 * 2 * TILES * D
        stage = big[:, 0:half_big].rearrange("p (x b t d) -> p x b t d", x=2, b=2, t=TILES)
        nat = big[:, half_big:2 * half_big].rearrange("p (x b t d) -> p x b t d", x=2, b=2, t=TILES)
        th = sb("th", [P, 2, 2, S], F32R)
        tl = sb("tl", [P, 2, 2, S], F32R)
        x1 = sb("x1", [P, PAD + B, 2 * D])
        xb = sb("xb", [P, PAD + B, D])

        ex = sb("ex", [P, NE, 2, K])
        xs = sb("xs", [P, NE, 2, D])
        nmin = sb("nmin", [P, NE, 2])
        rsum = sb("rsum", [P, NE, 2])
        rinv = sb("rinv", [P, NE, 2])

        slots = sb("slots", [P, 4, D])
        slots0 = sb("slots0", [P, 2, 4, D])
        prevb = sb("prevb", [P, 2, 4, D])
        qhi = sb("qhi", [P, 2, 4 * P], F32R)
        qlo = sb("qlo", [P, 2, 4 * P], F32R)
        epsc = sb("epsc", [P, 2, 2])
        cpart = sb("cpart", [P, 2, 2, 4])
        ut = sb("ut", [P, 2, K])
        upd = sb("upd", [P, 8 * 4 * D])
        s1, s1b, sn1, zt, zg, snq = [upd[:, k * 4 * D:(k + 1) * 4 * D].rearrange("p (j d) -> p j d", j=4)
                                     for k in (0, 1, 2, 3, 4, 5)]
        snt, gt = [upd[:, k * 4 * D:(k + 1) * 4 * D] for k in (6, 7)]
        snqt = sb("snqt", [P, 2, K])
        rsig = sb("rsig", [P, 4])
        bst = sb("bst", [P, 3, 4, 6])
        mv = sb("mv", [P, 3, 4, 2])
        ve = sb("ve", [P, 3, 4])
        mneg = sb("mneg", [P, 3, 4])
        rstd = sb("rstd", [P, 3, 4])
        NS = 2 * TILES + 4
        xbst = sb("xbst", [P, NS, 6])
        xmv = sb("xmv", [P, 2, NS, 2])
        xve = sb("xve", [P, 32])
        xrs = sb("xrs", [P, 2, NS])
        xsd = sb("xsd", [P, 32])

        w1e = upd[:, 0:RB * H].rearrange("p (b n) -> p b n", b=RB)
        w2e = upd[:, RB * H:RB * (H + HT * D)].rearrange("p (b j d) -> p b j d", b=RB, j=HT)
        brow = x1[:, :, :].rearrange("p b n -> p (b n)")[:, 0:RB * 2 * REC].rearrange(
            "p (b j r) -> p b j r", b=RB, j=2)
        rec = big[:, 0:NT * REC].rearrange("p (t r) -> p t r", r=REC)
        at_ = [NT * REC]

        def cut(n):
            at_[0] += n
            return big[:, at_[0] - n:at_[0]]

        xnt = cut(2 * 512).rearrange("p (b n) -> p b n", b=2)
        xte = cut(2 * BLK).rearrange("p (b n) -> p b n", b=2)
        ht = ex[:, :, :, :].rearrange("p a b k -> p (a b k)")[:, 0:2 * HT * BLK].rearrange("p (b j n) -> p b j n", b=2, j=HT)
        b2e = cut(RB * D).rearrange("p (b n) -> p b n", b=RB)
        yo = cut(2 * 2 * D).rearrange("p (b j n) -> p b j n", b=2, j=2)
        ys = cut(RB * 2 * D).rearrange("p (b j n) -> p b j n", b=RB, j=2)
        b1e = cut(RB * HT).rearrange("p (b n) -> p b n", b=RB)
        idxt = sb("idxt", [P, RB, 2], U32)
        tick = sb("tick", [P, RB])
        fbst = sb("fbst", [P, NT, 6])
        fmv = sb("fmv", [P, NT, 2])
        fve = sb("fve", [P, NT])
        frs = sb("frs", [P, NT])
        ga = [cut(E * NT).rearrange("p (e t) -> p e t", e=E) for i in range(4)]
        gr = sb("gr", [P, 3, NT])
        ltri = sb("ltri", [P, P])
        iota8 = sb("iota8", [P, E])
        iotaj = sb("iotaj", [P, NBLK])
        scanm = sb("scanm", [P, E * NT])
        cnt = sb("cnt", [P, 6, E])
        cmpb = sb("cmpb", [P, NBLK, E])
        bexp = sb("bexp", [P, NBLK])
        bexpi = sb("bexpi", [P, NBLK], I32)
        posi = sb("posi", [P, NT], U32)
        fill = sb("fill", [P, REC])

        lg = [pb(f"lg{i}", [P, 2, K]) for i in range(NL)]
        pv = [pb(f"pv{i}", [P, 2 * K]) for i in range(2)]
        px = pb("px", [P, 4 * P])
        py = pb("py", [P, 4 * P])
        pz = pb("pz", [P, 4 * P])
        ybank = [pz[:, 0:2 * D], py[:, 0:2 * D]]
        hbank = [lg[0][:, 0, :], lg[1][:, 0, :], lg[2][:, 0, :], pv[0][:, 0:BLK]]

        scratch = nc.dram_tensor("routed", (NBLK * BLK, REC), F32, kind="Internal").ap()

        weights_in = sem("weights_in")
        x_in = sem("x_in")
        rows_in = sem("rows_in")
        cond_in = sem("cond_in")
        stage_in = [sem("stage_p_in"), sem("stage_q_in")]
        consts = sem("consts")
        prep = sem("prep")
        fill_in = sem("fill_in")
        wstep = sem("wstep")
        lg_ready = sem("lg_ready")
        min_ready = sem("min_ready")
        exp_done = sem("exp_done")
        inv_ready = sem("inv_ready")
        xs_ready = sem("xs_ready")
        pv_done = sem("pv_done")
        def halves(name):
            return [sem(name + "_a"), sem(name + "_b")]

        ut_ready = halves("ut_ready")
        upd_ready = halves("upd_ready")
        st1_ready = halves("st1_ready")
        sn1_ready = halves("sn1_ready")
        tr1_ready = halves("tr1_ready")
        tc1_ready = halves("tc1_ready")
        s1b_ready = halves("s1b_ready")
        h_ready = halves("h_ready")
        g_ready = halves("g_ready")
        o_ready = halves("o_ready")
        stp_ready = halves("stp_ready")
        rsp_ready = halves("rsp_ready")
        slots_ready = halves("slots_ready")
        stq_ready = halves("stq_ready")
        snq_ready = halves("snq_ready")
        trq_ready = halves("trq_ready")
        tcq_ready = halves("tcq_ready")
        qk_ready = halves("qk_ready")
        qhi_ready = halves("qhi_ready")
        qlo_ready = halves("qlo_ready")
        slots0_ready = sem("slots0_ready")
        x1_done = sem("x1_done")
        xstat_ready = sem("xstat_ready")
        xrs_ready = sem("xrs_ready")
        xcm_ready = sem("xcm_ready")
        ap_ready = sem("ap_ready")
        app_ready = sem("app_ready")
        z_ready = sem("z_ready")
        hi_ready = sem("hi_ready")
        epsc_ready = sem("epsc_ready")
        lo_ready = sem("lo_ready")
        fstat = sem("fstat")
        frs_ready = sem("frs_ready")
        xn_ready = sem("xn_ready")
        xt_ready = sem("xt_ready")
        xtc_ready = sem("xtc_ready")
        gate_ready = sem("gate_ready")
        gmax_ready = sem("gmax_ready")
        gexp_ready = sem("gexp_ready")
        hot_ready = sem("hot_ready")
        rank_ready = sem("rank_ready")
        pos_ready = sem("pos_ready")
        recx_ready = sem("recx_ready")
        recid_ready = sem("recid_ready")
        scattered = sem("scattered")
        we_in = [sem(f"we_in{i}") for i in range(RB)]
        row_in = [sem(f"row_in{i}") for i in range(RB)]
        b1e_ready = sem("b1e_ready")
        bt_ready = sem("bt_ready")
        btc_ready = sem("btc_ready")
        bh_ready = sem("bh_ready")
        bg_ready = sem("bg_ready")
        by_ready = sem("by_ready")
        ys_ready = sem("ys_ready")
        ticked = sem("ticked")
        out_done = [sem(f"out_done{i}") for i in range(RB)]

        WEIGHTS_IN = 16 * (len(W) + 2)
        ROWS_IN = 16 * (len(COLS) + len(ROWS) + 1)

        def ctx_dram(b):
            rows = a["ctx_1024"][b]
            return rows[0:FULL * P, :].rearrange("(p t) d -> p t d", t=FULL), rows[FULL * P:S, :]

        def pre_pair(s):
            return 1 if s == 0 else 0

        def pre_base(i, s, per_pair):
            return i * (2 * per_pair) + (per_pair if s == 0 else 2 * per_pair)

        def pool_step(r):
            return r - r // 4

        def in_prologue(step, h):
            return when(step, h)[1] == 1 and step in Q_STEPS

        def credit(eng, sems, step):
            for h in range(2):
                eng.sem_inc(sems[h], CR - 1 if in_prologue(step, h) else CR)

        def made(i, s, source, step, h):
            return i * ROUNDS + (s + 1 + CR - (when(step, h)[1] - when(source, h)[1]))

        def latest(i, s, c, source, h):
            return i * ROUNDS + (s + CR + (1 if when(source, h)[0] < c else 0))

        def pair_of(s, step, h):
            return (s - when(step, h)[1]) % 2

        def finished(s, step, h):
            return (s - when(step, h)[1]) % ROUNDS >= ROUNDS - 2

        def now(c, step, h, final):
            if final and (when(step, h)[1] != 1 or step in Q_STEPS):
                return False
            return when(step, h)[0] == c

        def final_at(i, s):
            return i * 4 + (0 if s == 0 else 2)

        def cols_of(t0, n, rows):
            return slice(t0 * P, t0 * P + (n - 1) * P + rows)

        block = ctx.enter_context(nc.Block())

        @block.sync
        def _(sp):
            def load_stage(x, group):
                for b in range(2):
                    full, tail = ctx_dram(group * 4 + 2 * x + b)
                    sp.dma_start(stage[:, x, b, 0:FULL, :], full).then_inc(stage_in[x], 16)
                    sp.dma_start(stage[0:TAIL, x, b, FULL, :], tail).then_inc(stage_in[x], 16)

            load_stage(0, 0)
            sp.dma_start(x1[:, PAD:PAD + B, :], a["x"].rearrange("b (p j) d -> p b (j d)", j=2)).then_inc(x_in, 16)
            for n in W:
                sp.dma_start(W[n][:, :], a["L0_xcond_" + n]).then_inc(weights_in, 16)
            sp.dma_start(wg[:, :], a["L0_ffn_Wg"]).then_inc(weights_in, 16)
            sp.dma_start(b1r[:, :], a["L0_ffn_b1"].rearrange("e (j p) -> (e j) p", p=P)).then_inc(weights_in, 16)
            with nc.allow_non_contiguous_dma(reason="bias columns: 128 elements each"):
                for n in COLS:
                    sp.dma_start(col[n], a["L0_xcond_" + n].rearrange("(p o) -> p o", o=1)).then_inc(rows_in, 16)
            for n in ROWS:
                src = a["L0_xcond_" + n]
                src = src[0, 0] if len(src.shape) == 3 else src
                sp.dma_start(row[n], src.partition_broadcast(P)).then_inc(rows_in, 16)
            sp.dma_start(bgr[:, :], a["L0_ffn_bg"].partition_broadcast(P)).then_inc(rows_in, 16)
            load_stage(1, 0)
            sp.dma_start(xb[:, PAD:PAD + B, :].rearrange("p b d -> p (b d)"),
                         a["cond_1024"].rearrange("b d -> (b d)").partition_broadcast(P)).then_inc(cond_in, 16)
            sp.wait_ge(fill_in, 1)
            n = NBLK * BLK // P
            for i in range(n):
                sp.dma_start(scratch[i * P:(i + 1) * P, :], fill[:, :]).then_inc(fill_in, 16)

            with sp.Fori(0, GROUPS) as i:
                nxt = (i * 4 + 4) % B
                for x in range(2):
                    sp.wait_ge(z_ready, i * (2 * PRE) + PRE * (x + 1))
                    for b in range(2):
                        full, tail = ctx_dram(nxt + (2 * x + b))
                        sp.dma_start(stage[:, x, b, 0:FULL, :], full).then_inc(stage_in[x], 16)
                        sp.dma_start(stage[0:TAIL, x, b, FULL, :], tail).then_inc(stage_in[x], 16)

            w1d = a["L0_ffn_W1"]
            w2d = a["L0_ffn_W2"].rearrange("e (j p) d -> e p j d", p=P)
            b2d = a["L0_ffn_b2"]
            rows = scratch.rearrange("(k p j) r -> k p j r", p=P, j=2)
            sp.wait_ge(pos_ready, 1)

            def feed_weights(i, k):
                e = sp.value_load(bexpi[0:1, bass.ds(i * RB + k, 1)], min_val=0, max_val=E - 1)
                if not isinstance(i, int) or i:
                    sp.wait_ge(ys_ready, i * RB + (k + 1 - RB))
                sp.dma_start(w1e[:, k, :], w1d[e]).then_inc(we_in[k], 16)
                sp.dma_start(w2e[:, k, :, :], w2d[e]).then_inc(we_in[k], 16)
                sp.dma_start(b2e[:, k, :], b2d[e].partition_broadcast(P)).then_inc(we_in[k], 16)

            for k in range(RB):
                feed_weights(0, k)
            sp.wait_ge(scattered, 16 * NT)
            for k in range(RB):
                sp.dma_start(brow[:, k, :, :], rows[k]).then_inc(row_in[k], 16)
            with sp.Fori(1, NBLK // RB) as i:
                for k in range(RB):
                    feed_weights(i, k)
                    sp.dma_start(brow[:, k, :, :], rows[i * RB + k]).then_inc(row_in[k], 16)

        @block.gpsimd
        def _(pool):
            g = nc.gpsimd
            g.memset(ident[:, :], 0.0)
            g.memset(ltri[:, :], 0.0)
            pool.drain()
            g.affine_select(out=ident[:, :], in_=ident[:, :], compare_op=ALU.not_equal, fill=1.0, base=0,
                            pattern=[[-1, P]], channel_multiplier=1)
            g.affine_select(out=ltri[:, :], in_=ltri[:, :], compare_op=ALU.is_ge, fill=1.0, base=0,
                            pattern=[[-1, P]], channel_multiplier=1)
            g.memset(ones[:, :], 1.0)
            g.memset(negones[:, :], -1.0)
            g.memset(meanw[:, :], 1.0 / D)
            g.memset(epst[:, :], LN_EPS)
            g.memset(neghalf[:, :], -0.5).then_inc(consts, 1)
            g.memset(fill[:, :], 0.0)
            pool.drain()
            g.iota(fill[:, REC - 3:REC - 2].bitcast(U32), [[0, 1]], base=2 * B * K,
                   channel_multiplier=0).then_inc(fill_in, 1)
            g.iota(iota8[:, :], [[1, E]], base=0, channel_multiplier=0, allow_small_or_imprecise_dtypes=True)
            g.iota(iotaj[:, :], [[1, NBLK]], base=0, channel_multiplier=0, allow_small_or_imprecise_dtypes=True)
            g.memset(scanm[:, :], 1.0)
            pool.drain()
            g.memset(scanm[:, :].rearrange("p (e t) -> p e t", t=NT)[:, :, 0:1], 0.0).then_inc(consts, 1)
            g.memset(xb[:, 0:PAD, :], 0.0)
            g.memset(prevb[:, 1, :, :], 0.0)
            def context_rstd(x, piece, count):
                n = NS // PIECES
                ns = slice(NS - n * (piece + 1), NS - n * piece)
                pool.wait_ge(xstat_ready, count)
                g.tensor_tensor(xrs[:, x, ns], xve[:, ns], neghalf[:, ns], ALU.pow).then_inc(xrs_ready, 1)

            def layer_rstd(k, h, sem_in, count, sem_out=None):
                t0, t1 = 2 * h, 2 * h + 2
                pool.wait_ge(sem_in, count)
                g.tensor_tensor(ve[:, k, t0:t1], mv[:, k, t0:t1, 1], epst[:, t0:t1], ALU.add)
                if sem_out is None:
                    g.tensor_tensor(mneg[:, k, t0:t1], mv[:, k, t0:t1, 0], negones[:, t0:t1], ALU.mult)
                pool.drain()
                last = g.tensor_tensor(rstd[:, k, t0:t1], ve[:, k, t0:t1], neghalf[:, t0:t1], ALU.pow)
                if sem_out is not None:
                    last.then_inc(sem_out, 1)

            def layer_norm(k, h, src, dst, sem_in, count, sem_out):
                layer_rstd(k, h, sem_in, count)
                pool.drain()
                for t in range(2 * h, 2 * h + 2):
                    last = g.tensor_scalar(dst[:, t, :], src[:, t, :], mneg[:, k, t:t + 1], rstd[:, k, t:t + 1],
                                           ALU.add, ALU.mult)
                last.then_inc(sem_out, 1)

            def scale_rows(i, n, behind=None):
                m = n % TRIP
                b, t0, nt, rows = tiles_of(m % SLOTS)
                x = (m // SLOTS) % 2
                k = n % NE
                pool.wait_ge(pv_done, i * TRIP + (n + 1 - NE + CREDIT if behind is None else behind))
                pool.wait_ge(inv_ready, i * TRIP + (n + 1))
                g.tensor_tensor(xs[0:rows, k, 0:nt, :], nat[0:rows, x, b, t0:t0 + nt, :],
                                last_dim(rinv[0:rows, k, 0:nt], D), ALU.mult).then_inc(xs_ready, 1)

            def pre_apply(x, r):
                b, t0, nt, rows = pre_tiles(r)
                for t in range(t0, t0 + 2):
                    n = b * TILES + t
                    last = g.tensor_scalar(nat[:, x, b, t, :], stage[:, x, b, t, :], xmv[:, x, n, 0:1],
                                           xrs[:, x, n:n + 1], ALU.add, ALU.mult)
                last.then_inc(app_ready, 1)

            def add_cond(i, s, h):
                at = i * 4 + (PAD + 2 * pair_of(s, "cond", h) - (4 if s < when("cond", h)[1] else 0))
                src = xb[:, bass.ds(at + h, 1), :].to_broadcast([P, 2, D])
                g.tensor_tensor(s1b[:, 2 * h:2 * h + 2, :], s1[:, 2 * h:2 * h + 2, :], src,
                                ALU.add).then_inc(s1b_ready[h], 1)

            def new_prev(i, s, h, final):
                x, last_round = pair_of(s, "prev", h), finished(s, "prev", h)
                src = slots0[:, x, :, :] if last_round else slots
                pool.wait_ge(slots_ready[h], made(i, s, "nrm", "prev", h))
                if not final:
                    g.tensor_tensor(prevb[:, x, 2 * h:2 * h + 2, :], src[:, 2 * h:2 * h + 2, :], mid_dim(bvu[:, :], 2),
                                    ALU.add)
                if last_round:
                    at = final_at(i, s)
                    dst = x1[:, bass.ds(at + h, 1), :]
                    g.tensor_tensor(dst, dst, slots[:, 2 * h:2 * h + 2, :].rearrange("p (o j) d -> p o (j d)", o=1),
                                    ALU.add).then_inc(x1_done, 1)

            def update_first(i, s, c, final=False):
                for h in (1, 0):
                    if now(c, "ap1", h, final):
                        layer_norm(0, h, s1, sn1, st1_ready[h], made(i, s, "s1", "ap1", h), sn1_ready[h])

            def update(i, s, c, final=False):
                for h in (1, 0):
                    if now(c, "cond", h, final):
                        add_cond(i, s, h)
                    if now(c, "rsp", h, final):
                        layer_rstd(1, h, stp_ready[h], made(i, s, "z", "rsp", h), rsp_ready[h])
                    if now(c, "apq", h, final):
                        layer_norm(2, h, slots0[:, pair_of(s, "apq", h), :, :] if finished(s, "apq", h) else slots,
                                   snq, stq_ready[h], made(i, s, "stq", "apq", h), snq_ready[h])
                    if now(c, "prev", h, final):
                        new_prev(i, s, h, final)

            for sems, step in ((sn1_ready, "ap1"), (s1b_ready, "cond"), (rsp_ready, "rsp"), (snq_ready, "apq")):
                credit(pool, sems, step)
            for piece in range(PIECES):
                context_rstd(0, piece, 1)
            pool.wait_ge(xcm_ready, 1)
            pool.drain()
            for r in range(PRE):
                if r % 4 < 3:
                    pre_apply(0, r)
            pool.wait_ge(prep, 3)
            for h in range(2):
                layer_norm(2, h, slots0[:, 0, :, :], snq, stq_ready[h], CR, snq_ready[h])
            pool.wait_ge(slots0_ready, 1)
            g.tensor_tensor(prevb[:, 0, :, :], slots0[:, 0, :, :], mid_dim(bvu[:, :], 4), ALU.add)
            for n in range(SCALE - 1):
                scale_rows(0, n)
            for piece in range(PIECES):
                context_rstd(1, piece, 2)
            pool.wait_ge(rows_in, ROWS_IN)
            pool.wait_ge(cond_in, 16)
            g.tensor_tensor(xb[:, PAD:PAD + B, :], xb[:, PAD:PAD + B, :], mid_dim(row["b2"], B), ALU.add)
            pool.drain()
            scale_rows(0, SCALE - 1)
            with pool.Fori(0, GROUPS) as i:
                for s in range(ROUNDS):
                    for c in range(SLOTS):
                        n = s * SLOTS + c
                        pre = s in (0, 5)
                        update_first(i, s, c)
                        steps = [r for r in range(PRE) if pre and PRE_SLOT[r] == c and r % 4 < 3]
                        for r in steps:
                            if r:
                                pre_apply(pre_pair(s), r)
                        if pre and c == 0:
                            pool.wait_ge(xcm_ready, i * 2 + (2 if s == 0 else 3))
                        scale_rows(i, n + SCALE, n + CREDIT if pre and c == 0 else None)
                        if 0 in steps:
                            pre_apply(pre_pair(s), 0)
                        update(i, s, c)
                        if s in (2, 4) and c >= SLOTS - PIECES:
                            context_rstd(s // 2 - 1, c - (SLOTS - PIECES), i * 2 + (3 if s == 2 else 4))
            def final_rstd(t0, t1, count):
                pool.wait_ge(fstat, count)
                g.tensor_tensor(fve[:, t0:t1], fmv[:, t0:t1, 1], epst[:, t0:t1], ALU.add)
                pool.drain()
                g.tensor_tensor(frs[:, t0:t1], fve[:, t0:t1], neghalf[:, t0:t1], ALU.pow).then_inc(frs_ready, 1)

            for c in range(SLOTS):
                update_first(GROUPS, 0, c, final=True)
                update(GROUPS, 0, c, final=True)
                if c == when("rsp", 1)[0]:
                    final_rstd(0, FIRST, 1)
            final_rstd(FIRST, EARLY, 1)
            final_rstd(EARLY, NT, 2)
            g.iota(rec[:, :, 2 * D + 1].bitcast(U32).rearrange("p (b j) -> p b j", j=2), [[K, B], [1, 2]], base=0,
                   channel_multiplier=2).then_inc(recid_ready, 1)
            g.memset(rec[:, :, 2 * D + 2:REC], 0.0).then_inc(recid_ready, 1)
            pool.wait_ge(fill_in, 1 + 16 * (NBLK * BLK // P))
            pool.wait_ge(pos_ready, 1)
            pool.wait_ge(recx_ready, 1)
            pool.wait_ge(recid_ready, 2)
            for t in range(NT):
                g.indirect_dma_start(scratch, bass.IndirectOffsetOnAxis(posi[:, t:t + 1], 0), rec[:, t, :],
                                     None).then_inc(scattered, 16)
            last_row = pool.to_reg(B * K - 1)

            def store(i):
                for k in range(RB):
                    pool.wait_ge(ys_ready, i * RB + (k + 1))
                    g.tensor_tensor(tick[:, k:k + 1], ones[:, 0:1], ones[:, 0:1],
                                    ALU.mult).then_inc(ticked, 1)
                    for j in range(2):
                        g.indirect_dma_start(out.rearrange("b k d -> (b k) d"),
                                             bass.IndirectOffsetOnAxis(idxt[:, k, j:j + 1], 0),
                                             ys[:, k, j, :], None, bounds_check=last_row,
                                             oob_is_err=False).then_inc(out_done[k], 16)

            with pool.Fori(0, NBLK // RB) as i:
                store(i)
            for k in range(RB):
                pool.wait_ge(out_done[k], 32 * (NBLK // RB))

        @block.scalar
        def _(act):
            A = nc.scalar.activation

            def exp(i, n):
                _, _, nt, rows = tiles_of(n % SLOTS)
                k = n % NE
                act.wait_ge(pv_done, i * TRIP + (n + 1 - NE + CREDIT))
                act.wait_ge(min_ready, i * TRIP + (n + 1))
                for j in range(nt):
                    last = A(ex[0:rows, k, j, :], lg[n % NL][0:rows, j, :], ACT.Exp, bias=nmin[0:rows, k, j:j + 1],
                             scale=-1.0, accum_out=rsum[0:rows, k, j:j + 1])
                last.then_inc(exp_done, 1)

            def copy_u(h, x, products, i):
                act.wait_ge(pv_done, i * TRIP + (products + CREDIT))
                A(ut[:, h, :], pv[h][:, 0:K], ACT.Identity, bias=epsc[:, x, h:h + 1]).then_inc(ut_ready[h], 1)

            def copy_1(h, count):
                act.wait_ge(tr1_ready[h], count)
                A(snt[:, h * K:(h + 1) * K], px[:, K:2 * K], ACT.Copy).then_inc(tc1_ready[h], 1)

            def gelu(h, count):
                act.wait_ge(h_ready[h], count)
                A(gt[:, h * K:(h + 1) * K], px[:, 0:K], ACT.Gelu, bias=b1m).then_inc(g_ready[h], 1)

            def q_copy(h, count):
                act.wait_ge(trq_ready[h], count)
                A(snqt[:, h, :], px[:, K:2 * K], ACT.Copy).then_inc(tcq_ready[h], 1)

            def q_hi(h, x, count):
                act.wait_ge(qk_ready[h], count)
                A(qhi[:, x, h * K:(h + 1) * K], pv[h][:, K:2 * K], ACT.Identity, bias=bqk).then_inc(qhi_ready[h], 1)

            def update_first(i, s, c, final=False):
                for h in (1, 0):
                    if now(c, "ut", h, final):
                        copy_u(h, pair_of(s, "ut", h), (s + 1 - when("ut", h)[1]) * SLOTS - (0 if h else CH), i)

            def update(i, s, c, final=False):
                for h in (1, 0):
                    if now(c, "tc1", h, final):
                        copy_1(h, made(i, s, "tr1", "tc1", h))
                    if now(c, "gelu", h, final):
                        gelu(h, made(i, s, "hid", "gelu", h))
                    if now(c, "tcq", h, final):
                        q_copy(h, made(i, s, "trq", "tcq", h))
                    if now(c, "qhi", h, final):
                        q_hi(h, pair_of(s, "qhi", h), made(i, s, "qk", "qhi", h))

            def pre_hi(i, x, r, base, bank=pz):
                act.wait_ge(z_ready, base + r + 1)
                b, t0, nt, rows = pre_tiles(r)
                n = (nt - 1) * P + rows
                A(th[:, x, b, cols_of(t0, nt, rows)], bank[:, 0:n], ACT.Copy,
                  accum_out=cpart[:, x, b, r % 4:r % 4 + 1]).then_inc(hi_ready, 1)

            act.sem_inc(exp_done, CREDIT)
            for sems, step in ((ut_ready, "ut"), (tc1_ready, "tc1"), (g_ready, "gelu"),
                               (tcq_ready, "tcq"), (qhi_ready, "qhi")):
                credit(act, sems, step)
            act.wait_ge(rows_in, ROWS_IN)
            A(esig[:, :], row["q_logsig"], ACT.Exp).then_inc(prep, 1)
            for r in range(PRE):
                pre_hi(0, 0, r, 0, (pz, py)[r % 2])
            for h in range(2):
                if in_prologue("tcq", h):
                    q_copy(h, CR)
                if in_prologue("qhi", h):
                    q_hi(h, 0, CR)
            for n in range(AHEAD):
                exp(0, n)
            with act.Fori(0, GROUPS) as i:
                for s in range(ROUNDS):
                    for c in range(SLOTS):
                        update_first(i, s, c)
                        exp(i, s * SLOTS + c + AHEAD)
                        if s in (0, 5):
                            for r in range(PRE):
                                if PRE_SLOT[r] + TRANSPOSE == c:
                                    pre_hi(i, pre_pair(s), r, pre_base(i, s, PRE))
                        update(i, s, c)
            for c in range(SLOTS):
                update_first(GROUPS, 0, c, final=True)
                update(GROUPS, 0, c, final=True)

            act.wait_ge(frs_ready, 1)
            for t in range(0, NT, 8):
                if t == NT - 8:
                    act.wait_ge(frs_ready, 3)
                last = A(rec[:, t:t + 8, D:2 * D],
                         x1[:, PAD + t // 2:PAD + t // 2 + 4, :].rearrange("p b (j d) -> p (b j) d", d=D), ACT.Copy)
            last.then_inc(recx_ready, 1)
            for r in range(NT // 4):
                act.wait_ge(xt_ready, r + 1)
                if r >= 2:
                    act.wait_ge(gate_ready, r - 1)
                A(xnt[:, r % 2, :], lg[r % 2][:, :, :].rearrange("p a b -> p (a b)"), ACT.Copy).then_inc(xtc_ready, 1)
            act.wait_ge(gmax_ready, 1)
            A(ga[1][:, :, :], ga[1][:, :, :], ACT.Exp).then_inc(gexp_ready, 1)
            with act.Fori(0, NBLK // RB) as i:
                for k in range(RB):
                    act.wait_ge(b1e_ready, i * RB + (k + 1))
                    for j in range(HT):
                        act.wait_ge(bh_ready, i * (RB * HT) + (k * HT + j + 1))
                        A(ht[:, k % 2, j, :], hbank[j], ACT.Silu, bias=b1e[:, k, j:j + 1]).then_inc(bg_ready, 1)

        @block.vector
        def _(dve):
            v = nc.vector

            def layer_stats(k, t0, t1, tiles, sem_out):
                for j in range(t0, t1):
                    v.bn_stats(bst[:, k, j, :], tiles[:, j, :])
                dve.drain()
                for j in range(t0, t1):
                    last = v.bn_aggr(mv[:, k, j, :], bst[:, k, j, :])
                last.then_inc(sem_out, 1)

            def row_min(i, n):
                _, _, nt, rows = tiles_of(n % SLOTS)
                dve.wait_ge(lg_ready, i * TRIP + (n + 1))
                v.tensor_reduce(nmin[0:rows, n % NE, 0:nt], lg[n % NL][0:rows, 0:nt, :], AX.X,
                                ALU.min).then_inc(min_ready, 1)

            def row_inv(i, n):
                _, _, nt, rows = tiles_of(n % SLOTS)
                dve.wait_ge(exp_done, i * TRIP + (n + 1 + CREDIT))
                v.reciprocal(rinv[0:rows, n % NE, 0:nt], rsum[0:rows, n % NE, 0:nt]).then_inc(inv_ready, 1)

            def slots_from_x(i, x, at, h):
                for j in range(2):
                    t = 2 * h + j
                    xt = x1[:, bass.ds(at + h, 1), j * D:(j + 1) * D].rearrange("p a d -> p (a d)")
                    n = 2 * TILES + t
                    v.scalar_tensor_tensor(zg[:, t, :], xt, xmv[:, x, n, 0:1], esig[:, :], ALU.subtract, ALU.mult)
                dve.drain()
                for t in range(2 * h, 2 * h + 2):
                    n = 2 * TILES + t
                    last = v.scalar_tensor_tensor(slots0[:, x, t, :], zg[:, t, :], xrs[:, x, n:n + 1], row["q_mu"],
                                                  ALU.mult, ALU.add)
                return last

            def context_stats(i, x, n0, n1):
                for n in range(n0, n1):
                    b, t = n // TILES, n % TILES
                    rows = P if t < FULL else TAIL
                    v.bn_stats(xbst[0:rows, n, :], stage[0:rows, x, b, t, :])

            def x_stats(i, at):
                for j in range(4):
                    v.bn_stats(xbst[:, 2 * TILES + j, :],
                               x1[:, bass.ds(at + j // 2, 1), (j % 2) * D:(j % 2 + 1) * D].rearrange("p a d -> p (a d)"))

            def context_aggr(x, n0, n1):
                for n in range(n0, n1):
                    rows = TAIL if n < 2 * TILES and n % TILES == FULL else P
                    last = v.bn_aggr(xmv[0:rows, x, n, :], xbst[0:rows, n, :])
                return last

            def variances(x):
                dve.drain()
                v.tensor_tensor(xve[:, 0:NS], xmv[:, x, :, 1], epst[:, 0:NS], ALU.add).then_inc(xstat_ready, 1)

            def context_shift(x):
                m = xmv[:, x, 0:2 * TILES, 0]
                v.tensor_tensor(xsd[:, 0:2 * TILES], xve[:, 0:2 * TILES], xrs[:, x, 0:2 * TILES], ALU.mult)
                dve.drain()
                v.tensor_tensor(m, xsd[:, 0:2 * TILES], m, ALU.subtract).then_inc(xcm_ready, 1)
                dve.drain()

            def pre_apply(x, r):
                b, t0, nt, rows = pre_tiles(r)
                for t in range(t0 + (2 if nt == 4 else 0), t0 + nt):
                    n = b * TILES + t
                    last = v.tensor_scalar(nat[0:rows, x, b, t, :], stage[0:rows, x, b, t, :],
                                           xmv[0:rows, x, n, 0:1], xrs[0:rows, x, n:n + 1],
                                           ALU.add, ALU.mult)
                last.then_inc(ap_ready, 1)

            def pre_lo(x, r, base, bank=pz):
                dve.wait_ge(hi_ready, base + r + 1)
                b, t0, nt, rows = pre_tiles(r)
                n = (nt - 1) * P + rows
                cs = cols_of(t0, nt, rows)
                v.tensor_tensor(tl[:, x, b, cs], bank[:, 0:n], th[:, x, b, cs].bitcast(F32),
                                ALU.subtract).then_inc(lo_ready, 1)
                if r % 4 == 3:
                    v.tensor_reduce(epsc[:, x, b:b + 1], cpart[:, x, b, :], AX.X, ALU.add)
                    dve.drain()
                    v.tensor_scalar(epsc[:, x, b:b + 1], epsc[:, x, b:b + 1], ATTN_EPS, None,
                                    ALU.mult).then_inc(epsc_ready, 1)

            def q_lo(h, x, count):
                dve.wait_ge(qhi_ready[h], count)
                v.scalar_tensor_tensor(qlo[:, x, h * K:(h + 1) * K], pv[h][:, K:2 * K], bqk,
                                       qhi[:, x, h * K:(h + 1) * K].bitcast(F32), ALU.add,
                                       ALU.subtract).then_inc(qlo_ready[h], 1)

            def slots_1(h, x, count):
                dve.wait_ge(upd_ready[h], count)
                v.reciprocal(rsig[:, 2 * h:2 * h + 2], px[:, K:K + 2])
                dve.drain()
                for j in range(2):
                    t = 2 * h + j
                    v.scalar_tensor_tensor(s1[:, t, :], px[:, j * D:(j + 1) * D], rsig[:, t:t + 1],
                                           prevb[:, x, t, :], ALU.mult, ALU.add)
                dve.drain()
                layer_stats(0, 2 * h, 2 * h + 2, s1, st1_ready[h])

            def slots_2(i, s, h):
                dve.wait_ge(s1b_ready[h], made(i, s, "cond", "z", h))
                dve.wait_ge(o_ready[h], made(i, s, "mm2", "z", h))
                v.tensor_tensor(zt[:, 2 * h:2 * h + 2, :], py[:, 0:K].rearrange("p (j d) -> p j d", j=2),
                                s1b[:, 2 * h:2 * h + 2, :], ALU.add)
                dve.drain()
                layer_stats(1, 2 * h, 2 * h + 2, zt, stp_ready[h])

            def new_slots(h, count):
                dve.wait_ge(rsp_ready[h], count)
                for t in range(2 * h, 2 * h + 2):
                    v.scalar_tensor_tensor(zg[:, t, :], zt[:, t, :], mv[:, 1, t, 0:1], row["lnp_g"],
                                           ALU.subtract, ALU.mult)
                dve.drain()
                for t in range(2 * h, 2 * h + 2):
                    last = v.scalar_tensor_tensor(slots[:, t, :], zg[:, t, :], rstd[:, 1, t:t + 1],
                                                  row["lnp_b"], ALU.mult, ALU.add)
                last.then_inc(slots_ready[h], 1)
                dve.drain()

            def update_first(i, s, c):
                for h in (1, 0):
                    if now(c, "qlo", h, False):
                        q_lo(h, pair_of(s, "qlo", h), made(i, s, "qhi", "qlo", h))

            def update(i, s, c, final=False):
                for h in (1, 0):
                    if now(c, "s1", h, final):
                        slots_1(h, pair_of(s, "s1", h), made(i, s, "upd", "s1", h))
                    if now(c, "z", h, final):
                        slots_2(i, s, h)
                    if now(c, "nrm", h, final):
                        new_slots(h, made(i, s, "rsp", "nrm", h))
                    if now(c, "stq", h, final):
                        layer_stats(2, 2 * h, 2 * h + 2,
                                    slots0[:, pair_of(s, "stq", h), :, :] if finished(s, "stq", h) else slots,
                                    stq_ready[h])

            for sems, step in ((st1_ready, "s1"), (stp_ready, "z"), (slots_ready, "nrm"),
                               (stq_ready, "stq"), (qlo_ready, "qlo")):
                credit(dve, sems, step)
            v.memset(x1[:, 0:PAD, :], 0.0)
            v.memset(upd[:, :], 0.0)
            v.memset(epsc[:, :, :], 0.0)
            v.memset(xmv[:, :, :, :], 0.0)
            v.memset(xbst[:, :, :], 0.0)
            v.memset(pv[1][:, :], 1.0).then_inc(prep, 1)
            dve.drain()
            dve.wait_ge(stage_in[0], 64)
            context_stats(0, 0, 0, 2 * TILES)
            dve.wait_ge(x_in, 16)
            x_stats(0, PAD)
            dve.drain()
            context_aggr(0, 0, NS)
            dve.wait_ge(consts, 1)
            variances(0)
            dve.wait_ge(weights_in, WEIGHTS_IN)
            dve.wait_ge(rows_in, ROWS_IN)
            v.tensor_scalar(wtmp[:, 0, :], W["wk"][:, :], col["lnkv_g"], None, ALU.mult)
            v.tensor_scalar(wtmp[:, 1, :], W["wq"][:, :], col["lnq_g"], None, ALU.mult)
            v.tensor_scalar(wtmp[:, 2, :], W["wv"][:, :], col["lnkv_g"], None, ALU.mult)
            v.tensor_scalar(w1g[:, :], W["w1"][:, :], col["lnm_g"], None, ALU.mult).then_inc(consts, 1)
            dve.wait_ge(wstep, 1)
            pc = px[:, 0:8]
            v.tensor_tensor(ctmp[:, 2:3], pc[:, 0:1], col["bk"], ALU.add)
            v.tensor_tensor(ctmp[:, 3:4], pc[:, 1:2], col["bq"], ALU.add)
            v.tensor_tensor(ctmp[:, 4:5], pc[:, 2:3], col["bv"], ALU.add)
            v.tensor_tensor(b1m, pc[:, 3:4], col["b1"], ALU.add)
            dve.drain()
            v.tensor_tensor(ctmp[:, 5:6], ctmp[:, 2:3], pc[:, 4:5], ALU.subtract)
            dve.drain()
            v.tensor_scalar(ctmp[:, 6:7], ctmp[:, 5:6], 1.0 / D, None, ALU.mult)
            dve.drain()
            v.tensor_scalar(wtmp[:, 3, :], py[:, 0:D], ctmp[:, 6:7], None, ALU.add)
            v.tensor_copy(wtmp[:, 4, :], py[:, D:2 * D])
            v.tensor_copy(wtmp[:, 5, :], py[:, 2 * D:3 * D])
            v.tensor_scalar(v1b[:, :], ones[:, :], ctmp[:, 4:5], None, ALU.mult).then_inc(consts, 1)
            dve.wait_ge(wstep, 2)
            v.tensor_scalar(wqk[:, :], pz[:, 0:D], -float(D) ** 0.5, None, ALU.mult)
            v.tensor_scalar(bqk, pz[:, 2 * D:2 * D + 1], -float(D) ** 0.5, None, ALU.mult)
            v.tensor_copy(wvu[:, :], pz[:, D:2 * D]).then_inc(consts, 1)
            dve.wait_ge(wstep, 3)
            v.tensor_tensor(bvu[:, :], px[:, 0:D], row["bu"], ALU.add)
            v.tensor_copy(b1c[:, :], py[:, 0:E * HT]).then_inc(prep, 1)
            dve.wait_ge(prep, 3)
            dve.wait_ge(xrs_ready, PIECES)
            context_shift(0)
            dve.wait_ge(stage_in[1], 64)
            for r in range(PRE):
                pre_apply(0, r)
                if r:
                    pre_lo(0, r - 1, 0, (pz, py)[(r - 1) % 2])
                n = 2 * TILES // PRE
                context_stats(0, 1, n * r, n * (r + 1) if r < PRE - 1 else 2 * TILES)
                if r == 1:
                    for h in range(2):
                        last = slots_from_x(0, 0, PAD, h)
                    last.then_inc(slots0_ready, 1)
                    dve.drain()
                    for h in range(2):
                        layer_stats(2, 2 * h, 2 * h + 2, slots0[:, 0, :, :], stq_ready[h])
            x_stats(0, PAD + 2)
            dve.drain()
            context_aggr(1, 0, NS)
            variances(1)
            pre_lo(0, PRE - 1, 0, (pz, py)[(PRE - 1) % 2])
            for h in range(2):
                if in_prologue("qlo", h):
                    q_lo(h, 0, CR)
            for n in range(AHEAD):
                row_min(0, n)
            for n in range(SCALE - 1):
                row_inv(0, n)
            row_inv(0, SCALE - 1)
            dve.wait_ge(xrs_ready, 2 * PIECES)
            context_shift(1)
            for h in range(2):
                slots_from_x(0, 1, PAD + 2, h)
            dve.drain()

            with dve.Fori(0, GROUPS) as i:
                for s in range(ROUNDS):
                    for c in range(SLOTS):
                        n = s * SLOTS + c
                        update_first(i, s, c)
                        row_min(i, n + AHEAD)
                        row_inv(i, n + SCALE)
                        if s in (0, 5):
                            for r in range(PRE):
                                if PRE_SLOT[r] + LOWER == c:
                                    pre_lo(pre_pair(s), r, pre_base(i, s, PRE))
                        update(i, s, c)
                        if s in (0, 5):
                            for r in range(PRE):
                                if PRE_SLOT[r] == c:
                                    if r == 0:
                                        dve.wait_ge(pv_done, i * TRIP + (s * SLOTS + CREDIT))
                                    pre_apply(pre_pair(s), r)
                        if s in (1, 3):
                            x = s // 2
                            if c == 0:
                                dve.wait_ge(stage_in[x], i * 64 + 128)
                            if c < TILES:
                                context_stats(i, x, 2 * c, 2 * c + 2)
                            else:
                                x_stats(i, (i * 4 + 4) % B + (PAD + 2 * x))
                                dve.drain()
                        if s in (3, 5) and c == 0:
                            dve.wait_ge(xrs_ready, (i * 2 + (3 if s == 3 else 4)) * PIECES)
                            context_shift(s // 2 - 1)
                        if s in (2, 4):
                            x = s // 2 - 1
                            if c < 4:
                                context_aggr(x, 8 * c, min(8 * c + 8, NS))
                                if c == 3:
                                    variances(x)
                            for h in range(2):
                                if c == 11 + h:
                                    if h == 0:
                                        dve.wait_ge(xrs_ready, (i * 2 + (2 if s == 2 else 3)) * PIECES + 2)
                                    slots_from_x(i, x, (i * 4 + 4) % B + (PAD + 2 * x), h)
                                    if h == 1:
                                        dve.drain()
            def x1t(t):
                return x1[:, PAD + t // 2, (t % 2) * D:(t % 2 + 1) * D]

            for c in range(SLOTS):
                update(GROUPS, 0, c, final=True)
                if c == 0:
                    dve.wait_ge(x1_done, 4 * GROUPS)
                for t in range(4 * c, min(4 * c + 4, EARLY)):
                    v.bn_stats(fbst[:, t, :], x1t(t))
                if c == when("z", 1)[0]:
                    dve.drain()
                    for t in range(EARLY):
                        last = v.bn_aggr(fmv[:, t, :], fbst[:, t, :])
                    last.then_inc(fstat, 1)

            def rows_norm(t0, t1):
                for t in range(t0, t1):
                    last = v.tensor_scalar(rec[:, t, 0:D], x1t(t), fmv[:, t, 0:1], frs[:, t:t + 1],
                                           ALU.subtract, ALU.mult)
                    if t % 4 == 3:
                        last.then_inc(xn_ready, 1)

            dve.wait_ge(frs_ready, 1)
            rows_norm(0, FIRST)
            dve.wait_ge(x1_done, 4 * GROUPS + 2)
            for t in range(EARLY, NT):
                v.bn_stats(fbst[:, t, :], x1t(t))
            dve.drain()
            for t in range(EARLY, NT):
                last = v.bn_aggr(fmv[:, t, :], fbst[:, t, :])
            last.then_inc(fstat, 1)
            dve.wait_ge(frs_ready, 2)
            rows_norm(FIRST, EARLY)
            dve.wait_ge(frs_ready, 3)
            rows_norm(EARLY, NT)
            dve.wait_ge(gate_ready, NT // 4)
            v.tensor_tensor(ga[0][:, :, :], pv[0][:, 0:NT * E].rearrange("p (t e) -> p e t", e=E),
                            last_dim(bgr[:, :], NT), ALU.add)
            dve.drain()
            v.tensor_reduce(gr[:, 0, :], ga[0][:, :, :].rearrange("p e t -> p t e"), AX.X, ALU.max)
            dve.drain()
            v.tensor_tensor(ga[1][:, :, :], ga[0][:, :, :], mid_dim(gr[:, 0, :], E), ALU.subtract).then_inc(gmax_ready, 1)
            v.tensor_tensor(ga[2][:, :, :], ga[0][:, :, :], mid_dim(gr[:, 0, :], E), ALU.is_equal)
            dve.drain()
            v.scalar_tensor_tensor(ga[3][:, :, :], ga[2][:, :, :], -64.0, last_dim(iota8[:, :], NT), ALU.mult, ALU.add)
            dve.drain()
            v.tensor_reduce(gr[:, 1, :], ga[3][:, :, :].rearrange("p e t -> p t e"), AX.X, ALU.min)
            dve.drain()
            v.tensor_tensor(ga[2][:, :, :], ga[3][:, :, :], mid_dim(gr[:, 1, :], E), ALU.is_equal).then_inc(hot_ready, 1)
            dve.wait_ge(gexp_ready, 1)
            v.tensor_reduce(gr[:, 2, :], ga[1][:, :, :].rearrange("p e t -> p t e"), AX.X, ALU.add)
            dve.drain()
            v.reciprocal(rec[:, :, 2 * D], gr[:, 2, :])
            dve.wait_ge(rank_ready, 1)
            prefix = pv[1][:, 0:E * NT].rearrange("p (e t) -> p e t", e=E)
            totals = pv[1][:, E * NT:2 * E * NT].rearrange("p (e t) -> p e t", e=E)
            v.tensor_tensor_scan(ga[3][:, :, :].rearrange("p e t -> p (e t)"), scanm[:, :],
                                 pv[1][:, E * NT:2 * E * NT], 0.0, ALU.mult, ALU.add)
            dve.drain()
            v.tensor_tensor(ga[0][:, :, :], ga[3][:, :, :], totals, ALU.subtract)
            v.tensor_scalar(cnt[:, 0, :], ga[3][:, :, NT - 1], 1.0 / BLK, None, ALU.mult)
            dve.drain()
            v.tensor_tensor(cmpb[:, :, :], mid_dim(cnt[:, 0, :], NBLK), last_dim(iotaj[:, :], E), ALU.is_gt)
            v.tensor_tensor(ga[0][:, :, :], ga[0][:, :, :], prefix, ALU.add)
            dve.drain()
            v.tensor_reduce(cnt[:, 1, :], cmpb[:, :, :].rearrange("p j e -> p e j"), AX.X, ALU.add)
            dve.drain()
            src = 1
            for step, dst in ((1, 2), (2, 3), (4, 4)):
                v.tensor_copy(cnt[:, dst, 0:step], cnt[:, src, 0:step])
                v.tensor_tensor(cnt[:, dst, step:E], cnt[:, src, step:E], cnt[:, src, 0:E - step], ALU.add)
                dve.drain()
                src = dst
            v.tensor_tensor(cnt[:, 5, :], cnt[:, 4, :], cnt[:, 1, :], ALU.subtract)
            v.tensor_tensor(cmpb[:, :, :], last_dim(iotaj[:, :], E), mid_dim(cnt[:, 4, :], NBLK), ALU.is_ge)
            dve.drain()
            v.scalar_tensor_tensor(ga[1][:, :, :], last_dim(cnt[:, 5, :], NT), float(BLK), ga[0][:, :, :],
                                   ALU.mult, ALU.add)
            v.tensor_reduce(bexp[:, :], cmpb[:, :, :], AX.X, ALU.add)
            dve.drain()
            v.tensor_tensor(ga[3][:, :, :], ga[1][:, :, :], ga[2][:, :, :], ALU.mult)
            v.tensor_scalar(bexpi[:, :], bexp[:, :], float(E - 1), None, ALU.min)
            dve.drain()
            v.tensor_reduce(gr[:, 0, :], ga[3][:, :, :].rearrange("p e t -> p t e"), AX.X, ALU.add)
            dve.drain()
            v.tensor_copy(posi[:, :], gr[:, 0, :]).then_inc(pos_ready, 1)
            dve.drain()

            def take(i, k):
                e = dve.value_load(bexpi[0:1, bass.ds(i * RB + k, 1)], min_val=0, max_val=E - 1)
                v.tensor_copy(b1e[:, k % RB, :], b1c[:, bass.ds(e * HT, HT)]).then_inc(b1e_ready, 1)
                dve.wait_ge(bt_ready, i * RB + (k + 1))
                v.tensor_copy(xte[:, k % 2, :], px[:, 0:BLK]).then_inc(btc_ready, 1)

            def finish(i, first=False, last_trip=False):
                for k in range(RB):
                    if not (last_trip and k == RB - 1):
                        take(i, k + 1)
                    dve.wait_ge(we_in[k], i * 48 + 48)
                    dve.wait_ge(row_in[k], i * 16 + 16)
                    if not first:
                        dve.wait_ge(out_done[k], i * 32)
                    if not first or k > 1:
                        dve.wait_ge(ticked, i * RB + (k - 1))
                    v.tensor_copy(idxt[:, k, :], brow[:, k, :, 2 * D + 1].bitcast(U32))
                    dve.wait_ge(by_ready, i * RB + (k + 1))
                    v.tensor_tensor(yo[:, k % 2, :, :], ybank[k % 2].rearrange("p (j d) -> p j d", j=2),
                                    mid_dim(b2e[:, k, :], 2), ALU.add)
                    dve.drain()
                    for j in range(2):
                        last = v.scalar_tensor_tensor(ys[:, k, j, :], yo[:, k % 2, j, :],
                                                      brow[:, k, j, 2 * D:2 * D + 1], brow[:, k, j, D:2 * D],
                                                      ALU.mult, ALU.add)
                    last.then_inc(ys_ready, 1)

            take(0, 0)
            finish(0, first=True)
            with dve.Fori(1, NBLK // RB - 1) as i:
                finish(i)
            finish(NBLK // RB - 1, last_trip=True)

        @block.tensor
        def _(pe):
            mm = nc.tensor.matmul

            def logits(i, n):
                m = n % TRIP
                x, c = (m // SLOTS) % 2, m % SLOTS
                b, t0, nt, rows = tiles_of(c)
                pe.wait_ge(exp_done, i * TRIP + (n + 1 - NL + CREDIT))
                for j in range(nt):
                    cs = slice((t0 + j) * P, (t0 + j) * P + rows)
                    qs = slice(b * K, (b + 1) * K)
                    o = lg[n % NL][0:rows, j, :]
                    mm(o, th[:, x, b, cs], qhi[:, x, qs], start=True, stop=False)
                    mm(o, tl[:, x, b, cs], qhi[:, x, qs], start=False, stop=False)
                    last = mm(o, th[:, x, b, cs], qlo[:, x, qs], start=False, stop=True)
                last.then_inc(lg_ready, 1)

            def product(i, n):
                b, t0, nt, rows = tiles_of(n % SLOTS)
                k = n % NE
                if t0 == 0:
                    pe.wait_ge(ut_ready[b], latest(i, n // SLOTS, n % SLOTS, "ut", b))
                    pe.wait_ge(qlo_ready[b], latest(i, n // SLOTS, n % SLOTS, "qlo", b))
                pe.wait_ge(xs_ready, i * TRIP + (n + 1))
                for j in range(nt):
                    last = mm(pv[b][:, 0:K], xs[0:rows, k, j, :], ex[0:rows, k, j, :],
                              start=(t0 + j == 0), stop=(t0 + j == FULL))
                last.then_inc(pv_done, 1)

            def project_u(h, count):
                pe.wait_ge(ut_ready[h], count)
                for j in range(2):
                    mm(px[:, K + j:K + j + 1], ut[:, h, j * P:(j + 1) * P], meanw[:, :], start=True, stop=True)
                for j in range(2):
                    last = mm(px[:, j * D:(j + 1) * D], ut[:, h, j * P:(j + 1) * P], wvu[:, :], start=True, stop=True)
                last.then_inc(upd_ready[h], 1)

            def transpose_1(h, count):
                pe.wait_ge(sn1_ready[h], count)
                for j in range(2):
                    last = nc.tensor.transpose(px[:, K + j * P:K + (j + 1) * P], sn1[:, 2 * h + j, :], ident[:, :])
                last.then_inc(tr1_ready[h], 1)

            def q_transpose(h, count):
                pe.wait_ge(snq_ready[h], count)
                for j in range(2):
                    last = nc.tensor.transpose(px[:, K + j * P:K + (j + 1) * P], snq[:, 2 * h + j, :], ident[:, :])
                last.then_inc(trq_ready[h], 1)

            def q_product(h, count):
                pe.wait_ge(tcq_ready[h], count)
                mm(pv[h][:, K:2 * K], wqk[:, :], snqt[:, h, :], start=True, stop=True).then_inc(qk_ready[h], 1)

            def update(i, s, c, final=False):
                for h in (1, 0):
                    if now(c, "upd", h, final):
                        pe.wait_ge(g_ready[1 - h], latest(i, s, c, "gelu", 1 - h))
                        pe.wait_ge(tcq_ready[h], latest(i, s, c, "tcq", h))
                        project_u(h, made(i, s, "ut", "upd", h))
                    if now(c, "tr1", h, final):
                        transpose_1(h, made(i, s, "ap1", "tr1", h))
                    if now(c, "hid", h, final):
                        pe.wait_ge(tc1_ready[h], made(i, s, "tc1", "hid", h))
                        mm(px[:, 0:K], w1g[:, :], snt[:, h * K:(h + 1) * K], start=True,
                           stop=True).then_inc(h_ready[h], 1)
                    if now(c, "mm2", h, final):
                        pe.wait_ge(g_ready[h], made(i, s, "gelu", "mm2", h))
                        for j in range(2):
                            t = 2 * h + j
                            last = mm(py[:, j * D:(j + 1) * D], gt[:, t * P:(t + 1) * P], W["w2"][:, :],
                                      start=True, stop=True)
                        last.then_inc(o_ready[h], 1)
                    if now(c, "trq", h, final):
                        pe.wait_ge(g_ready[1 - h], latest(i, s, c, "gelu", 1 - h))
                        q_transpose(h, made(i, s, "apq", "trq", h))
                    if now(c, "qk", h, final):
                        pe.wait_ge(ut_ready[h], latest(i, s, c, "ut", h))
                        q_product(h, made(i, s, "tcq", "qk", h))

            for sems, step in ((upd_ready, "upd"), (tr1_ready, "tr1"), (h_ready, "hid"), (o_ready, "mm2"),
                               (trq_ready, "trq"), (qk_ready, "qk")):
                credit(pe, sems, step)

            def pre_transpose(x, r, base, pbase, bank=pz):
                if not isinstance(base, int):
                    pe.wait_ge(lo_ready, base + r)
                elif r >= 2:
                    pe.wait_ge(lo_ready, r - 1)
                pe.wait_ge(ap_ready, base + r + 1)
                b, t0, nt, rows = pre_tiles(r)
                if nt == 4:
                    pe.wait_ge(app_ready, pbase + (pool_step(r) + 1))
                for t in range(t0, t0 + nt):
                    at = (t - t0) * P
                    last = nc.tensor.transpose(bank[:, at:at + rows], nat[0:rows, x, b, t, :], ident[0:rows, 0:rows])
                last.then_inc(z_ready, 1)

            pe.sem_inc(pv_done, CREDIT)
            pe.wait_ge(consts, 3)
            pe.wait_ge(weights_in, WEIGHTS_IN)
            pe.wait_ge(rows_in, ROWS_IN)
            mm(px[:, 0:1], W["wk"][:, :], col["lnkv_b"], start=True, stop=True)
            mm(px[:, 1:2], W["wq"][:, :], col["lnq_b"], start=True, stop=True)
            mm(px[:, 2:3], W["wv"][:, :], col["lnkv_b"], start=True, stop=True)
            mm(px[:, 3:4], W["w1"][:, :], col["lnm_b"], start=True, stop=True)
            mm(px[:, 4:5], wtmp[:, 0, :], ones[:, 0:1], start=True, stop=True)
            for j in range(3):
                last = nc.tensor.transpose(py[:, j * D:(j + 1) * D], wtmp[:, j, :], ident[:, :])
            last.then_inc(wstep, 1)
            pe.wait_ge(consts, 4)
            mm(pz[:, 0:D], wtmp[:, 4, :], wtmp[:, 3, :], start=True, stop=True)
            mm(pz[:, D:2 * D], wtmp[:, 5, :], W["wu"][:, :], start=True, stop=True)
            mm(pz[:, 2 * D:2 * D + 1], wtmp[:, 3, :], ctmp[:, 3:4], start=True, stop=True).then_inc(wstep, 1)
            pe.wait_ge(consts, 5)
            mm(px[:, 0:D], v1b[:, :], W["wu"][:, :], start=True, stop=False)
            mm(px[:, 0:D], negones[:, :], wvu[:, :], start=False, stop=True)
            nc.tensor.transpose(py[:, 0:E * HT], b1r[:, :], ident[0:E * HT, 0:E * HT]).then_inc(wstep, 1)
            for r in range(PRE):
                if r == 1:
                    pe.wait_ge(prep, 3)
                pre_transpose(0, r, 0, 0, (pz, py)[r % 2])
            for h in range(2):
                if in_prologue("trq", h):
                    if h:
                        pe.wait_ge(tcq_ready[0], CR)
                    q_transpose(h, CR)
                if in_prologue("qk", h):
                    q_product(h, CR)
            pe.wait_ge(lo_ready, PRE)
            pe.wait_ge(qlo_ready[0], CR)
            for n in range(AHEAD):
                logits(0, n)

            with pe.Fori(0, GROUPS) as i:
                for s in range(ROUNDS):
                    for c in range(SLOTS):
                        n = s * SLOTS + c
                        ahead = (c + AHEAD) % SLOTS
                        if ahead == 0:
                            if s in (0, 5):
                                pe.wait_ge(lo_ready, pre_base(i, s, PRE) + PRE // 2)
                            pe.wait_ge(qlo_ready[0], latest(i, s, SLOTS, "qlo", 0))
                        if ahead == CH:
                            if s == 0:
                                pe.wait_ge(lo_ready, i * (2 * PRE) + PRE)
                            if s == 1:
                                pe.wait_ge(lo_ready, i * (2 * PRE) + 2 * PRE)
                            pe.wait_ge(qlo_ready[1], latest(i, s, SLOTS, "qlo", 1))
                        logits(i, n + AHEAD)
                        product(i, n)
                        if s in (0, 5):
                            for r in range(PRE):
                                if PRE_SLOT[r] + TRANSPOSE == c:
                                    pre_transpose(pre_pair(s), r, pre_base(i, s, PRE), pre_base(i, s, PPRE))
                        update(i, s, c)
            for c in range(SLOTS):
                update(GROUPS, 0, c, final=True)

            pe.wait_ge(exp_done, GROUPS * TRIP + AHEAD + CREDIT)
            def gate_transpose(r):
                pe.wait_ge(xn_ready, r + 1)
                if r >= 2:
                    pe.wait_ge(xtc_ready, r - 1)
                for j in range(4):
                    last = nc.tensor.transpose(lg[r % 2][:, j // 2, (j % 2) * P:(j % 2 + 1) * P],
                                               rec[:, 4 * r + j, 0:D], ident[:, :])
                last.then_inc(xt_ready, 1)

            gate_transpose(0)
            for r in range(NT // 4):
                if r + 1 < NT // 4:
                    gate_transpose(r + 1)
                pe.wait_ge(xtc_ready, r + 1)
                for j in range(4):
                    t = 4 * r + j
                    last = mm(pv[0][:, t * E:(t + 1) * E], xnt[:, r % 2, j * P:(j + 1) * P], wg[:, :],
                              start=True, stop=True)
                last.then_inc(gate_ready, 1)
            pe.wait_ge(hot_ready, 1)
            hot = ga[2][:, :, :].rearrange("p e t -> p (e t)")
            mm(pv[1][:, 0:E * NT], ltri[:, :], hot, start=True, stop=True)
            mm(pv[1][:, E * NT:2 * E * NT], ones[:, :], hot, start=True, stop=True).then_inc(rank_ready, 1)

            def expert_rows(i, k):
                pe.wait_ge(row_in[k % RB], i * 16 + (16 + 16 * (k // RB)))
                for j in range(2):
                    last = nc.tensor.transpose(px[:, j * P:(j + 1) * P], brow[:, k % RB, j, 0:D], ident[:, :])
                last.then_inc(bt_ready, 1)

            def expert(i, first=False, last_trip=False):
                for k in range(RB):
                    pe.wait_ge(we_in[k], i * 48 + 48)
                    pe.wait_ge(btc_ready, i * RB + (k + 1))
                    for j in range(HT):
                        mm(hbank[j], w1e[:, k, j * P:(j + 1) * P], xte[:, k % 2, :],
                           start=True, stop=True).then_inc(bh_ready, 1)
                    if not (last_trip and k == RB - 1):
                        expert_rows(i, k + 1)
                    if not first or k > 1:
                        pe.wait_ge(ys_ready, i * RB + (k - 1))
                    for r in range(2):
                        for j in range(HT):
                            if r == 0:
                                pe.wait_ge(bg_ready, i * (RB * HT) + (k * HT + j + 1))
                            last = mm(ybank[k % 2][:, r * D:(r + 1) * D], ht[:, k % 2, j, r * P:(r + 1) * P],
                                      w2e[:, k, j, :], start=(j == 0), stop=(j == HT - 1))
                    last.then_inc(by_ready, 1)

            expert_rows(0, 0)
            expert(0, first=True)
            with pe.Fori(1, NBLK // RB - 1) as i:
                expert(i)
            expert(NBLK // RB - 1, last_trip=True)


_INS = ['x', 'cond_1024', 'ctx_1024'] + ['L0_xcond_' + n for n in (
    'q_mu', 'q_logsig', 'lnkv_g', 'lnkv_b', 'lnq_g', 'lnq_b', 'lnm_g', 'lnm_b', 'lnp_g', 'lnp_b', 'wk', 'bk',
    'wv', 'bv', 'wq', 'bq', 'wu', 'bu', 'w1', 'b1', 'w2', 'b2')] + ['L0_ffn_' + n for n in (
        'Wg', 'bg', 'W1', 'b1', 'W2', 'b2')]


def kernel(**inputs):
    import numpy as _np
    import concourse.bacc as _bacc
    from concourse import mybir as _mybir
    from concourse.bass_utils import run_bass_kernel_spmd as _run

    nc = _bacc.Bacc("TRN2", target_bir_lowering=False, num_devices=1)
    arrays, aps = {}, {}
    for name in _INS:
        arr = _np.ascontiguousarray(inputs[name])
        arrays[f"in_{name}"] = arr
        aps[name] = nc.dram_tensor(f"in_{name}", arr.shape, _mybir.dt.from_np(arr.dtype), kind="ExternalInput").ap()
    out = nc.dram_tensor("out", (B, K, D), F32, kind="ExternalOutput").ap()
    build(nc, aps, out)
    r = _run(nc, [arrays], core_ids=[0])
    return r.results[0]["out"]
```
